# Optimizing a Trainium2 kernel written in Bass

```python
import numpy as np
import jax
import jax.numpy as jnp

def _softmax(x, axis=-1):
    return jax.nn.softmax(x, axis=axis)

def _gelu(x):
    return jax.nn.gelu(x, approximate=True)

def _silu(x):
    return jax.nn.silu(x)

def _sigmoid(x):
    return jax.nn.sigmoid(x)

def _layernorm(x, axis=-1, eps=1e-05):
    m = jnp.mean(x, axis=axis, keepdims=True)
    v = jnp.var(x, axis=axis, keepdims=True)
    return (x - m) / jnp.sqrt(v + eps)

def _scatter_add(tgt, idx, src, axis=0):
    return tgt.at[idx].add(src)

def _segment_sum(src, seg, n):
    return jax.ops.segment_sum(src, seg, n)
kernel_name = 'mk_recurrent_d2_jaxref_r8_5c15aa'

def setup_inputs(seed: int=0):
    np.random.seed(seed)
    _w = jnp.asarray

    def _L0_attn_setup():
        import jax, jax.numpy as jnp
        import numpy as np
        H = 32
        D = 64
        BS = 32
        LAYER_IDX = 0
        NUM_LAYERS = 32
        EPS = 1e-05

        def _decay_buffers():
            base = 1.0 / 2.0 ** (8.0 / H)
            rate = base ** (jnp.arange(H, dtype=jnp.float32) + 1.0)
            factor = 1.0 - LAYER_IDX / (NUM_LAYERS - 1 + 1e-05) + 1e-05
            slope = (rate * factor)[:, None, None]
            r = jnp.arange(BS, dtype=jnp.float32) + 1.0
            query_decay = jnp.exp(-slope * r[:, None])
            key_decay = jnp.exp(-slope * (BS - r[:, None]))
            dd = r[:, None] - r[None, :]
            dd = slope * dd[None, :, :]
            dd = jnp.where(dd >= 0, -dd, -jnp.inf)
            diagonal_decay = jnp.exp(dd)[None]
            block_decay = jnp.exp(-slope * BS)
            return (slope, query_decay, key_decay, diagonal_decay, block_decay)

        def _rmsnorm(x, w):
            v = jnp.mean(x.astype(jnp.float32) ** 2, axis=-1, keepdims=True)
            return (x * jax.lax.rsqrt(v + EPS)).astype(x.dtype) * w
        key = jax.random.key(seed)
        ks = jax.random.split(key, 4)
        b, s, hid = (2, 512, 256)
        return {'hidden_states': jax.random.normal(ks[0], (b, s, hid), jnp.float32), 'qkv_w': jax.random.normal(ks[1], (3 * H * D, hid), jnp.float32) * 0.02, 'out_w': jax.random.normal(ks[2], (hid, H * D), jnp.float32) * 0.02, 'gate_w': jax.random.normal(ks[3], (H * D, hid), jnp.float32) * 0.02, 'norm_w': jnp.ones((H * D,), jnp.float32)}
    _L0_attn_in = _L0_attn_setup()

    def _L0_ffn_setup():
        import jax, jax.numpy as jnp
        import numpy as np
        EPS = 1e-07

        def per_token_quant_int8(x, eps=EPS):
            absmax = jnp.max(jnp.abs(x), axis=-1, keepdims=True)
            scale = jnp.maximum(absmax, eps) / 127.0
            q = jnp.clip(jnp.round(x / scale), -128, 127).astype(jnp.int8)
            return (q, scale)
        key = jax.random.key(seed)
        k1, k2, k3, k4 = jax.random.split(key, 4)
        B, S, IN, OUT = (4, 512, 256, 256)
        x = jax.random.normal(k1, (B, S, IN), dtype=jnp.float32)
        weight = jax.random.randint(k2, (OUT, IN), -127, 128, dtype=jnp.int32).astype(jnp.int8)
        w_scale = jax.random.uniform(k3, (OUT, 1), dtype=jnp.float32) * 0.01 + 0.0001
        bias = jax.random.normal(k4, (OUT,), dtype=jnp.float32)
        return {'x': x, 'weight': weight, 'w_scale': w_scale, 'bias': bias}
    _L0_ffn_in = _L0_ffn_setup()

    def _L1_attn_setup():
        import jax, jax.numpy as jnp
        import numpy as np
        N_HEADS = 16
        key = jax.random.key(seed)
        ks = jax.random.split(key, 9)
        B, S, D = (2, 256, 256)
        s = 0.02
        return {'X': jax.random.normal(ks[0], (B, S, D), jnp.float32), 'Wq': jax.random.normal(ks[1], (D, D), jnp.float32) * s, 'bq': jax.random.normal(ks[2], (D,), jnp.float32) * s, 'Wk': jax.random.normal(ks[3], (D, D), jnp.float32) * s, 'bk': jax.random.normal(ks[4], (D,), jnp.float32) * s, 'Wv': jax.random.normal(ks[5], (D, D), jnp.float32) * s, 'bv': jax.random.normal(ks[6], (D,), jnp.float32) * s, 'Wo': jax.random.normal(ks[7], (D, D), jnp.float32) * s, 'bo': jax.random.normal(ks[8], (D,), jnp.float32) * s}
    _L1_attn_in = _L1_attn_setup()

    def _L1_ffn_setup():
        import jax, jax.numpy as jnp
        import numpy as np
        DIM = 256
        HID = 128
        E = 8
        K = 2
        SHID = HID * 1
        INIT = 0.02
        key = jax.random.key(seed)
        ks = jax.random.split(key, 9)
        return {'x': jax.random.normal(ks[0], (2, 128, DIM), jnp.float32), 'expert_bias': jnp.zeros((E,), jnp.float32), 'gate_w': jax.random.normal(ks[1], (E, DIM), jnp.float32) * INIT, 'w1': jax.random.normal(ks[2], (E, HID, DIM), jnp.float32) * INIT, 'w2': jax.random.normal(ks[3], (E, DIM, HID), jnp.float32) * INIT, 'w3': jax.random.normal(ks[4], (E, HID, DIM), jnp.float32) * INIT, 'sw1': jax.random.normal(ks[5], (SHID, DIM), jnp.float32) * INIT, 'sw2': jax.random.normal(ks[6], (DIM, SHID), jnp.float32) * INIT, 'sw3': jax.random.normal(ks[7], (SHID, DIM), jnp.float32) * INIT}
    _L1_ffn_in = _L1_ffn_setup()
    _d = {'L0_attn_hidden_states': _L0_attn_in['hidden_states'], 'L0_attn_qkv_w': _L0_attn_in['qkv_w'], 'L0_attn_out_w': _L0_attn_in['out_w'], 'L0_attn_gate_w': _L0_attn_in['gate_w'], 'L0_attn_norm_w': _L0_attn_in['norm_w'], 'L0_ffn_weight': _L0_ffn_in['weight'], 'L0_ffn_w_scale': _L0_ffn_in['w_scale'], 'L0_ffn_bias': _L0_ffn_in['bias'], 'L1_attn_Wq': _L1_attn_in['Wq'], 'L1_attn_bq': _L1_attn_in['bq'], 'L1_attn_Wk': _L1_attn_in['Wk'], 'L1_attn_bk': _L1_attn_in['bk'], 'L1_attn_Wv': _L1_attn_in['Wv'], 'L1_attn_bv': _L1_attn_in['bv'], 'L1_attn_Wo': _L1_attn_in['Wo'], 'L1_attn_bo': _L1_attn_in['bo'], 'L1_ffn_expert_bias': _L1_ffn_in['expert_bias'], 'L1_ffn_gate_w': _L1_ffn_in['gate_w'], 'L1_ffn_w1': _L1_ffn_in['w1'], 'L1_ffn_w2': _L1_ffn_in['w2'], 'L1_ffn_w3': _L1_ffn_in['w3'], 'L1_ffn_sw1': _L1_ffn_in['sw1'], 'L1_ffn_sw2': _L1_ffn_in['sw2'], 'L1_ffn_sw3': _L1_ffn_in['sw3']}
    _x0 = _d['L0_attn_hidden_states']
    _d['L0_attn_hidden_states'] = jax.random.normal(jax.random.fold_in(jax.random.key(seed), 1), (8, 256, 256), dtype=_x0.dtype)
    del _x0
    return _d

def reference(L0_attn_hidden_states, L0_attn_qkv_w, L0_attn_out_w, L0_attn_gate_w, L0_attn_norm_w, L0_ffn_weight, L0_ffn_w_scale, L0_ffn_bias, L1_attn_Wq, L1_attn_bq, L1_attn_Wk, L1_attn_bk, L1_attn_Wv, L1_attn_bv, L1_attn_Wo, L1_attn_bo, L1_ffn_expert_bias, L1_ffn_gate_w, L1_ffn_w1, L1_ffn_w2, L1_ffn_w3, L1_ffn_sw1, L1_ffn_sw2, L1_ffn_sw3):

    def _L0_attn_ref(hidden_states, qkv_w, out_w, gate_w, norm_w):
        import jax, jax.numpy as jnp
        import numpy as np
        H = 32
        D = 64
        BS = 32
        LAYER_IDX = 0
        NUM_LAYERS = 32
        EPS = 1e-05

        def _decay_buffers():
            base = 1.0 / 2.0 ** (8.0 / H)
            rate = base ** (jnp.arange(H, dtype=jnp.float32) + 1.0)
            factor = 1.0 - LAYER_IDX / (NUM_LAYERS - 1 + 1e-05) + 1e-05
            slope = (rate * factor)[:, None, None]
            r = jnp.arange(BS, dtype=jnp.float32) + 1.0
            query_decay = jnp.exp(-slope * r[:, None])
            key_decay = jnp.exp(-slope * (BS - r[:, None]))
            dd = r[:, None] - r[None, :]
            dd = slope * dd[None, :, :]
            dd = jnp.where(dd >= 0, -dd, -jnp.inf)
            diagonal_decay = jnp.exp(dd)[None]
            block_decay = jnp.exp(-slope * BS)
            return (slope, query_decay, key_decay, diagonal_decay, block_decay)

        def _rmsnorm(x, w):
            v = jnp.mean(x.astype(jnp.float32) ** 2, axis=-1, keepdims=True)
            return (x * jax.lax.rsqrt(v + EPS)).astype(x.dtype) * w
        b, s, hid = hidden_states.shape
        nb = s // BS
        _, qd, kd, dd, bd = _decay_buffers()
        qkv = jax.nn.silu(hidden_states @ qkv_w.T)
        qkv = qkv.reshape(b, s, H, 3 * D)
        q, k, v = jnp.split(qkv, 3, axis=-1)

        def to_blocks(t):
            return t.transpose(0, 2, 1, 3).reshape(b, H, nb, BS, D).transpose(2, 0, 1, 3, 4)
        qb, kb, vb = (to_blocks(q), to_blocks(k), to_blocks(v))
        qd_ = qd[None]
        kd_ = kd[None]
        bd_ = bd[None]

        def step(state, blk):
            qi, ki, vi = blk
            aw = jnp.einsum('bhid,bhjd->bhij', qi, ki) * dd
            intra = jnp.einsum('bhij,bhjd->bhid', aw, vi)
            inter = jnp.einsum('bhid,bhde->bhie', qi * qd_, state)
            new_state = state * bd_ + jnp.einsum('bhsd,bhse->bhde', ki * kd_, vi)
            return (new_state, intra + inter)
        state0 = jnp.zeros((b, H, D, D), hidden_states.dtype)
        _, ys = jax.lax.scan(step, state0, (qb, kb, vb))
        attn = ys.transpose(1, 2, 0, 3, 4).reshape(b, H, s, D)
        attn = attn.transpose(0, 2, 1, 3).reshape(b, s, H * D)
        attn = _rmsnorm(attn, norm_w)
        gate = jax.nn.sigmoid(hidden_states @ gate_w.T)
        return gate * attn @ out_w.T

    def _L0_ffn_ref(x, weight, w_scale, bias):
        import jax, jax.numpy as jnp
        import numpy as np
        EPS = 1e-07

        def per_token_quant_int8(x, eps=EPS):
            absmax = jnp.max(jnp.abs(x), axis=-1, keepdims=True)
            scale = jnp.maximum(absmax, eps) / 127.0
            q = jnp.clip(jnp.round(x / scale), -128, 127).astype(jnp.int8)
            return (q, scale)
        q, in_scale = per_token_quant_int8(x)
        acc = jnp.einsum('bsk,nk->bsn', q, weight, preferred_element_type=jnp.int32)
        out = acc.astype(jnp.float32) * in_scale * w_scale[:, 0] + bias
        return out.astype(jnp.float16)

    def _L1_attn_ref(X, Wq, bq, Wk, bk, Wv, bv, Wo, bo):
        import jax, jax.numpy as jnp
        import numpy as np
        N_HEADS = 16
        B, S, D = X.shape
        H = N_HEADS
        d_head = D // H
        scale = jnp.asarray(1.0 / np.sqrt(np.sqrt(d_head)), X.dtype)
        Q = (X @ Wq.T + bq).reshape(B, S, H, d_head) * scale
        K = (X @ Wk.T + bk).reshape(B, S, H, d_head) * scale
        V = (X @ Wv.T + bv).reshape(B, S, H, d_head)
        scores = jnp.einsum('bqhd,bkhd->bhqk', Q, K)
        causal = jnp.tril(jnp.ones((S, S), bool))
        scores = jnp.where(causal[None, None], scores, -jnp.inf)
        attn = jax.nn.softmax(scores.astype(jnp.float32), axis=-1).astype(X.dtype)
        out = jnp.einsum('bhqk,bkhd->bqhd', attn, V).reshape(B, S, D)
        return out @ Wo.T + bo

    def _L1_ffn_ref(x, expert_bias, gate_w, w1, w2, w3, sw1, sw2, sw3):
        import jax, jax.numpy as jnp
        import numpy as np
        DIM = 256
        HID = 128
        E = 8
        K = 2
        SHID = HID * 1
        INIT = 0.02
        B, S, D = x.shape
        xf = x.reshape(-1, D)
        N = xf.shape[0]
        scores = jax.nn.sigmoid((xf @ gate_w.T).astype(jnp.float32))
        _, sel = jax.lax.top_k(scores + expert_bias[None, :], K)
        top_scores = jnp.take_along_axis(scores, sel, axis=1)
        flat_exp = sel.reshape(-1)
        order = jnp.argsort(flat_exp, stable=True)
        sorted_exp = flat_exp[order]
        tok_idx = order // K
        sc_sorted = top_scores.reshape(-1)[order]
        rin = xf[tok_idx] * sc_sorted[:, None].astype(x.dtype)
        out_sorted = jnp.zeros_like(rin)
        for e in range(E):
            m = (sorted_exp == e)[:, None].astype(rin.dtype)
            h = jax.nn.silu(rin @ w1[e].T) * (rin @ w3[e].T)
            out_sorted = out_sorted + m * (h @ w2[e].T)
        routed = jnp.zeros((N, D), x.dtype).at[tok_idx].add(out_sorted)
        shared = jax.nn.silu(xf @ sw1.T) * (xf @ sw3.T) @ sw2.T
        return (routed + shared).reshape(B, S, D)
    x = L0_attn_hidden_states
    xn = _layernorm(x, axis=-1)
    s = _L0_attn_ref(xn, L0_attn_qkv_w, L0_attn_out_w, L0_attn_gate_w, L0_attn_norm_w)
    g = _silu(_L0_ffn_ref(xn, L0_ffn_weight, L0_ffn_w_scale, L0_ffn_bias))
    x = x + s * g
    xn = _layernorm(x, axis=-1)
    s = _L1_attn_ref(xn, L1_attn_Wq, L1_attn_bq, L1_attn_Wk, L1_attn_bk, L1_attn_Wv, L1_attn_bv, L1_attn_Wo, L1_attn_bo)
    g = _silu(_L1_ffn_ref(xn, L1_ffn_expert_bias, L1_ffn_gate_w, L1_ffn_w1, L1_ffn_w2, L1_ffn_w3, L1_ffn_sw1, L1_ffn_sw2, L1_ffn_sw3))
    x = x + s * g
    return x

_drawn_inputs = setup_inputs


def setup_inputs(seed=0):
    import zlib

    import numpy as np

    out = dict(_drawn_inputs(seed))
    spreads = {'L0_attn_norm_w': (1.0, 0.2), 'L1_ffn_expert_bias': (0.0, 0.8)}
    factors = {'L1_attn_Wq': 8.0,
     'L1_attn_bq': 8.0,
     'L1_attn_Wk': 8.0,
     'L1_attn_Wv': 8.0,
     'L1_attn_bv': 8.0,
     'L1_attn_Wo': 8.0,
     'L1_attn_bo': 8.0,
     'L1_ffn_gate_w': 8.0,
     'L1_ffn_w1': 8.0,
     'L1_ffn_w2': 8.0,
     'L1_ffn_w3': 8.0,
     'L1_ffn_sw1': 8.0,
     'L1_ffn_sw2': 8.0,
     'L1_ffn_sw3': 8.0}
    for name, (base, spread) in spreads.items():
        noise = np.random.default_rng([zlib.crc32(name.encode()), seed]).standard_normal(out[name].shape)
        drawn = base * np.exp(spread * noise) if base else spread * noise
        out[name] = jnp.asarray(drawn.astype(out[name].dtype))
    for name, factor in factors.items():
        out[name] = (out[name] * factor).astype(out[name].dtype)
    return out
```

```python
from contextlib import ExitStack

import concourse.bass as bass
from concourse import mybir

ALU = mybir.AluOpType
ACT = mybir.ActivationFunctionType
AX = mybir.AxisListType
F32 = mybir.dt.float32
F32R = mybir.dt.float32r
F16 = mybir.dt.float16
BF16 = mybir.dt.bfloat16
I8 = mybir.dt.int8
I32 = mybir.dt.int32
U32 = mybir.dt.uint32

P = 128
BATCHES, SEQ, HID = 8, 256, 256
TOK = BATCHES * SEQ
TILES = TOK // P
CH = HID // P

HEADS0, D0 = 32, 64
PAIRS = HEADS0 // 2
GROUP = 512
GROUPS = TOK // GROUP
GT = GROUP // P
COLS = 4 * P
WROW = CH * COLS + HID + 1
STEPS = PAIRS * GROUPS
BODY = 2 * GROUPS
ROUND = 12582912.0

HEADS1, D1 = 16, 16
EXPERTS = 8
EX = EXPERTS + 1
EG = 3
BT = SEQ // P
UNITS = BT * (EX // EG)


def wait(eng, sem, value):
    if isinstance(value, int) and value <= 0:
        return
    eng.wait_ge(sem, value)


def slopes():
    base = 1.0 / 2.0 ** (8.0 / HEADS0)
    factor = 1.0 - 0 / (32 - 1 + 1e-05) + 1e-05
    return [base ** (h + 1.0) * factor for h in range(HEADS0)]


def build(nc, x_d, w0_d, ffn_w_d, ffn_sc_d, ffn_b_d, wqkv1_d, wo1_d, bq_d, bk_d, bv_d, bo_d,
          ebias_d, router_d, w13_d, w2_d, out_d):
    with ExitStack() as keep:
        def ksb(name, shape, dt):
            return keep.enter_context(nc.sbuf_tensor(name, shape, dt))

        bank = [keep.enter_context(nc.psum_tensor(f"bank{i}", [P, 512], F32)) for i in range(8)]
        x = ksb("x", [P, TILES, HID], F32)
        acc = ksb("acc", [P, TILES, HID], F32)
        ssq = ksb("ssq", [P, TOK], F32)
        g16 = ksb("g16", [P, TILES, HID], F16)
        ident = ksb("ident", [P, P], F32)
        identb = ksb("identb", [P, P], BF16)
        with ExitStack() as layer0:
            xn_hi = layer0.enter_context(nc.sbuf_tensor("xn_hi", [P, CH, TOK], F32R))
            xn_lo = layer0.enter_context(nc.sbuf_tensor("xn_lo", [P, CH, TOK], F32R))
            decay = layer0.enter_context(nc.sbuf_tensor("decay", [P, HEADS0, 2 * P], F32))
            norm_and_ffn(nc, bank, x, g16, ident, identb, xn_hi, xn_lo, decay, ssq, acc,
                         x_d, ffn_w_d, ffn_sc_d, ffn_b_d)
            linear_attention(nc, bank, ident, xn_hi, xn_lo, decay, acc, ssq, w0_d)
        layer_one(nc, bank, x, acc, ssq, g16, ident, identb, wqkv1_d, wo1_d, bq_d, bk_d, bv_d, bo_d,
                  ebias_d, router_d, w13_d, w2_d, out_d)


def norm_and_ffn(nc, bank, x, g16, ident, identb, xn_hi, xn_lo, decay, ssq, acc,
                 x_d, ffn_w_d, ffn_sc_d, ffn_b_d):
    with ExitStack() as ctx:
        def sb(name, shape, dt):
            return ctx.enter_context(nc.sbuf_tensor(name, shape, dt))

        def sem(name):
            return ctx.enter_context(nc.semaphore(name))

        xn = sb("xn", [P, TILES, HID], F32)
        qr = sb("qr", [P, TILES, HID], F32)
        q16 = sb("q16", [P, TILES, HID], BF16)
        qT = sb("qT", [P, TILES // 2, CH, SEQ], BF16)
        stats = sb("stats", [P, TILES, 6], F32)
        mv = sb("mv", [P, TILES, 2], F32)
        var = sb("var", [P, TILES], F32)
        half = sb("half", [P, TILES], F32)
        rstd = sb("rstd", [P, TILES], F32)
        absmax = sb("absmax", [P, TILES], F32)
        in_sc = sb("in_sc", [P, TILES], F32)
        in_inv = sb("in_inv", [P, TILES], F32)
        w8 = sb("w8", [P, CH, HID // 4], I32)
        wb = sb("wb", [P, CH, HID], BF16)
        w_sc = sb("w_sc", [P, HID], F32)
        bias = sb("bias", [P, HID], F32)
        z = sb("z", [P, 2, HID], F32)
        z16 = sb("z16", [P, 2, 2, HID], F16)
        sg16 = sb("sg16", [P, 2, 2, HID], F16)
        dist_i = sb("dist_i", [P, 2 * P], I32)
        dist = sb("dist", [P, 2 * P], F32)

        x_in = [sem(f"x_in{g}") for g in range(4)]
        w_in = sem("ffn_w_in")
        consts = sem("consts")
        idents = sem("idents")
        dist_ready = sem("dist_ready")
        decay_exp = sem("decay_exp")
        decay_ready = sem("decay_ready")
        stats_done = sem("stats_done")
        mv_done = sem("mv_done")
        var_done = sem("var_done")
        rstd_done = sem("rstd_done")
        xn_done = sem("xn_done")
        absmax_done = sem("absmax_done")
        scale_done = sem("scale_done")
        quant_step = sem("quant_step")
        q_done = sem("q_done")
        wb_done = sem("wb_done")
        xT_done = sem("xT_done")
        hi_done = sem("hi_done")
        lo_done = sem("lo_done")
        qT_done = sem("qT_done")
        qT_copied = sem("qT_copied")
        lin_done = sem("lin_done")
        z_step = sem("z_step")
        z_done = sem("z_done")
        sig_done = sem("sig_done")
        g_done = sem("g_done")
        block = ctx.enter_context(nc.Block())
        NG = TILES // 4
        NB = TILES // 2

        @block.sync
        def _(sp):
            xv = x_d.rearrange("(g t p) d -> g p t d", g=NG, p=P)
            for g in range(NG):
                sp.dma_start(x[:, 4 * g:4 * g + 4, :], xv[g]).then_inc(x_in[g], 16)
            sp.dma_start(w8[:], ffn_w_d.rearrange("(c p) n -> p c n", p=P)).then_inc(w_in, 16)
            sp.dma_start(w_sc[:], ffn_sc_d).then_inc(w_in, 16)
            sp.dma_start(bias[:], ffn_b_d).then_inc(w_in, 16)

        @block.gpsimd
        def _(pool):
            pool.memset(half[:], -0.5).then_inc(consts, 1)
            pool.memset(ident[:], 0.0).then_inc(consts, 1)
            pool.memset(identb[:], 0.0).then_inc(consts, 1)
            pool.wait_ge(consts, 3)
            pool.affine_select(out=ident[:], in_=ident[:], compare_op=ALU.not_equal, fill=1.0,
                               base=0, pattern=[[-1, P]], channel_multiplier=1).then_inc(idents, 1)
            pool.affine_select(out=identb[:], in_=identb[:], compare_op=ALU.not_equal, fill=1.0,
                               base=0, pattern=[[-1, P]], channel_multiplier=1).then_inc(idents, 1)
            pool.iota(dist_i[:], pattern=[[1, 2 * P]], base=0, channel_multiplier=-1).then_inc(dist_ready, 1)
            pool.wait_ge(dist_ready, 1)
            pool.tensor_scalar(dist[:], dist_i[:], 0.0, 1.0, ALU.max, ALU.mult).then_inc(dist_ready, 1)
            for g in range(NG):
                pool.wait_ge(var_done, g + 1)
                s = slice(4 * g, 4 * g + 4)
                pool.tensor_tensor(rstd[:, s], var[:, s], half[:, s], ALU.pow).then_inc(rstd_done, 1)
            pool.wait_ge(decay_exp, HEADS0)
            pool.affine_select(out=decay[:, :, 0:P], in_=decay[:, :, 0:P], compare_op=ALU.is_ge, fill=0.0,
                               base=0, pattern=[[0, HEADS0], [1, P]], channel_multiplier=-1)\
                .then_inc(decay_ready, 1)
            pool.memset(ssq[:], 0.0).then_inc(decay_ready, 1)
            pool.memset(acc[:], 0.0).then_inc(decay_ready, 1)

        @block.vector
        def _(dve):
            for g in range(NG):
                dve.wait_ge(x_in[g], 16)
                for t in range(4 * g, 4 * g + 4):
                    dve.bn_stats(stats[:, t, :], x[:, t, :]).then_inc(stats_done, 1)
                for t in range(4 * g, 4 * g + 4):
                    dve.wait_ge(stats_done, t + 1)
                    dve.bn_aggr(mv[:, t, :], stats[:, t, :]).then_inc(mv_done, 1)
                dve.wait_ge(mv_done, 4 * g + 4)
                s = slice(4 * g, 4 * g + 4)
                dve.tensor_scalar(var[:, s], mv[:, s, 1], 1e-5, None, ALU.add).then_inc(var_done, 1)
            dve.wait_ge(w_in, 48)
            dve.tensor_copy(wb[:], w8[:].bitcast(I8)).then_inc(wb_done, 1)
            for g in range(NG):
                s = slice(4 * g, 4 * g + 4)
                dve.wait_ge(rstd_done, g + 1)
                for t in range(4 * g, 4 * g + 4):
                    dve.tensor_scalar(xn[:, t, :], x[:, t, :], mv[:, t, 0:1], rstd[:, t:t + 1],
                                      ALU.subtract, ALU.mult).then_inc(xn_done, 1)
                dve.wait_ge(xn_done, 4 * g + 4)
                dve.tensor_reduce(absmax[:, s], xn[:, s, :], AX.X, ALU.max,
                                  apply_absolute_value=True).then_inc(absmax_done, 1)
                dve.wait_ge(absmax_done, g + 1)
                dve.tensor_scalar(in_sc[:, s], absmax[:, s], 1e-7, 1.0 / 127.0, ALU.max, ALU.mult)\
                    .then_inc(scale_done, 1)
                dve.wait_ge(scale_done, 2 * g + 1)
                dve.reciprocal(in_inv[:, s], in_sc[:, s]).then_inc(scale_done, 1)
                dve.wait_ge(scale_done, 2 * g + 2)
                for t in range(4 * g, 4 * g + 4):
                    dve.tensor_scalar(qr[:, t, :], xn[:, t, :], in_inv[:, t:t + 1], ROUND,
                                      ALU.mult, ALU.add).then_inc(quant_step, 1)
                dve.wait_ge(quant_step, 5 * g + 4)
                dve.tensor_scalar(qr[:, s, :], qr[:, s, :], ROUND + 127.0, ROUND - 128.0,
                                  ALU.min, ALU.max).then_inc(quant_step, 1)
                dve.wait_ge(quant_step, 5 * g + 5)
                dve.tensor_scalar(q16[:, s, :], qr[:, s, :], -ROUND, None, ALU.add).then_inc(q_done, 1)
                for b in range(2 * g, 2 * g + 2):
                    dve.wait_ge(hi_done, b + 1)
                    c = slice(b * SEQ, (b + 1) * SEQ)
                    dve.tensor_tensor(xn_lo[:, :, c], bank[b % 2][:].rearrange("p (c n) -> p c n", c=CH),
                                      xn_hi[:, :, c].bitcast(F32), ALU.subtract).then_inc(lo_done, 1)
            for b in range(NB):
                dve.wait_ge(lin_done, b + 1)
                for m in range(2):
                    t = 2 * b + m
                    if b:
                        dve.wait_ge(z_done, 2 * b - 1 + m)
                    dve.scalar_tensor_tensor(z[:, m, :], bank[4 + b % 2][:, m * HID:(m + 1) * HID],
                                             in_sc[:, t:t + 1], w_sc[:], ALU.mult, ALU.mult).then_inc(z_step, 1)
                for m in range(2):
                    t = 2 * b + m
                    dve.wait_ge(z_step, t + 1)
                    if b >= 2:
                        dve.wait_ge(g_done, b - 1)
                    dve.tensor_tensor(z16[:, b % 2, m, :], z[:, m, :], bias[:], ALU.add).then_inc(z_done, 1)
                if b:
                    dve.wait_ge(sig_done, b)
                    dve.tensor_tensor(g16[:, 2 * b - 2:2 * b, :], z16[:, (b - 1) % 2], sg16[:, (b - 1) % 2],
                                      ALU.mult).then_inc(g_done, 1)
            dve.wait_ge(sig_done, NB)
            dve.tensor_tensor(g16[:, TILES - 2:TILES, :], z16[:, (NB - 1) % 2], sg16[:, (NB - 1) % 2],
                              ALU.mult).then_inc(g_done, 1)

        @block.scalar
        def _(act):
            act.wait_ge(dist_ready, 2)
            for h, s in enumerate(slopes()):
                act.activation(decay[:, h, :], dist[:], ACT.Exp, scale=-float(s)).then_inc(decay_exp, 1)

            def copy_q(b):
                act.wait_ge(qT_done, b + 1)
                act.activation(qT[:, b], bank[2 + b % 2][:, 0:256].bitcast(BF16)
                               .rearrange("p (c n) -> p c n", c=CH), ACT.Copy).then_inc(qT_copied, 1)

            for b in range(NB):
                act.wait_ge(xT_done, b + 1)
                act.activation(xn_hi[:, :, b * SEQ:(b + 1) * SEQ],
                               bank[b % 2][:].rearrange("p (c n) -> p c n", c=CH), ACT.Copy).then_inc(hi_done, 1)
                copy_q(b)
            for b in range(NB):
                act.wait_ge(z_done, 2 * b + 2)
                if b >= 2:
                    act.wait_ge(g_done, b - 1)
                act.activation(sg16[:, b % 2], z16[:, b % 2], ACT.Sigmoid).then_inc(sig_done, 1)

        @block.tensor
        def _(pe):
            pe.wait_ge(idents, 2)
            pe.wait_ge(wb_done, 1)

            def linear(b):
                pe.wait_ge(qT_copied, b + 1)
                if b >= 2:
                    pe.wait_ge(z_step, 2 * b - 2)
                for m in range(2):
                    for c in range(CH):
                        last = pe.matmul(bank[4 + b % 2][:, m * HID:(m + 1) * HID],
                                         qT[:, b, c, m * P:(m + 1) * P], wb[:, c, :],
                                         start=(c == 0), stop=(c == CH - 1))
                last.then_inc(lin_done, 1)

            for b in range(NB):
                pe.wait_ge(xn_done, 2 * b + 2)
                if b >= 2:
                    pe.wait_ge(lo_done, b - 1)
                for m in range(2):
                    for c in range(CH):
                        last = pe.transpose(bank[b % 2][:, c * SEQ + m * P:c * SEQ + (m + 1) * P],
                                            xn[:, 2 * b + m, c * P:(c + 1) * P], ident[:])
                last.then_inc(xT_done, 1)
                pe.wait_ge(q_done, b // 2 + 1)
                if b >= 2:
                    pe.wait_ge(qT_copied, b - 1)
                for m in range(2):
                    for c in range(CH):
                        last = pe.transpose(bank[2 + b % 2][:].bitcast(BF16)[:, c * SEQ + m * P:c * SEQ + (m + 1) * P],
                                            q16[:, 2 * b + m, c * P:(c + 1) * P], identb[:])
                last.then_inc(qT_done, 1)
            for b in range(NB):
                linear(b)


def linear_attention(nc, bank, ident, xn_hi, xn_lo, decay, acc, ssq, w0_d):
    with ExitStack() as ctx:
        def sb(name, shape, dt):
            return ctx.enter_context(nc.sbuf_tensor(name, shape, dt))

        def sem(name):
            return ctx.enter_context(nc.semaphore(name))

        stage = [sb(f"w_stage{i}", [P, WROW], F32) for i in range(2)]
        w_hi = [sb(f"w_hi{i}", [P, CH, COLS], F32R) for i in range(2)]
        w_lo = [sb(f"w_lo{i}", [P, CH, COLS], F32R) for i in range(2)]
        wo = [sb(f"wo{i}", [P, HID], F32) for i in range(2)]
        wo_hi = [sb(f"wo_hi{i}", [P, HID], F32R) for i in range(2)]
        wo_lo = [sb(f"wo_lo{i}", [P, HID], F32R) for i in range(2)]
        q = sb("q", [P, 2, GROUP], F32)
        k = sb("k", [P, 2, GROUP], F32)
        vT = sb("vT", [P, GROUP], F32)
        v = sb("v", [P, GT, P], F32)
        th = sb("th", [P, 2, GROUP], F32)
        aw = sb("aw", [P, 4, 3 * P], F32)
        gated = sb("gated", [P, GROUP], F32)
        gated_hi = sb("gated_hi", [P, 2, GROUP], F32R)
        gated_lo = sb("gated_lo", [P, 2, GROUP], F32R)
        sq = sb("sq", [P, 2, GROUP], F32)

        w_in = [sem(f"w0_in{i}") for i in range(2)]
        w_split = sem("w_split")
        w_hi_done = sem("w_hi_done")
        wo_ready = sem("wo_ready")
        projected = sem("projected")
        activated = sem("activated")
        scored = sem("scored")
        decayed = sem("decayed")
        attended = sem("attended")
        squared = sem("squared")
        ssq_added = sem("ssq_added")
        gated_done = sem("gated_done")
        gated_high = sem("gated_high")
        gated_split = sem("gated_split")
        wo_high = sem("wo_high")
        wo_split = sem("wo_split")
        v_turned = sem("v_turned")
        v_copied = sem("v_copied")
        out_done = sem("out_done")
        acc_done = sem("acc_done")
        block = ctx.enter_context(nc.Block())

        @block.sync
        def _(sp):
            def load(pair, i):
                wait(sp, w_split, pair - 1)
                wait(sp, wo_ready, pair - 1)
                sp.dma_start(stage[i][:], w0_d[pair]).then_inc(w_in[i], 16)

            load(0, 0)
            load(1, 1)
            with sp.Fori(1, PAIRS // 2) as it:
                load(2 * it, 0)
                load(2 * it + 1, 1)

        @block.gpsimd
        def _(pool):
            def split(pair, i):
                pool.wait_ge(w_hi_done, pair + 1)
                wide = stage[i][:, 0:CH * COLS].rearrange("p (c n) -> p c n", c=CH)
                pool.tensor_tensor(w_lo[i][:], wide, w_hi[i][:].bitcast(F32), ALU.subtract).then_inc(w_split, 1)

            def split_out_weights(pair, i):
                pool.wait_ge(wo_high, pair + 1)
                pool.tensor_tensor(wo_lo[i][:], wo[i][:], wo_hi[i][:].bitcast(F32), ALU.subtract)\
                    .then_inc(wo_split, 1)

            def split_gated(t, s):
                pool.wait_ge(gated_high, t + 1)
                pool.tensor_tensor(gated_lo[:, s % 2, :], gated[:], gated_hi[:, s % 2, :].bitcast(F32),
                                   ALU.subtract).then_inc(gated_split, 1)

            def add_squares(t, s):
                pool.wait_ge(squared, t + 1)
                g = s % GROUPS
                wait(pool, ssq_added, t + 1 - GROUPS)
                pool.tensor_tensor(ssq[:, g * GROUP:(g + 1) * GROUP], ssq[:, g * GROUP:(g + 1) * GROUP],
                                   sq[:, s % 2, :], ALU.add).then_inc(ssq_added, 1)

            def steps(it, last=False):
                for s in range(BODY):
                    add_squares(it * BODY + s, s)
                    split_gated(it * BODY + s, s)
                    if s == 0:
                        split(2 * it + 1, 1)
                    if s == 1:
                        split_out_weights(2 * it + 1, 1)
                    if s == GROUPS and not last:
                        split(2 * it + 2, 0)
                    if s == GROUPS + 1 and not last:
                        split_out_weights(2 * it + 2, 0)

            split(0, 0)
            split_out_weights(0, 0)
            steps(0)
            with pool.Fori(1, STEPS // BODY - 1) as it:
                steps(it)
            steps(STEPS // BODY - 1, True)

        @block.scalar
        def _(act):
            def silu(n, s, what, src, dst):
                act.wait_ge(projected, 4 * n + what + 1)
                act.activation(dst, src, ACT.Silu).then_inc(activated, 1)

            def qkv(n, s):
                silu(n, s, 0, bank[0][:], q[:, s % 2, :])
                silu(n, s, 1, bank[1][:], k[:, s % 2, :])
                silu(n, s, 2, bank[0][:], vT[:])

            def gate(n, s):
                act.wait_ge(projected, 4 * n + 4)
                wait(act, gated_done, n - 1)
                act.activation(th[:, s % 2, :], bank[1][:], ACT.Tanh, scale=0.5).then_inc(activated, 1)

            def high_weights(pair, i, turn):
                wait(act, projected, 4 * GROUPS * (pair - 1))
                act.wait_ge(w_in[i], 16 * (turn + 1))
                act.activation(w_hi[i][:], stage[i][:, 0:CH * COLS].rearrange("p (c n) -> p c n", c=CH),
                               ACT.Copy).then_inc(w_hi_done, 1)

            def high_out_weights(pair, i):
                act.wait_ge(wo_ready, pair + 1)
                wait(act, out_done, 2 * GROUPS * (pair - 1))
                act.activation(wo_hi[i][:], wo[i][:], ACT.Copy).then_inc(wo_high, 1)

            def high_gated(t, s):
                act.wait_ge(gated_done, t + 1)
                wait(act, out_done, 2 * t - 2)
                act.activation(gated_hi[:, s % 2, :], gated[:], ACT.Copy).then_inc(gated_high, 1)

            def square(t, s):
                act.wait_ge(attended, t + 1)
                wait(act, ssq_added, t - 1)
                act.activation(sq[:, s % 2, :], bank[4][:], ACT.Square).then_inc(squared, 1)

            def steps(it, last=False):
                for s in range(BODY):
                    t = it * BODY + s
                    more = not (last and s == BODY - 1)
                    if s == 0:
                        high_weights(2 * it + 1, 1, it)
                    if s == GROUPS and not last:
                        high_weights(2 * it + 2, 0, it + 1)
                    if more:
                        qkv(t + 1, s + 1)
                    square(t, s)
                    if more:
                        gate(t + 1, s + 1)
                    high_gated(t, s)
                    if s == 0:
                        high_out_weights(2 * it + 1, 1)
                    if s == GROUPS and not last:
                        high_out_weights(2 * it + 2, 0)

            high_weights(0, 0, 0)
            high_out_weights(0, 0)
            qkv(0, 0)
            gate(0, 0)
            steps(0)
            with act.Fori(1, STEPS // BODY - 1) as it:
                steps(it)
            steps(STEPS // BODY - 1, True)

        @block.vector
        def _(dve):
            def out_weights(pair, i, turn):
                wait(dve, wo_split, pair - 1)
                dve.wait_ge(w_in[i], 16 * (turn + 1))
                dve.tensor_scalar(wo[i][:], stage[i][:, CH * COLS:CH * COLS + HID],
                                  stage[i][:, WROW - 1:WROW], 0.5, ALU.mult, ALU.mult).then_inc(wo_ready, 1)

            def decays(t, j, pair):
                dve.wait_ge(scored, 4 * t + j + 1)
                head = 2 * pair + j % 2
                dve.tensor_tensor(aw[:, j, 0:2 * P], bank[2 + j % 2][:, 0:2 * P], decay[:, head, :], ALU.mult)
                dve.tensor_tensor(aw[:, j, 2 * P:3 * P], bank[2 + j % 2][:, 2 * P:3 * P],
                                  decay[:, head, 0:P], ALU.mult).then_inc(decayed, 1)

            def copy_v(n):
                dve.wait_ge(v_turned, n + 1)
                dve.tensor_copy(v[:].rearrange("p t n -> p (t n)"), bank[7][:]).then_inc(v_copied, 1)

            def gates(t, s):
                dve.wait_ge(squared, t + 1)
                dve.wait_ge(activated, 4 * t + 4)
                wait(dve, gated_split, t)
                dve.scalar_tensor_tensor(gated[:], th[:, s % 2, :], 1.0, bank[4][:], ALU.add, ALU.mult)\
                    .then_inc(gated_done, 1)

            def accumulate(t, s, u):
                dve.wait_ge(out_done, 2 * t + u + 1)
                wait(dve, acc_done, 2 * (t - GROUPS) + u + 1)
                m = GT * (s % GROUPS) + 2 * u
                part = acc[:, m:m + 2, :].rearrange("p t n -> p (t n)")
                dve.tensor_tensor(part, bank[5 + u][:], part, ALU.add).then_inc(acc_done, 1)

            def steps(it, last=False):
                for s in range(BODY):
                    t = it * BODY + s
                    for j in range(4):
                        decays(t, j, 2 * it + s // GROUPS)
                    for u in range(2):
                        if s or not isinstance(it, int) or it:
                            accumulate(t - 1, s + BODY - 1, u)
                    gates(t, s)
                    if not (last and s == BODY - 1):
                        copy_v(t + 1)
                    if s == 0:
                        out_weights(2 * it + 1, 1, it)
                    if s == GROUPS and not last:
                        out_weights(2 * it + 2, 0, it + 1)

            out_weights(0, 0, 0)
            copy_v(0)
            steps(0)
            with dve.Fori(1, STEPS // BODY - 1) as it:
                steps(it)
            steps(STEPS // BODY - 1, True)
            for u in range(2):
                accumulate(STEPS - 1, BODY - 1, u)

        @block.tensor
        def _(pe):
            def columns(n, s, what, out):
                i, g = (s // GROUPS) % 2, s % GROUPS
                toks = slice(g * GROUP, (g + 1) * GROUP)
                cols = slice(what * P, (what + 1) * P)
                for c in range(CH):
                    for a, b in ((w_hi, xn_hi), (w_hi, xn_lo), (w_lo, xn_hi)):
                        last = pe.matmul(out, a[i][:, c, cols], b[:, c, toks],
                                         start=(c == 0 and a is w_hi and b is xn_hi),
                                         stop=(c == CH - 1 and a is w_lo))
                last.then_inc(projected, 1)

            def query(n, s, pair):
                pe.wait_ge(w_split, pair + 1)
                wait(pe, activated, 4 * n - 1)
                columns(n, s, 0, bank[0][:])

            def key(n, s):
                wait(pe, activated, 4 * n)
                columns(n, s, 1, bank[1][:])

            def value(n, s):
                pe.wait_ge(activated, 4 * n + 1)
                columns(n, s, 2, bank[0][:])

            def turn_value(n):
                pe.wait_ge(activated, 4 * n + 3)
                wait(pe, v_copied, n)
                for m in range(GT):
                    last = pe.transpose(bank[7][:, m * P:(m + 1) * P], vT[:, m * P:(m + 1) * P], ident[:])
                last.then_inc(v_turned, 1)

            def gate(n, s):
                pe.wait_ge(activated, 4 * n + 2)
                columns(n, s, 3, bank[1][:])

            def scores(t, s, j):
                pe.wait_ge(activated, 4 * t + 2)
                wait(pe, decayed, 4 * t + j - 1)
                b, r = (j // 2) * SEQ, slice(D0 * (j % 2), D0 * (j % 2 + 1))
                out = bank[2 + j % 2]
                pe.matmul(out[:, 0:2 * P], k[r, s % 2, b:b + P], q[r, s % 2, b:b + SEQ], start=True, stop=True)
                pe.matmul(out[:, 2 * P:3 * P], k[r, s % 2, b + P:b + SEQ], q[r, s % 2, b + P:b + SEQ],
                          start=True, stop=True).then_inc(scored, 1)

            def attend(t, s):
                pe.wait_ge(decayed, 4 * t + 4)
                pe.wait_ge(v_copied, t + 1)
                wait(pe, gated_done, t)
                wait(pe, squared, t)
                for b in range(2):
                    for tile in range(2):
                        for h in range(2):
                            r = slice(D0 * h, D0 * (h + 1))
                            cols = aw[:, 2 * b + h, 0:2 * P] if tile == 0 else aw[:, 2 * b + h, 2 * P:3 * P]
                            last = pe.matmul(bank[4][r, b * SEQ + tile * P:(b + 1) * SEQ], v[:, 2 * b + tile, r],
                                             cols, start=(tile == 0), stop=(tile == 1))
                last.then_inc(attended, 1)

            def back(t, s, pair):
                i = (s // GROUPS) % 2
                pe.wait_ge(gated_split, t + 1)
                pe.wait_ge(wo_split, pair + 1)
                for u in range(2):
                    wait(pe, acc_done, 2 * t + u - 1)
                    for m in range(2):
                        toks = slice((2 * u + m) * P, (2 * u + m + 1) * P)
                        for a, b in ((gated_hi, wo_hi), (gated_hi, wo_lo), (gated_lo, wo_hi)):
                            last = pe.matmul(bank[5 + u][:, m * HID:(m + 1) * HID], a[:, s % 2, toks], b[i][:],
                                             start=(a is gated_hi and b is wo_hi), stop=(a is gated_lo))
                    last.then_inc(out_done, 1)

            def steps(it, last=False):
                for s in range(BODY):
                    t = it * BODY + s
                    more = not (last and s == BODY - 1)
                    scores(t, s, 0)
                    scores(t, s, 1)
                    if more:
                        query(t + 1, s + 1, 2 * it + (s + 1) // GROUPS)
                    scores(t, s, 2)
                    scores(t, s, 3)
                    if s or not isinstance(it, int) or it:
                        back(t - 1, s + BODY - 1, 2 * it + (s - 1) // GROUPS)
                    if more:
                        key(t + 1, s + 1)
                        value(t + 1, s + 1)
                    attend(t, s)
                    if more:
                        turn_value(t + 1)
                        gate(t + 1, s + 1)

            query(0, 0, 0)
            key(0, 0)
            value(0, 0)
            turn_value(0)
            gate(0, 0)
            steps(0)
            with pe.Fori(1, STEPS // BODY - 1) as it:
                steps(it)
            steps(STEPS // BODY - 1, True)
            back(STEPS - 1, BODY - 1, PAIRS - 1)


HEAD_OF_UP = [1, 3, 5, 7, 9, 11]


def transposes_before_head(h):
    return h + sum(a + 1 < h for a in HEAD_OF_UP)


def transposes_before_unit(u):
    return HEAD_OF_UP[u] + 2 + u


TURNS = HEADS1 + UNITS


def layer_one(nc, bank, x, acc, ssq, g16, ident, identb, wqkv_d, wo_d, bq_d, bk_d, bv_d, bo_d,
              ebias_d, router_d, w13_d, w2_d, out_d):
    with ExitStack() as ctx:
        def sb(name, shape, dt):
            return ctx.enter_context(nc.sbuf_tensor(name, shape, dt))

        def sem(name):
            return ctx.enter_context(nc.semaphore(name))

        NE = EX * P
        ones = sb("ones", [P, 1], F32)
        ms = sb("ms", [P, TILES], F32)
        half = sb("half1", [P, TILES], F32)
        rms = sb("rms", [P, TILES], F32)
        branch = sb("branch", [P, TILES, HID], F32)
        wqkv = sb("wqkv", [P, CH, 3 * HID], F32)
        wqkv_hi = sb("wqkv_hi", [P, CH, 3 * HID], F32R)
        wqkv_lo = sb("wqkv_lo", [P, CH, 3 * HID], F32R)
        wo = sb("w_out1", [P, CH, HID], F32)
        router = sb("router", [P, CH, EXPERTS], F32)
        router_hi = sb("router_hi", [P, CH, EXPERTS], F32R)
        router_lo = sb("router_lo", [P, CH, EXPERTS], F32R)
        w13_hi = sb("w13_hi", [P, CH, 2 * NE], F32R)
        w13_lo = sb("w13_lo", [P, CH, 2 * NE], F32R)
        w2 = sb("w2", [P, EX, HID], F32)
        bq = sb("bq", [P, CH], F32)
        bk = sb("bk", [P, CH], F32)
        bv = sb("bv", [P, HID], F32)
        bo = sb("bo", [P, HID], F32)
        ebias = sb("ebias", [P, EXPERTS], F32)
        row_i = sb("row_i", [P, 2], I32)
        par = sb("par", [P, 2], F32)
        causal = sb("causal", [P, P], BF16)
        number = sb("number", [P, EXPERTS], I32)
        numberf = sb("numberf", [P, EXPERTS], F32)

        w_in = sem("w1_in")
        w13_in = sem("w13_in")
        ones_done = sem("ones_done")
        consts = sem("consts1")
        ms_sum = sem("ms_sum")
        ms_done = sem("ms_done")
        rms_done = sem("rms_done")
        branch_done = sem("branch_done")
        x1_done = sem("x1_done")
        hi_copied = sem("hi_copied")
        split_done = sem("split_done")
        prepare = ExitStack()
        block = prepare.enter_context(nc.Block())
        N_IN = 8

        @block.sync
        def _(sp):
            sp.dma_start(wqkv[:], wqkv_d.rearrange("(c p) n -> p c n", p=P)).then_inc(w_in, 16)
            sp.dma_start(wo[:], wo_d.rearrange("(c p) n -> p c n", p=P)).then_inc(w_in, 16)
            sp.dma_start(router[:], router_d.rearrange("(c p) n -> p c n", p=P)).then_inc(w_in, 16)
            sp.dma_start(bq[:], bq_d).then_inc(w_in, 16)
            sp.dma_start(bk[:], bk_d).then_inc(w_in, 16)
            sp.dma_start(bv[:], bv_d).then_inc(w_in, 16)
            sp.dma_start(bo[:], bo_d).then_inc(w_in, 16)
            sp.dma_start(ebias[:], ebias_d).then_inc(w_in, 16)
            sp.dma_start(w2[:], w2_d.rearrange("e p n -> p e n")).then_inc(w13_in, 16)
            sp.wait_ge(branch_done, 4)
            sp.dma_start(acc[:].rearrange("p t n -> p (t n)")[:, 0:2 * NE], w13_d[0:P, :]).then_inc(w13_in, 16)
            sp.wait_ge(x1_done, 4)
            sp.dma_start(branch[:].rearrange("p t n -> p (t n)")[:, 0:2 * NE], w13_d[P:2 * P, :]).then_inc(w13_in, 16)

        @block.gpsimd
        def _(pool):
            pool.memset(half[:], -0.5).then_inc(consts, 1)
            pool.memset(causal[:], 0.0).then_inc(consts, 1)
            pool.iota(row_i[:], pattern=[[0, 2]], base=0, channel_multiplier=1).then_inc(consts, 1)
            pool.iota(number[:], pattern=[[1, EXPERTS]], base=0, channel_multiplier=0).then_inc(consts, 1)
            pool.wait_ge(consts, 4)
            pool.affine_select(out=causal[:], in_=causal[:], compare_op=ALU.is_ge, fill=-1e30,
                               base=0, pattern=[[-1, P]], channel_multiplier=1).then_inc(consts, 1)
            pool.wait_ge(ms_done, 1)
            pool.tensor_tensor(rms[:], ms[:], half[:], ALU.pow).then_inc(rms_done, 1)
            for g in range(4):
                s = slice(4 * g, 4 * g + 4)
                pool.wait_ge(branch_done, g + 1)
                pool.tensor_tensor(x[:, s, :], x[:, s, :], branch[:, s, :], ALU.add).then_inc(x1_done, 1)

        @block.vector
        def _(dve):
            dve.memset(ones[:], 1.0).then_inc(ones_done, 1)
            dve.wait_ge(ms_sum, 1)
            dve.tensor_scalar(ms[:], bank[7][:, 0:TILES], 1.0 / (HEADS0 * D0), 1e-5, ALU.mult, ALU.add)\
                .then_inc(ms_done, 1)
            dve.wait_ge(rms_done, 1)
            for t in range(TILES):
                last = dve.scalar_tensor_tensor(branch[:, t, :], acc[:, t, :], rms[:, t:t + 1], g16[:, t, :],
                                                ALU.mult, ALU.mult)
                if t % 4 == 3:
                    last.then_inc(branch_done, 1)
            dve.wait_ge(consts, 5)
            dve.tensor_scalar(row_i[:, 0:2], row_i[:, 0:2], 4, 1, ALU.logical_shift_right, ALU.bitwise_and)\
                .then_inc(consts, 1)
            dve.wait_ge(consts, 6)
            dve.tensor_scalar(par[:, 1:2], row_i[:, 1:2], 0.25, None, ALU.mult).then_inc(consts, 1)
            dve.tensor_scalar(par[:, 0:1], row_i[:, 0:1], -0.25, 0.25, ALU.mult, ALU.add).then_inc(consts, 1)
            dve.tensor_copy(numberf[:], number[:]).then_inc(consts, 1)
            dve.wait_ge(w_in, 16 * N_IN)
            dve.wait_ge(hi_copied, 2)
            dve.tensor_tensor(wqkv_lo[:], wqkv[:], wqkv_hi[:].bitcast(F32), ALU.subtract).then_inc(split_done, 1)
            dve.tensor_tensor(router_lo[:], router[:], router_hi[:].bitcast(F32), ALU.subtract).then_inc(split_done, 1)
            for c, src in enumerate((acc, branch)):
                dve.wait_ge(hi_copied, 3 + c)
                dve.tensor_tensor(w13_lo[:, c, :], src[:].rearrange("p t n -> p (t n)")[:, 0:2 * NE],
                                  w13_hi[:, c, :].bitcast(F32), ALU.subtract).then_inc(split_done, 1)

        @block.scalar
        def _(act):
            act.wait_ge(w_in, 16 * N_IN)
            act.activation(wqkv_hi[:], wqkv[:], ACT.Copy).then_inc(hi_copied, 1)
            act.activation(router_hi[:], router[:], ACT.Copy).then_inc(hi_copied, 1)
            act.wait_ge(w13_in, 48)
            for c, src in enumerate((acc, branch)):
                act.activation(w13_hi[:, c, :], src[:].rearrange("p t n -> p (t n)")[:, 0:2 * NE], ACT.Copy)\
                    .then_inc(hi_copied, 1)

        @block.tensor
        def _(pe):
            pe.wait_ge(ones_done, 1)
            for t in range(TILES):
                last = pe.matmul(bank[7][:, t:t + 1], ssq[:, t * P:(t + 1) * P], ones[:], start=True, stop=True)
            last.then_inc(ms_sum, 1)

        prepare.close()
        batches(nc, ctx, bank, x, ident, identb, wqkv_hi, wqkv_lo, wo, router_hi, router_lo, w13_hi, w13_lo,
                w2, bq, bk, bv, bo, ebias, par, causal, numberf, half, out_d)


def batches(nc, ctx, bank, x, ident, identb, wqkv_hi, wqkv_lo, wo, router_hi, router_lo, w13_hi, w13_lo,
            w2, bq, bk, bv, bo, ebias, par, causal, numberf, half, out_d):
    def sb(name, shape, dt):
        return ctx.enter_context(nc.sbuf_tensor(name, shape, dt))

    def sem(name):
        return ctx.enter_context(nc.semaphore(name))

    NE = EX * P
    GE = EG * P
    tick = sb("tick", [P, 1], F32)
    stats = sb("stats1", [P, BT, 6], F32)
    mv = sb("mv1", [P, BT, 2], F32)
    var = sb("var1", [P, BT], F32)
    rstd = sb("rstd1", [P, BT], F32)
    xn = sb("xn1", [P, BT, HID], F32)
    xh = sb("xh", [P, CH, SEQ], F32R)
    xl = sb("xl", [P, CH, SEQ], F32R)
    bqm = sb("bqm", [P, 2, CH], F32)
    qm = sb("qm", [P, 2, CH, SEQ], F32)
    kT = sb("kT", [P, CH, SEQ], F32)
    vg = sb("vg", [P, BT, HEADS1, D1 + 1], F32)
    nmax = sb("nmax", [P, HEADS1, BT], F32)
    prob = sb("prob", [P, 2, 3 * P], F32)
    probT = sb("probT", [P, 2, 3 * P], F32)
    rsum = sb("rsum", [P, 2, BT, 8], F32)
    on = sb("on", [P, BT, HID], F32)
    oT = sb("oT", [P, CH, SEQ], F32)
    s1 = sb("s1", [P, BT, HID], F32)
    en = sb("en", [P, BT, EXPERTS], F32)
    en1 = sb("en1", [P, BT, EXPERTS], F32)
    score = sb("score", [P, BT, EXPERTS], F32)
    ranked = sb("ranked", [P, BT, EXPERTS], F32)
    top = sb("top", [P, BT, 8], F32)
    topi = sb("topi", [P, BT, 8], U32)
    topf = sb("topf", [P, BT, 2], F32)
    first = sb("first", [P, BT, EXPERTS], F32)
    chosen = sb("chosen", [P, BT, EXPERTS], F32)
    share = sb("share", [P, BT, EX], F32)
    half_s = sb("half_s", [P, BT, EX], F32)
    half_s2 = sb("half_s2", [P, BT, EX], F32)
    th = sb("th1", [P, GE], F32)
    tu = sb("tu", [P, GE], F32)
    hh = sb("hh", [P, GE], F32)
    hT = sb("hT", [P, BT, EX, P], F32)
    thy = sb("thy", [P, BT * HID], F32)
    gy = sb("gy", [P, BT * HID], F32)
    prod = sb("prod", [P, BT * HID], F32)
    xo = sb("xo", [P, BT, HID], F32)

    once = sem("once")
    stats_done = sem("stats1_done")
    mv_done = sem("mv1_done")
    var_done = sem("var1_done")
    rstd_done = sem("rstd1_done")
    xn_done = sem("xn1_done")
    xT_done = sem("xT1_done")
    hi_done = sem("hi1_done")
    lo_done = sem("lo1_done")
    q_proj = sem("q_proj")
    k_proj = sem("k_proj")
    v_proj = sem("v_proj")
    r_proj = sem("r_proj")
    q_done = sem("q1_done")
    k_done = sem("k1_done")
    v_done = sem("v1_done")
    r_exp = sem("r_exp")
    route = sem("route")
    scored = sem("scored1")
    max_done = sem("max_done")
    exp_done = sem("exp_done")
    turned = sem("turned")
    turn_copied = sem("turn_copied")
    pv_done = sem("pv_done")
    rec_done = sem("rec_done")
    norm_done = sem("norm_done")
    oT_done = sem("oT_done")
    oT_copied = sem("oT_copied")
    wo_done = sem("wo_done")
    s1_done = sem("s1_done")
    up_done = sem("up_done")
    tanh_done = sem("tanh_done")
    tu_done = sem("tu_done")
    h_done = sem("h_done")
    y_done = sem("y_done")
    thy_done = sem("thy_done")
    gy_done = sem("gy_done")
    prod_done = sem("prod_done")
    xo_done = sem("xo_done")
    stored = sem("stored")
    block = ctx.enter_context(nc.Block())
    ROUTE = 13

    def program(eng, body):
        body(0)
        with eng.Fori(1, BATCHES) as b:
            body(b)

    @block.sync
    def _(sp):
        def body(b):
            sp.wait_ge(xo_done, b + 1)
            sp.dma_start(out_d.rearrange("(b t p) d -> b p t d", b=BATCHES, p=P)[b], xo[:]).then_inc(stored, 16)

        program(sp, body)
        sp.wait_ge(stored, 16 * BATCHES)

    @block.gpsimd
    def _(pool):
        def body(b):
            pool.wait_ge(var_done, b + 1)
            pool.tensor_tensor(rstd[:], var[:], half[:, 0:BT], ALU.pow).then_inc(rstd_done, 1)
            pool.wait_ge(prod_done, b + 1)
            wait(pool, stored, 16 * b)
            pool.tensor_tensor(xo[:], x[:, 2 * b:2 * b + 2, :] if isinstance(b, int) else
                               x[:, bass.ds(2 * b, 2), :],
                               prod[:].rearrange("p (t n) -> p t n", t=BT), ALU.add).then_inc(xo_done, 1)

        program(pool, body)

    @block.vector
    def _(dve):
        dve.memset(vg[:], 1.0).then_inc(once, 1)
        dve.memset(share[:], 1.0).then_inc(once, 1)
        for m in range(2):
            dve.tensor_scalar(bqm[:, m, :], bq[:], par[:, m:m + 1], None, ALU.mult).then_inc(once, 1)
        dve.wait_ge(once, 4)

        def head_max(b, h):
            dve.wait_ge(scored, HEADS1 * b + h + 1)
            dve.tensor_reduce(nmax[:, h, 0:1], bank[2 + h % 2][:, 0:P], AX.X, ALU.max, negate=True)
            dve.tensor_reduce(nmax[:, h, 1:2], bank[2 + h % 2][:, P:3 * P], AX.X, ALU.max, negate=True)\
                .then_inc(max_done, 1)

        def copy_turn(b, h):
            n = TURNS * b + transposes_before_head(h)
            dve.wait_ge(turned, n + 1)
            dve.tensor_copy(probT[:, h % 2, :], bank[4][:, 0:3 * P]).then_inc(turn_copied, 1)

        def normalise(b, f):
            sums = bank[5][:, 0:BT * 8 * (D1 + 1)].rearrange("p (t h d) -> p t h d", t=BT, h=8)
            dve.wait_ge(pv_done, 2 * b + f + 1)
            dve.reciprocal(rsum[:, f], sums[:, :, :, D1]).then_inc(rec_done, 1)
            dve.wait_ge(rec_done, 2 * b + f + 1)
            for t in range(BT):
                last = dve.tensor_tensor(on[:, t, f * 8 * D1:(f + 1) * 8 * D1].rearrange("p (h d) -> p h d", h=8),
                                         sums[:, t, :, 0:D1],
                                         rsum[:, f, t, :].rearrange("p (h o) -> p h o", o=1).to_broadcast([P, 8, D1]),
                                         ALU.mult)
            last.then_inc(norm_done, 1)

        def hidden(b, u):
            t, g = u // (UNITS // BT), u % (UNITS // BT)
            dve.wait_ge(tanh_done, UNITS * b + u + 1)
            dve.scalar_tensor_tensor(tu[:], th[:], 1.0, bank[6][:, 0:GE], ALU.add, ALU.mult).then_inc(tu_done, 1)
            dve.wait_ge(tu_done, UNITS * b + u + 1)
            for e in range(EG):
                c = slice(e * P, (e + 1) * P)
                last = dve.scalar_tensor_tensor(hh[:, c], tu[:, c], half_s2[:, t, g * EG + e:g * EG + e + 1],
                                                bank[7][:, c], ALU.mult, ALU.mult)
            last.then_inc(h_done, 1)

        def router_scores(b):
            r0 = ROUTE * b

            def link(n):
                dve.wait_ge(route, r0 + n)

            dve.wait_ge(r_exp, b + 1)
            dve.tensor_scalar(en1[:], en[:], 1.0, None, ALU.add).then_inc(route, 1)
            link(1)
            dve.reciprocal(score[:], en1[:]).then_inc(route, 1)
            link(2)
            for t in range(BT):
                dve.tensor_tensor(ranked[:, t], score[:, t], ebias[:], ALU.add).then_inc(route, 1)
            link(4)
            dve.memset(tick[:], 0.0)
            for t in range(BT):
                dve.max(top[:, t], ranked[:, t]).then_inc(route, 1)
            link(6)
            dve.memset(tick[:], 0.0)
            for t in range(BT):
                dve.max_index(topi[:, t], top[:, t], ranked[:, t]).then_inc(route, 1)
            link(8)
            dve.tensor_copy(topf[:], topi[:, :, 0:2]).then_inc(route, 1)
            link(9)
            for t in range(BT):
                last = dve.tensor_scalar(first[:, t], numberf[:], topf[:, t, 0:1], None, ALU.is_equal)
            last.then_inc(route, 1)
            link(10)
            for t in range(BT):
                last = dve.scalar_tensor_tensor(chosen[:, t], numberf[:], topf[:, t, 1:2], first[:, t],
                                                ALU.is_equal, ALU.add)
            last.then_inc(route, 1)
            link(11)
            dve.tensor_tensor(share[:, :, 0:EXPERTS], chosen[:], score[:], ALU.mult).then_inc(route, 1)
            link(12)
            dve.tensor_scalar(half_s[:], share[:], 0.5, None, ALU.mult)
            dve.scalar_tensor_tensor(half_s2[:], share[:], 0.5, share[:], ALU.mult, ALU.mult).then_inc(route, 1)

        def body(b):
            tile = (lambda m: x[:, 2 * b + m, :]) if isinstance(b, int) else \
                (lambda m: x[:, bass.ds(2 * b + m, 1), :].rearrange("p o n -> p (o n)"))
            for m in range(BT):
                dve.bn_stats(stats[:, m, :], tile(m)).then_inc(stats_done, 1)
            for m in range(BT):
                if m == 0:
                    dve.wait_ge(stats_done, BT * b + BT)
                    dve.memset(tick[:], 0.0)
                dve.bn_aggr(mv[:, m, :], stats[:, m, :]).then_inc(mv_done, 1)
            dve.wait_ge(mv_done, BT * b + BT)
            dve.tensor_scalar(var[:], mv[:, :, 1], 1e-5, None, ALU.add).then_inc(var_done, 1)
            dve.wait_ge(rstd_done, b + 1)
            for m in range(BT):
                dve.tensor_scalar(xn[:, m, :], tile(m), mv[:, m, 0:1], rstd[:, m:m + 1],
                                  ALU.subtract, ALU.mult).then_inc(xn_done, 1)
            dve.wait_ge(hi_done, b + 1)
            dve.tensor_tensor(xl[:].rearrange("p c n -> p (c n)"), bank[0][:],
                              xh[:].bitcast(F32).rearrange("p c n -> p (c n)"), ALU.subtract).then_inc(lo_done, 1)
            dve.wait_ge(q_proj, b + 1)
            for m in range(2):
                for c in range(CH):
                    last = dve.tensor_scalar(qm[:, m, c, :], bank[1][:, c * SEQ:(c + 1) * SEQ], par[:, m:m + 1],
                                             bqm[:, m, c:c + 1], ALU.mult, ALU.add)
            last.then_inc(q_done, 1)
            dve.wait_ge(v_proj, b + 1)
            for t in range(BT):
                last = dve.tensor_tensor(vg[:, t, :, 0:D1], bank[1][:, t * HID:(t + 1) * HID]
                                         .rearrange("p (h d) -> p h d", h=HEADS1),
                                         bv[:].rearrange("p (h d) -> p h d", h=HEADS1), ALU.add)
            last.then_inc(v_done, 1)
            head_max(b, 0)
            router_scores(b)
            for h in range(HEADS1):
                if h + 1 < HEADS1:
                    head_max(b, h + 1)
                copy_turn(b, h)
                if h in HEAD_OF_UP:
                    hidden(b, HEAD_OF_UP.index(h))
                if h == 9:
                    normalise(b, 0)
            normalise(b, 1)
            dve.wait_ge(thy_done, b + 1)
            dve.scalar_tensor_tensor(gy[:], thy[:], 1.0, bank[1][:], ALU.add, ALU.mult).then_inc(gy_done, 1)
            dve.wait_ge(wo_done, b + 1)
            for t in range(BT):
                last = dve.tensor_tensor(s1[:, t], bank[1][:, t * HID:(t + 1) * HID], bo[:], ALU.add)
            last.then_inc(s1_done, 1)
            dve.wait_ge(s1_done, b + 1)
            wait(dve, xo_done, b)
            dve.wait_ge(gy_done, b + 1)
            dve.scalar_tensor_tensor(prod[:], s1[:].rearrange("p t n -> p (t n)"), 0.5, gy[:],
                                     ALU.mult, ALU.mult).then_inc(prod_done, 1)

        program(dve, body)

    @block.scalar
    def _(act):
        def exps(b, h):
            act.wait_ge(max_done, HEADS1 * b + h + 1)
            wait(act, turned, TURNS * b + transposes_before_head(h - 2) + 1 if h >= 2 else TURNS * b)
            act.activation(prob[:, h % 2, 0:P], bank[2 + h % 2][:, 0:P], ACT.Exp, bias=nmax[:, h, 0:1])
            act.activation(prob[:, h % 2, P:3 * P], bank[2 + h % 2][:, P:3 * P], ACT.Exp,
                           bias=nmax[:, h, 1:2]).then_inc(exp_done, 1)

        def tanhs(b, u):
            t, g = u // (UNITS // BT), u % (UNITS // BT)
            act.wait_ge(up_done, UNITS * b + u + 1)
            act.wait_ge(route, ROUTE * b + ROUTE)
            wait(act, tu_done, UNITS * b + u)
            for e in range(EG):
                c = slice(e * P, (e + 1) * P)
                last = act.activation(th[:, c], bank[6][:, c], ACT.Tanh,
                                      scale=half_s[:, t, g * EG + e:g * EG + e + 1])
            last.then_inc(tanh_done, 1)

        def copy_hidden(b, u):
            t, g = u // (UNITS // BT), u % (UNITS // BT)
            n = TURNS * b + transposes_before_unit(u)
            act.wait_ge(turned, n + 1)
            act.activation(hT[:, t, g * EG:(g + 1) * EG, :].rearrange("p e n -> p (e n)"), bank[4][:, 0:GE],
                           ACT.Copy).then_inc(turn_copied, 1)

        def body(b):
            act.wait_ge(xT_done, b + 1)
            act.activation(xh[:].rearrange("p c n -> p (c n)"), bank[0][:], ACT.Copy).then_inc(hi_done, 1)
            act.wait_ge(k_proj, b + 1)
            for c in range(CH):
                last = act.activation(kT[:, c, :], bank[0][:, c * SEQ:(c + 1) * SEQ], ACT.Identity,
                                      bias=bk[:, c:c + 1])
            last.then_inc(k_done, 1)
            act.wait_ge(r_proj, b + 1)
            act.activation(en[:].rearrange("p t e -> p (t e)"), bank[0][:, 0:BT * EXPERTS], ACT.Exp, scale=-1.0)\
                .then_inc(r_exp, 1)
            exps(b, 0)
            for h in range(HEADS1):
                if h + 1 < HEADS1:
                    exps(b, h + 1)
                if h in HEAD_OF_UP:
                    tanhs(b, HEAD_OF_UP.index(h))
                if h - 1 in HEAD_OF_UP:
                    copy_hidden(b, HEAD_OF_UP.index(h - 1))
            act.wait_ge(y_done, b + 1)
            act.activation(thy[:], bank[1][:], ACT.Tanh, scale=0.5).then_inc(thy_done, 1)
            act.wait_ge(oT_done, b + 1)
            act.activation(oT[:].rearrange("p c n -> p (c n)"), bank[0][:], ACT.Copy).then_inc(oT_copied, 1)

        program(act, body)

    @block.tensor
    def _(pe):
        pe.wait_ge(once, 4)

        def three(out, a_hi, a_lo, b_hi, b_lo, first, last):
            pe.matmul(out, a_hi, b_hi, start=first, stop=False)
            pe.matmul(out, a_hi, b_lo, start=False, stop=False)
            return pe.matmul(out, a_lo, b_hi, start=False, stop=last)

        def columns(out, off):
            for f in range(CH):
                w = slice(off + f * P, off + (f + 1) * P)
                for c in range(CH):
                    last = three(out[:, f * SEQ:(f + 1) * SEQ], wqkv_hi[:, c, w], wqkv_lo[:, c, w],
                                 xh[:, c, :], xl[:, c, :], c == 0, c == CH - 1)
            return last

        def scores(b, h):
            wait(pe, exp_done, HEADS1 * b + h - 1)
            c, r = h // 8, slice(32 * (h % 8 // 2), 32 * (h % 8 // 2) + 32)
            out = bank[2 + h % 2]
            for o, keys, queries in ((0, 0, 0), (2 * P, P, P)):
                pe.matmul(out[:, o:o + P], qm[r, h % 2, c, queries:queries + P], kT[r, c, keys:keys + P],
                          start=True, stop=False)
                pe.matmul(out[:, o:o + P], identb[:], causal[:], start=False, stop=True)
            pe.matmul(out[:, P:2 * P], qm[r, h % 2, c, P:SEQ], kT[r, c, 0:P],
                      start=True, stop=True).then_inc(scored, 1)

        def turn(b, h):
            n = TURNS * b + transposes_before_head(h)
            pe.wait_ge(exp_done, HEADS1 * b + h + 1)
            wait(pe, turn_copied, n)
            for i in range(3):
                last = pe.transpose(bank[4][:, i * P:(i + 1) * P], prob[:, h % 2, i * P:(i + 1) * P], ident[:])
            last.then_inc(turned, 1)

        def product(b, h):
            n = TURNS * b + transposes_before_head(h)
            pe.wait_ge(turn_copied, n + 1)
            if h % 8 == 0:
                wait(pe, norm_done, 2 * b + h // 8)
            f = h // 8
            for t, i, j in ((0, 0, 0), (1, 1, 0), (1, 2, 1)):
                o = (t * 8 + h % 8) * (D1 + 1)
                last = pe.matmul(bank[5][:, o:o + D1 + 1], probT[:, h % 2, i * P:(i + 1) * P], vg[:, j, h, :],
                                 start=(i < 2), stop=(i != 1))
            if h % 8 == 7:
                last.then_inc(pv_done, 1)

        def up(b, u):
            t, g = u // (UNITS // BT), u % (UNITS // BT)
            wait(pe, h_done, UNITS * b + u)
            for i in range(2):
                w = slice(i * NE + g * GE, i * NE + (g + 1) * GE)
                for c in range(CH):
                    s = slice(t * P, (t + 1) * P)
                    last = three(bank[6 + i][:, 0:GE], xh[:, c, s], xl[:, c, s], w13_hi[:, c, w], w13_lo[:, c, w],
                                 c == 0, c == CH - 1)
            last.then_inc(up_done, 1)

        def turn_hidden(b, u):
            n = TURNS * b + transposes_before_unit(u)
            pe.wait_ge(h_done, UNITS * b + u + 1)
            pe.wait_ge(turn_copied, n)
            for e in range(EG):
                last = pe.transpose(bank[4][:, e * P:(e + 1) * P], hh[:, e * P:(e + 1) * P], ident[:])
            last.then_inc(turned, 1)

        def body(b):
            pe.wait_ge(xn_done, BT * b + BT)
            wait(pe, oT_copied, b)
            for m in range(BT):
                for c in range(CH):
                    last = pe.transpose(bank[0][:, c * SEQ + m * P:c * SEQ + (m + 1) * P],
                                        xn[:, m, c * P:(c + 1) * P], ident[:])
            last.then_inc(xT_done, 1)
            pe.wait_ge(lo_done, b + 1)
            wait(pe, s1_done, b)
            columns(bank[1], 0).then_inc(q_proj, 1)
            columns(bank[0], HID).then_inc(k_proj, 1)
            pe.wait_ge(q_done, b + 1)
            for t in range(BT):
                for c in range(CH):
                    s = slice(t * P, (t + 1) * P)
                    last = three(bank[1][:, t * HID:(t + 1) * HID], xh[:, c, s], xl[:, c, s],
                                 wqkv_hi[:, c, 2 * HID:3 * HID], wqkv_lo[:, c, 2 * HID:3 * HID], c == 0, c == CH - 1)
            last.then_inc(v_proj, 1)
            pe.wait_ge(k_done, b + 1)
            for t in range(BT):
                for c in range(CH):
                    s = slice(t * P, (t + 1) * P)
                    last = three(bank[0][:, t * EXPERTS:(t + 1) * EXPERTS], xh[:, c, s], xl[:, c, s],
                                 router_hi[:, c, :], router_lo[:, c, :], c == 0, c == CH - 1)
            last.then_inc(r_proj, 1)
            scores(b, 0)
            pe.wait_ge(v_done, b + 1)
            for h in range(HEADS1):
                if h + 1 < HEADS1:
                    scores(b, h + 1)
                if h in HEAD_OF_UP:
                    up(b, HEAD_OF_UP.index(h))
                turn(b, h)
                if h:
                    product(b, h - 1)
                if h - 1 in HEAD_OF_UP:
                    turn_hidden(b, HEAD_OF_UP.index(h - 1))
            product(b, HEADS1 - 1)
            for t in range(BT):
                for e in range(EX):
                    last = pe.matmul(bank[1][:, t * HID:(t + 1) * HID], hT[:, t, e, :], w2[:, e, :],
                                     start=(e == 0), stop=(e == EX - 1))
            last.then_inc(y_done, 1)
            pe.wait_ge(norm_done, 2 * b + 2)
            pe.wait_ge(r_exp, b + 1)
            for m in range(BT):
                for c in range(CH):
                    last = pe.transpose(bank[0][:, c * SEQ + m * P:c * SEQ + (m + 1) * P],
                                        on[:, m, c * P:(c + 1) * P], ident[:])
            last.then_inc(oT_done, 1)
            pe.wait_ge(oT_copied, b + 1)
            pe.wait_ge(gy_done, b + 1)
            for t in range(BT):
                for c in range(CH):
                    last = pe.matmul(bank[1][:, t * HID:(t + 1) * HID], oT[:, c, t * P:(t + 1) * P], wo[:, c, :],
                                     start=(c == 0), stop=(c == CH - 1))
            last.then_inc(wo_done, 1)

        program(pe, body)


def kernel(**inputs):
    import numpy as np
    import concourse.bacc as bacc
    from concourse.bass_utils import run_bass_kernel_spmd

    a = {n: np.asarray(v) for n, v in inputs.items()}

    def rows(name):
        v = a[name].reshape(1, -1)
        return np.broadcast_to(v, (P, v.shape[1]))

    heads = a["L0_attn_qkv_w"].reshape(PAIRS, 2, 3, D0, HID).transpose(0, 2, 1, 3, 4).reshape(PAIRS, 3 * P, HID)
    gates = a["L0_attn_gate_w"].reshape(PAIRS, P, HID)
    w0 = np.concatenate([heads, gates], axis=1).transpose(0, 2, 1).reshape(PAIRS, CH, P, COLS)
    w0 = np.concatenate([w0.transpose(0, 2, 1, 3).reshape(PAIRS, P, CH * COLS),
                         a["L0_attn_out_w"].T.reshape(PAIRS, P, HID),
                         a["L0_attn_norm_w"].reshape(PAIRS, P, 1)], axis=2)
    e1 = np.concatenate([a["L1_ffn_w1"].reshape(-1, HID), a["L1_ffn_sw1"]], axis=0)
    e3 = np.concatenate([a["L1_ffn_w3"].reshape(-1, HID), a["L1_ffn_sw3"]], axis=0)
    arrays = {
        "x": a["L0_attn_hidden_states"].reshape(TOK, HID),
        "w0": w0,
        "ffn_w": np.ascontiguousarray(a["L0_ffn_weight"].T).view(np.int32),
        "ffn_sc": rows("L0_ffn_w_scale"),
        "ffn_b": rows("L0_ffn_bias"),
        "wqkv1": np.concatenate([a["L1_attn_Wq"].T, a["L1_attn_Wk"].T, a["L1_attn_Wv"].T], axis=1),
        "wo1": a["L1_attn_Wo"].T,
        "bq": a["L1_attn_bq"].reshape(CH, P).T,
        "bk": a["L1_attn_bk"].reshape(CH, P).T,
        "bv": rows("L1_attn_bv"),
        "bo": rows("L1_attn_bo"),
        "ebias": rows("L1_ffn_expert_bias"),
        "router": a["L1_ffn_gate_w"].T,
        "w13": np.concatenate([e1.T, e3.T], axis=1),
        "w2": np.concatenate([a["L1_ffn_w2"].transpose(0, 2, 1), a["L1_ffn_sw2"].T[None]], axis=0),
    }
    nc = bacc.Bacc("TRN2", target_bir_lowering=False, num_devices=1)
    given, args = {}, []
    for name, v in arrays.items():
        v = np.ascontiguousarray(v)
        given[f"in_{name}"] = v
        args.append(nc.dram_tensor(f"in_{name}", v.shape, mybir.dt.from_np(v.dtype), kind="ExternalInput").ap())
    args.append(nc.dram_tensor("out_0", (TOK, HID), F32, kind="ExternalOutput").ap())
    build(nc, *args)
    r = run_bass_kernel_spmd(nc, [given], core_ids=[0])
    return r.results[0]["out_0"].reshape(BATCHES, SEQ, HID)
```

```python
from contextlib import ExitStack

import concourse.bass as bass
from concourse import mybir

ALU = mybir.AluOpType
ACT = mybir.ActivationFunctionType
AX = mybir.AxisListType
F32 = mybir.dt.float32
F32R = mybir.dt.float32r
F16 = mybir.dt.float16
BF16 = mybir.dt.bfloat16
I8 = mybir.dt.int8
I32 = mybir.dt.int32
U32 = mybir.dt.uint32

P = 128
BATCHES, SEQ, HID = 8, 256, 256
TOK = BATCHES * SEQ
TILES = TOK // P
CH = HID // P

HEADS0, D0 = 32, 64
PAIRS = HEADS0 // 2
GROUP = 512
GROUPS = TOK // GROUP
GT = GROUP // P
COLS = 4 * P
WROW = CH * COLS + HID + 1
STEPS = PAIRS * GROUPS
BODY = 2 * GROUPS
ROUND = 12582912.0

HEADS1, D1 = 16, 16
EXPERTS = 8
EX = EXPERTS + 1
EG = 3
BT = SEQ // P
UNITS = BT * (EX // EG)


def wait(eng, sem, value):
    if isinstance(value, int) and value <= 0:
        return
    eng.wait_ge(sem, value)


def slopes():
    base = 1.0 / 2.0 ** (8.0 / HEADS0)
    factor = 1.0 - 0 / (32 - 1 + 1e-05) + 1e-05
    return [base ** (h + 1.0) * factor for h in range(HEADS0)]


def build(nc, x_d, w0_d, ffn_w_d, ffn_sc_d, ffn_b_d, wqkv1_d, wo1_d, bq_d, bk_d, bv_d, bo_d,
          ebias_d, w13_d, w2_d, out_d):
    with ExitStack() as keep:
        def ksb(name, shape, dt):
            return keep.enter_context(nc.sbuf_tensor(name, shape, dt))

        bank = [keep.enter_context(nc.psum_tensor(f"bank{i}", [P, 512], F32)) for i in range(8)]
        x = ksb("x", [P, TILES, HID], F32)
        acc = ksb("acc", [P, TILES, HID], F32)
        ssq = ksb("ssq", [P, TOK], F32)
        g16 = ksb("g16", [P, TILES, HID], F16)
        ident = ksb("ident", [P, P], F32)
        identb = ksb("identb", [P, P], BF16)
        with ExitStack() as layer0:
            xn_hi = layer0.enter_context(nc.sbuf_tensor("xn_hi", [P, CH, TOK], F32R))
            xn_lo = layer0.enter_context(nc.sbuf_tensor("xn_lo", [P, CH, TOK], F32R))
            decay = layer0.enter_context(nc.sbuf_tensor("decay", [P, HEADS0, 2 * P], F32))
            norm_and_ffn(nc, bank, x, g16, ident, identb, xn_hi, xn_lo, decay, ssq, acc,
                         x_d, ffn_w_d, ffn_sc_d, ffn_b_d)
            linear_attention(nc, bank, ident, xn_hi, xn_lo, decay, acc, ssq, w0_d)
        layer_one(nc, bank, x, acc, ssq, g16, ident, identb, wqkv1_d, wo1_d, bq_d, bk_d, bv_d, bo_d,
                  ebias_d, w13_d, w2_d, out_d)


def norm_and_ffn(nc, bank, x, g16, ident, identb, xn_hi, xn_lo, decay, ssq, acc,
                 x_d, ffn_w_d, ffn_sc_d, ffn_b_d):
    with ExitStack() as ctx:
        def sb(name, shape, dt):
            return ctx.enter_context(nc.sbuf_tensor(name, shape, dt))

        def sem(name):
            return ctx.enter_context(nc.semaphore(name))

        xn = sb("xn", [P, TILES, HID], F32)
        qr = sb("qr", [P, TILES, HID], F32)
        q16 = sb("q16", [P, TILES, HID], BF16)
        qT = sb("qT", [P, TILES // 2, CH, SEQ], BF16)
        stats = sb("stats", [P, TILES, 6], F32)
        mv = sb("mv", [P, TILES, 2], F32)
        var = sb("var", [P, TILES], F32)
        half = sb("half", [P, TILES], F32)
        rstd = sb("rstd", [P, TILES], F32)
        absmax = sb("absmax", [P, TILES], F32)
        in_sc = sb("in_sc", [P, TILES], F32)
        in_inv = sb("in_inv", [P, TILES], F32)
        w8 = sb("w8", [P, CH, HID // 4], I32)
        wb = sb("wb", [P, CH, HID], BF16)
        w_sc = sb("w_sc", [P, HID], F32)
        bias = sb("bias", [P, HID], F32)
        z = sb("z", [P, 2, HID], F32)
        z16 = sb("z16", [P, 2, 2, HID], F16)
        sg16 = sb("sg16", [P, 2, 2, HID], F16)
        dist_i = sb("dist_i", [P, 2 * P], I32)
        dist = sb("dist", [P, 2 * P], F32)

        x_in = [sem(f"x_in{g}") for g in range(4)]
        w_in = sem("ffn_w_in")
        consts = sem("consts")
        idents = sem("idents")
        dist_ready = sem("dist_ready")
        decay_exp = sem("decay_exp")
        decay_ready = sem("decay_ready")
        stats_done = sem("stats_done")
        mv_done = sem("mv_done")
        var_done = sem("var_done")
        rstd_done = sem("rstd_done")
        xn_done = sem("xn_done")
        absmax_done = sem("absmax_done")
        scale_done = sem("scale_done")
        quant_step = sem("quant_step")
        q_done = sem("q_done")
        wb_done = sem("wb_done")
        xT_done = sem("xT_done")
        hi_done = sem("hi_done")
        lo_done = sem("lo_done")
        qT_done = sem("qT_done")
        qT_copied = sem("qT_copied")
        lin_done = sem("lin_done")
        z_step = sem("z_step")
        z_done = sem("z_done")
        sig_done = sem("sig_done")
        g_done = sem("g_done")
        block = ctx.enter_context(nc.Block())
        NG = TILES // 4
        NB = TILES // 2

        @block.sync
        def _(sp):
            xv = x_d.rearrange("(g t p) d -> g p t d", g=NG, p=P)
            for g in range(NG):
                sp.dma_start(x[:, 4 * g:4 * g + 4, :], xv[g]).then_inc(x_in[g], 16)
            sp.dma_start(w8[:], ffn_w_d.rearrange("(c p) n -> p c n", p=P)).then_inc(w_in, 16)
            sp.dma_start(w_sc[:], ffn_sc_d).then_inc(w_in, 16)
            sp.dma_start(bias[:], ffn_b_d).then_inc(w_in, 16)

        @block.gpsimd
        def _(pool):
            pool.memset(half[:], -0.5).then_inc(consts, 1)
            pool.memset(ident[:], 0.0).then_inc(consts, 1)
            pool.memset(identb[:], 0.0).then_inc(consts, 1)
            pool.wait_ge(consts, 3)
            pool.affine_select(out=ident[:], in_=ident[:], compare_op=ALU.not_equal, fill=1.0,
                               base=0, pattern=[[-1, P]], channel_multiplier=1).then_inc(idents, 1)
            pool.affine_select(out=identb[:], in_=identb[:], compare_op=ALU.not_equal, fill=1.0,
                               base=0, pattern=[[-1, P]], channel_multiplier=1).then_inc(idents, 1)
            pool.iota(dist_i[:], pattern=[[1, 2 * P]], base=0, channel_multiplier=-1).then_inc(dist_ready, 1)
            pool.wait_ge(dist_ready, 1)
            pool.tensor_scalar(dist[:], dist_i[:], 0.0, 1.0, ALU.max, ALU.mult).then_inc(dist_ready, 1)
            for g in range(NG):
                pool.wait_ge(var_done, g + 1)
                s = slice(4 * g, 4 * g + 4)
                pool.tensor_tensor(rstd[:, s], var[:, s], half[:, s], ALU.pow).then_inc(rstd_done, 1)
            pool.wait_ge(decay_exp, HEADS0)
            pool.affine_select(out=decay[:, :, 0:P], in_=decay[:, :, 0:P], compare_op=ALU.is_ge, fill=0.0,
                               base=0, pattern=[[0, HEADS0], [1, P]], channel_multiplier=-1)\
                .then_inc(decay_ready, 1)
            pool.memset(ssq[:], 0.0).then_inc(decay_ready, 1)
            pool.memset(acc[:], 0.0).then_inc(decay_ready, 1)

        @block.vector
        def _(dve):
            for g in range(NG):
                dve.wait_ge(x_in[g], 16)
                for t in range(4 * g, 4 * g + 4):
                    dve.bn_stats(stats[:, t, :], x[:, t, :]).then_inc(stats_done, 1)
                for t in range(4 * g, 4 * g + 4):
                    dve.wait_ge(stats_done, t + 1)
                    dve.bn_aggr(mv[:, t, :], stats[:, t, :]).then_inc(mv_done, 1)
                dve.wait_ge(mv_done, 4 * g + 4)
                s = slice(4 * g, 4 * g + 4)
                dve.tensor_scalar(var[:, s], mv[:, s, 1], 1e-5, None, ALU.add).then_inc(var_done, 1)
            dve.wait_ge(w_in, 48)
            dve.tensor_copy(wb[:], w8[:].bitcast(I8)).then_inc(wb_done, 1)
            for g in range(NG):
                s = slice(4 * g, 4 * g + 4)
                dve.wait_ge(rstd_done, g + 1)
                for t in range(4 * g, 4 * g + 4):
                    dve.tensor_scalar(xn[:, t, :], x[:, t, :], mv[:, t, 0:1], rstd[:, t:t + 1],
                                      ALU.subtract, ALU.mult).then_inc(xn_done, 1)
                dve.wait_ge(xn_done, 4 * g + 4)
                dve.tensor_reduce(absmax[:, s], xn[:, s, :], AX.X, ALU.max,
                                  apply_absolute_value=True).then_inc(absmax_done, 1)
                dve.wait_ge(absmax_done, g + 1)
                dve.tensor_scalar(in_sc[:, s], absmax[:, s], 1e-7, 1.0 / 127.0, ALU.max, ALU.mult)\
                    .then_inc(scale_done, 1)
                dve.wait_ge(scale_done, 2 * g + 1)
                dve.reciprocal(in_inv[:, s], in_sc[:, s]).then_inc(scale_done, 1)
                dve.wait_ge(scale_done, 2 * g + 2)
                for t in range(4 * g, 4 * g + 4):
                    dve.tensor_scalar(qr[:, t, :], xn[:, t, :], in_inv[:, t:t + 1], ROUND,
                                      ALU.mult, ALU.add).then_inc(quant_step, 1)
                dve.wait_ge(quant_step, 5 * g + 4)
                dve.tensor_scalar(qr[:, s, :], qr[:, s, :], ROUND + 127.0, ROUND - 128.0,
                                  ALU.min, ALU.max).then_inc(quant_step, 1)
                dve.wait_ge(quant_step, 5 * g + 5)
                dve.tensor_scalar(q16[:, s, :], qr[:, s, :], -ROUND, None, ALU.add).then_inc(q_done, 1)
                for b in range(2 * g, 2 * g + 2):
                    dve.wait_ge(hi_done, b + 1)
                    c = slice(b * SEQ, (b + 1) * SEQ)
                    dve.tensor_tensor(xn_lo[:, :, c], bank[b % 2][:].rearrange("p (c n) -> p c n", c=CH),
                                      xn_hi[:, :, c].bitcast(F32), ALU.subtract).then_inc(lo_done, 1)
            for b in range(NB):
                dve.wait_ge(lin_done, b + 1)
                for m in range(2):
                    t = 2 * b + m
                    if b:
                        dve.wait_ge(z_done, 2 * b - 1 + m)
                    dve.scalar_tensor_tensor(z[:, m, :], bank[4 + b % 2][:, m * HID:(m + 1) * HID],
                                             in_sc[:, t:t + 1], w_sc[:], ALU.mult, ALU.mult).then_inc(z_step, 1)
                for m in range(2):
                    t = 2 * b + m
                    dve.wait_ge(z_step, t + 1)
                    if b >= 2:
                        dve.wait_ge(g_done, b - 1)
                    dve.tensor_tensor(z16[:, b % 2, m, :], z[:, m, :], bias[:], ALU.add).then_inc(z_done, 1)
                if b:
                    dve.wait_ge(sig_done, b)
                    dve.tensor_tensor(g16[:, 2 * b - 2:2 * b, :], z16[:, (b - 1) % 2], sg16[:, (b - 1) % 2],
                                      ALU.mult).then_inc(g_done, 1)
            dve.wait_ge(sig_done, NB)
            dve.tensor_tensor(g16[:, TILES - 2:TILES, :], z16[:, (NB - 1) % 2], sg16[:, (NB - 1) % 2],
                              ALU.mult).then_inc(g_done, 1)

        @block.scalar
        def _(act):
            act.wait_ge(dist_ready, 2)
            for h, s in enumerate(slopes()):
                act.activation(decay[:, h, :], dist[:], ACT.Exp, scale=-float(s)).then_inc(decay_exp, 1)

            def copy_q(b):
                act.wait_ge(qT_done, b + 1)
                act.activation(qT[:, b], bank[2 + b % 2][:, 0:256].bitcast(BF16)
                               .rearrange("p (c n) -> p c n", c=CH), ACT.Copy).then_inc(qT_copied, 1)

            for b in range(NB):
                act.wait_ge(xT_done, b + 1)
                act.activation(xn_hi[:, :, b * SEQ:(b + 1) * SEQ],
                               bank[b % 2][:].rearrange("p (c n) -> p c n", c=CH), ACT.Copy).then_inc(hi_done, 1)
                copy_q(b)
            for b in range(NB):
                act.wait_ge(z_done, 2 * b + 2)
                if b >= 2:
                    act.wait_ge(g_done, b - 1)
                act.activation(sg16[:, b % 2], z16[:, b % 2], ACT.Sigmoid).then_inc(sig_done, 1)

        @block.tensor
        def _(pe):
            pe.wait_ge(idents, 2)
            pe.wait_ge(wb_done, 1)

            def linear(b):
                pe.wait_ge(qT_copied, b + 1)
                if b >= 2:
                    pe.wait_ge(z_step, 2 * b - 2)
                for m in range(2):
                    for c in range(CH):
                        last = pe.matmul(bank[4 + b % 2][:, m * HID:(m + 1) * HID],
                                         qT[:, b, c, m * P:(m + 1) * P], wb[:, c, :],
                                         start=(c == 0), stop=(c == CH - 1))
                last.then_inc(lin_done, 1)

            for b in range(NB):
                pe.wait_ge(xn_done, 2 * b + 2)
                if b >= 2:
                    pe.wait_ge(lo_done, b - 1)
                for m in range(2):
                    for c in range(CH):
                        last = pe.transpose(bank[b % 2][:, c * SEQ + m * P:c * SEQ + (m + 1) * P],
                                            xn[:, 2 * b + m, c * P:(c + 1) * P], ident[:])
                last.then_inc(xT_done, 1)
                pe.wait_ge(q_done, b // 2 + 1)
                if b >= 2:
                    pe.wait_ge(qT_copied, b - 1)
                for m in range(2):
                    for c in range(CH):
                        last = pe.transpose(bank[2 + b % 2][:].bitcast(BF16)[:, c * SEQ + m * P:c * SEQ + (m + 1) * P],
                                            q16[:, 2 * b + m, c * P:(c + 1) * P], identb[:])
                last.then_inc(qT_done, 1)
            for b in range(NB):
                linear(b)


def linear_attention(nc, bank, ident, xn_hi, xn_lo, decay, acc, ssq, w0_d):
    with ExitStack() as ctx:
        def sb(name, shape, dt):
            return ctx.enter_context(nc.sbuf_tensor(name, shape, dt))

        def sem(name):
            return ctx.enter_context(nc.semaphore(name))

        stage = [sb(f"w_stage{i}", [P, WROW], F32) for i in range(2)]
        w_hi = [sb(f"w_hi{i}", [P, CH, COLS], F32R) for i in range(2)]
        w_lo = [sb(f"w_lo{i}", [P, CH, COLS], F32R) for i in range(2)]
        wo = [sb(f"wo{i}", [P, HID], F32) for i in range(2)]
        wo_hi = [sb(f"wo_hi{i}", [P, HID], F32R) for i in range(2)]
        wo_lo = [sb(f"wo_lo{i}", [P, HID], F32R) for i in range(2)]
        q = sb("q", [P, 2, GROUP], F32)
        k = sb("k", [P, 2, GROUP], F32)
        vT = sb("vT", [P, GROUP], F32)
        v = sb("v", [P, GT, P], F32)
        th = sb("th", [P, 2, GROUP], F32)
        aw = sb("aw", [P, 4, 3 * P], F32)
        gated = sb("gated", [P, GROUP], F32)
        gated_hi = sb("gated_hi", [P, 2, GROUP], F32R)
        gated_lo = sb("gated_lo", [P, 2, GROUP], F32R)
        sq = sb("sq", [P, 2, GROUP], F32)

        w_in = [sem(f"w0_in{i}") for i in range(2)]
        w_split = sem("w_split")
        w_hi_done = sem("w_hi_done")
        wo_ready = sem("wo_ready")
        projected = sem("projected")
        activated = sem("activated")
        scored = sem("scored")
        decayed = sem("decayed")
        attended = sem("attended")
        squared = sem("squared")
        ssq_added = sem("ssq_added")
        gated_done = sem("gated_done")
        gated_high = sem("gated_high")
        gated_split = sem("gated_split")
        wo_high = sem("wo_high")
        wo_split = sem("wo_split")
        v_turned = sem("v_turned")
        v_copied = sem("v_copied")
        out_done = sem("out_done")
        acc_done = sem("acc_done")
        block = ctx.enter_context(nc.Block())

        @block.sync
        def _(sp):
            def load(pair, i):
                wait(sp, w_split, pair - 1)
                wait(sp, wo_ready, pair - 1)
                sp.dma_start(stage[i][:], w0_d[pair]).then_inc(w_in[i], 16)

            load(0, 0)
            load(1, 1)
            with sp.Fori(1, PAIRS // 2) as it:
                load(2 * it, 0)
                load(2 * it + 1, 1)

        @block.gpsimd
        def _(pool):
            def split(pair, i):
                pool.wait_ge(w_hi_done, pair + 1)
                wide = stage[i][:, 0:CH * COLS].rearrange("p (c n) -> p c n", c=CH)
                pool.tensor_tensor(w_lo[i][:], wide, w_hi[i][:].bitcast(F32), ALU.subtract).then_inc(w_split, 1)

            def split_out_weights(pair, i):
                pool.wait_ge(wo_high, pair + 1)
                pool.tensor_tensor(wo_lo[i][:], wo[i][:], wo_hi[i][:].bitcast(F32), ALU.subtract)\
                    .then_inc(wo_split, 1)

            def split_gated(t, s):
                pool.wait_ge(gated_high, t + 1)
                pool.tensor_tensor(gated_lo[:, s % 2, :], gated[:], gated_hi[:, s % 2, :].bitcast(F32),
                                   ALU.subtract).then_inc(gated_split, 1)

            def add_squares(t, s):
                pool.wait_ge(squared, t + 1)
                g = s % GROUPS
                wait(pool, ssq_added, t + 1 - GROUPS)
                pool.tensor_tensor(ssq[:, g * GROUP:(g + 1) * GROUP], ssq[:, g * GROUP:(g + 1) * GROUP],
                                   sq[:, s % 2, :], ALU.add).then_inc(ssq_added, 1)

            def steps(it, last=False):
                for s in range(BODY):
                    add_squares(it * BODY + s, s)
                    split_gated(it * BODY + s, s)
                    if s == 0:
                        split(2 * it + 1, 1)
                    if s == 1:
                        split_out_weights(2 * it + 1, 1)
                    if s == GROUPS and not last:
                        split(2 * it + 2, 0)
                    if s == GROUPS + 1 and not last:
                        split_out_weights(2 * it + 2, 0)

            split(0, 0)
            split_out_weights(0, 0)
            steps(0)
            with pool.Fori(1, STEPS // BODY - 1) as it:
                steps(it)
            steps(STEPS // BODY - 1, True)

        @block.scalar
        def _(act):
            def silu(n, s, what, src, dst):
                act.wait_ge(projected, 4 * n + what + 1)
                act.activation(dst, src, ACT.Silu).then_inc(activated, 1)

            def qkv(n, s):
                silu(n, s, 0, bank[0][:], q[:, s % 2, :])
                silu(n, s, 1, bank[1][:], k[:, s % 2, :])
                silu(n, s, 2, bank[0][:], vT[:])

            def gate(n, s):
                act.wait_ge(projected, 4 * n + 4)
                wait(act, gated_done, n - 1)
                act.activation(th[:, s % 2, :], bank[1][:], ACT.Tanh, scale=0.5).then_inc(activated, 1)

            def high_weights(pair, i, turn):
                wait(act, projected, 4 * GROUPS * (pair - 1))
                act.wait_ge(w_in[i], 16 * (turn + 1))
                act.activation(w_hi[i][:], stage[i][:, 0:CH * COLS].rearrange("p (c n) -> p c n", c=CH),
                               ACT.Copy).then_inc(w_hi_done, 1)

            def high_out_weights(pair, i):
                act.wait_ge(wo_ready, pair + 1)
                wait(act, out_done, 2 * GROUPS * (pair - 1))
                act.activation(wo_hi[i][:], wo[i][:], ACT.Copy).then_inc(wo_high, 1)

            def high_gated(t, s):
                act.wait_ge(gated_done, t + 1)
                wait(act, out_done, 2 * t - 2)
                act.activation(gated_hi[:, s % 2, :], gated[:], ACT.Copy).then_inc(gated_high, 1)

            def square(t, s):
                act.wait_ge(attended, t + 1)
                wait(act, ssq_added, t - 1)
                act.activation(sq[:, s % 2, :], bank[4][:], ACT.Square).then_inc(squared, 1)

            def steps(it, last=False):
                for s in range(BODY):
                    t = it * BODY + s
                    more = not (last and s == BODY - 1)
                    if s == 0:
                        high_weights(2 * it + 1, 1, it)
                    if s == GROUPS and not last:
                        high_weights(2 * it + 2, 0, it + 1)
                    if more:
                        qkv(t + 1, s + 1)
                    square(t, s)
                    if more:
                        gate(t + 1, s + 1)
                    high_gated(t, s)
                    if s == 0:
                        high_out_weights(2 * it + 1, 1)
                    if s == GROUPS and not last:
                        high_out_weights(2 * it + 2, 0)

            high_weights(0, 0, 0)
            high_out_weights(0, 0)
            qkv(0, 0)
            gate(0, 0)
            steps(0)
            with act.Fori(1, STEPS // BODY - 1) as it:
                steps(it)
            steps(STEPS // BODY - 1, True)

        @block.vector
        def _(dve):
            def out_weights(pair, i, turn):
                wait(dve, wo_split, pair - 1)
                dve.wait_ge(w_in[i], 16 * (turn + 1))
                dve.tensor_scalar(wo[i][:], stage[i][:, CH * COLS:CH * COLS + HID],
                                  stage[i][:, WROW - 1:WROW], 0.5, ALU.mult, ALU.mult).then_inc(wo_ready, 1)

            def decays(t, j, pair):
                dve.wait_ge(scored, 4 * t + j + 1)
                head = 2 * pair + j % 2
                dve.tensor_tensor(aw[:, j, 0:2 * P], bank[2 + j % 2][:, 0:2 * P], decay[:, head, :], ALU.mult)
                dve.tensor_tensor(aw[:, j, 2 * P:3 * P], bank[2 + j % 2][:, 2 * P:3 * P],
                                  decay[:, head, 0:P], ALU.mult).then_inc(decayed, 1)

            def copy_v(n):
                dve.wait_ge(v_turned, n + 1)
                dve.tensor_copy(v[:].rearrange("p t n -> p (t n)"), bank[7][:]).then_inc(v_copied, 1)

            def gates(t, s):
                dve.wait_ge(squared, t + 1)
                dve.wait_ge(activated, 4 * t + 4)
                wait(dve, gated_split, t)
                dve.scalar_tensor_tensor(gated[:], th[:, s % 2, :], 1.0, bank[4][:], ALU.add, ALU.mult)\
                    .then_inc(gated_done, 1)

            def accumulate(t, s, u):
                dve.wait_ge(out_done, 2 * t + u + 1)
                wait(dve, acc_done, 2 * (t - GROUPS) + u + 1)
                m = GT * (s % GROUPS) + 2 * u
                part = acc[:, m:m + 2, :].rearrange("p t n -> p (t n)")
                dve.tensor_tensor(part, bank[5 + u][:], part, ALU.add).then_inc(acc_done, 1)

            def steps(it, last=False):
                for s in range(BODY):
                    t = it * BODY + s
                    for j in range(4):
                        decays(t, j, 2 * it + s // GROUPS)
                    for u in range(2):
                        if s or not isinstance(it, int) or it:
                            accumulate(t - 1, s + BODY - 1, u)
                    gates(t, s)
                    if not (last and s == BODY - 1):
                        copy_v(t + 1)
                    if s == 0:
                        out_weights(2 * it + 1, 1, it)
                    if s == GROUPS and not last:
                        out_weights(2 * it + 2, 0, it + 1)

            out_weights(0, 0, 0)
            copy_v(0)
            steps(0)
            with dve.Fori(1, STEPS // BODY - 1) as it:
                steps(it)
            steps(STEPS // BODY - 1, True)
            for u in range(2):
                accumulate(STEPS - 1, BODY - 1, u)

        @block.tensor
        def _(pe):
            def columns(n, s, what, out):
                i, g = (s // GROUPS) % 2, s % GROUPS
                toks = slice(g * GROUP, (g + 1) * GROUP)
                cols = slice(what * P, (what + 1) * P)
                for c in range(CH):
                    for a, b in ((w_hi, xn_hi), (w_hi, xn_lo), (w_lo, xn_hi)):
                        last = pe.matmul(out, a[i][:, c, cols], b[:, c, toks],
                                         start=(c == 0 and a is w_hi and b is xn_hi),
                                         stop=(c == CH - 1 and a is w_lo))
                last.then_inc(projected, 1)

            def query(n, s, pair):
                pe.wait_ge(w_split, pair + 1)
                wait(pe, activated, 4 * n - 1)
                columns(n, s, 0, bank[0][:])

            def key(n, s):
                wait(pe, activated, 4 * n)
                columns(n, s, 1, bank[1][:])

            def value(n, s):
                pe.wait_ge(activated, 4 * n + 1)
                columns(n, s, 2, bank[0][:])

            def turn_value(n):
                pe.wait_ge(activated, 4 * n + 3)
                wait(pe, v_copied, n)
                for m in range(GT):
                    last = pe.transpose(bank[7][:, m * P:(m + 1) * P], vT[:, m * P:(m + 1) * P], ident[:])
                last.then_inc(v_turned, 1)

            def gate(n, s):
                pe.wait_ge(activated, 4 * n + 2)
                columns(n, s, 3, bank[1][:])

            def scores(t, s, j):
                pe.wait_ge(activated, 4 * t + 2)
                wait(pe, decayed, 4 * t + j - 1)
                b, r = (j // 2) * SEQ, slice(D0 * (j % 2), D0 * (j % 2 + 1))
                out = bank[2 + j % 2]
                pe.matmul(out[:, 0:2 * P], k[r, s % 2, b:b + P], q[r, s % 2, b:b + SEQ], start=True, stop=True)
                pe.matmul(out[:, 2 * P:3 * P], k[r, s % 2, b + P:b + SEQ], q[r, s % 2, b + P:b + SEQ],
                          start=True, stop=True).then_inc(scored, 1)

            def attend(t, s):
                pe.wait_ge(decayed, 4 * t + 4)
                pe.wait_ge(v_copied, t + 1)
                wait(pe, gated_done, t)
                wait(pe, squared, t)
                for b in range(2):
                    for tile in range(2):
                        for h in range(2):
                            r = slice(D0 * h, D0 * (h + 1))
                            cols = aw[:, 2 * b + h, 0:2 * P] if tile == 0 else aw[:, 2 * b + h, 2 * P:3 * P]
                            last = pe.matmul(bank[4][r, b * SEQ + tile * P:(b + 1) * SEQ], v[:, 2 * b + tile, r],
                                             cols, start=(tile == 0), stop=(tile == 1))
                last.then_inc(attended, 1)

            def back(t, s, pair):
                i = (s // GROUPS) % 2
                pe.wait_ge(gated_split, t + 1)
                pe.wait_ge(wo_split, pair + 1)
                for u in range(2):
                    wait(pe, acc_done, 2 * t + u - 1)
                    for m in range(2):
                        toks = slice((2 * u + m) * P, (2 * u + m + 1) * P)
                        for a, b in ((gated_hi, wo_hi), (gated_hi, wo_lo), (gated_lo, wo_hi)):
                            last = pe.matmul(bank[5 + u][:, m * HID:(m + 1) * HID], a[:, s % 2, toks], b[i][:],
                                             start=(a is gated_hi and b is wo_hi), stop=(a is gated_lo))
                    last.then_inc(out_done, 1)

            def steps(it, last=False):
                for s in range(BODY):
                    t = it * BODY + s
                    more = not (last and s == BODY - 1)
                    scores(t, s, 0)
                    scores(t, s, 1)
                    if more:
                        query(t + 1, s + 1, 2 * it + (s + 1) // GROUPS)
                    scores(t, s, 2)
                    scores(t, s, 3)
                    if s or not isinstance(it, int) or it:
                        back(t - 1, s + BODY - 1, 2 * it + (s - 1) // GROUPS)
                    if more:
                        key(t + 1, s + 1)
                        value(t + 1, s + 1)
                    attend(t, s)
                    if more:
                        turn_value(t + 1)
                        gate(t + 1, s + 1)

            query(0, 0, 0)
            key(0, 0)
            value(0, 0)
            turn_value(0)
            gate(0, 0)
            steps(0)
            with pe.Fori(1, STEPS // BODY - 1) as it:
                steps(it)
            steps(STEPS // BODY - 1, True)
            back(STEPS - 1, BODY - 1, PAIRS - 1)


ORDER = [4 * k + i for k in range(HEADS1 // 4) for i in (0, 2, 1, 3)]
SLOTS = len(ORDER)
QKVR = 3 * HID + EXPERTS


def score_bank(n):
    return 1 + (1 if n == SLOTS - 1 else n % 3)


def score_bank_before(n):
    return {0: -4, 1: -1, 2: -2, SLOTS - 1: SLOTS - 3}.get(n, n - 3)


def layer_one(nc, bank, x, acc, ssq, g16, ident, identb, wqkv_d, wo_d, bq_d, bk_d, bv_d, bo_d,
              ebias_d, w13_d, w2_d, out_d):
    with ExitStack() as ctx:
        def sb(name, shape, dt):
            return ctx.enter_context(nc.sbuf_tensor(name, shape, dt))

        def sem(name):
            return ctx.enter_context(nc.semaphore(name))

        NE = EX * P
        ones = sb("ones", [P, 1], F32)
        ms = sb("ms", [P, TILES], F32)
        half = sb("half1", [P, TILES], F32)
        rms = sb("rms", [P, TILES], F32)
        branch = sb("branch", [P, TILES, HID], F32)
        wqkv_hi = sb("wqkv_hi", [P, CH, QKVR], F32R)
        wqkv_lo = sb("wqkv_lo", [P, CH, QKVR], F32R)
        wo = sb("w_out1", [P, CH, HID], F32)
        w13_hi = sb("w13_hi", [P, CH, 2 * NE], F32R)
        w13_lo = sb("w13_lo", [P, CH, 2 * NE], F32R)
        w2 = sb("w2", [P, EX, HID], F32)
        bq = sb("bq", [P, CH], F32)
        bk = sb("bk", [P, CH], F32)
        bv = sb("bv", [P, HID], F32)
        bo = sb("bo", [P, HID], F32)
        ebias = sb("ebias", [P, EXPERTS], F32)
        row_i = sb("row_i", [P, 2], I32)
        par = sb("par", [P, 2], F32)
        causal = sb("causal", [P, 2 * P], BF16)
        number = sb("number", [P, EXPERTS], I32)
        numberf = sb("numberf", [P, EXPERTS], F32)

        w_in = sem("w1_in")
        w13_in = sem("w13_in")
        ones_done = sem("ones_done")
        consts = sem("consts1")
        ms_sum = sem("ms_sum")
        ms_done = sem("ms_done")
        rms_done = sem("rms_done")
        branch_done = sem("branch_done")
        x1_done = sem("x1_done")
        hi_copied = sem("hi_copied")
        split_done = sem("split_done")
        N_IN = 7
        with ExitStack() as prepare:
            wqkv = prepare.enter_context(nc.sbuf_tensor("wqkv", [P, CH, QKVR], F32))
            block = prepare.enter_context(nc.Block())

            @block.sync
            def _(sp):
                sp.dma_start(wqkv[:], wqkv_d.rearrange("(c p) n -> p c n", p=P)).then_inc(w_in, 16)
                sp.dma_start(wo[:], wo_d.rearrange("(c p) n -> p c n", p=P)).then_inc(w_in, 16)
                sp.dma_start(bq[:], bq_d).then_inc(w_in, 16)
                sp.dma_start(bk[:], bk_d).then_inc(w_in, 16)
                sp.dma_start(bv[:], bv_d).then_inc(w_in, 16)
                sp.dma_start(bo[:], bo_d).then_inc(w_in, 16)
                sp.dma_start(ebias[:], ebias_d).then_inc(w_in, 16)
                sp.dma_start(w2[:], w2_d.rearrange("e p n -> p e n")).then_inc(w13_in, 16)
                sp.wait_ge(branch_done, 4)
                sp.dma_start(acc[:].rearrange("p t n -> p (t n)")[:, 0:2 * NE], w13_d[0:P, :]).then_inc(w13_in, 16)
                sp.wait_ge(x1_done, 4)
                sp.dma_start(branch[:].rearrange("p t n -> p (t n)")[:, 0:2 * NE], w13_d[P:2 * P, :])\
                    .then_inc(w13_in, 16)

            @block.gpsimd
            def _(pool):
                pool.memset(half[:], -0.5).then_inc(consts, 1)
                pool.memset(causal[:], 0.0).then_inc(consts, 1)
                pool.iota(row_i[:], pattern=[[0, 2]], base=0, channel_multiplier=1).then_inc(consts, 1)
                pool.iota(number[:], pattern=[[1, EXPERTS]], base=0, channel_multiplier=0).then_inc(consts, 1)
                pool.wait_ge(consts, 4)
                pool.affine_select(out=causal[:].rearrange("p (i n) -> p i n", i=2),
                                   in_=causal[:].rearrange("p (i n) -> p i n", i=2), compare_op=ALU.is_ge, fill=-1e30,
                                   base=0, pattern=[[0, 2], [-1, P]], channel_multiplier=1).then_inc(consts, 1)
                pool.wait_ge(ms_done, 1)
                pool.tensor_tensor(rms[:], ms[:], half[:], ALU.pow).then_inc(rms_done, 1)
                for g in range(4):
                    s = slice(4 * g, 4 * g + 4)
                    pool.wait_ge(branch_done, g + 1)
                    pool.tensor_tensor(x[:, s, :], x[:, s, :], branch[:, s, :], ALU.add).then_inc(x1_done, 1)

            @block.vector
            def _(dve):
                dve.memset(ones[:], 1.0).then_inc(ones_done, 1)
                dve.wait_ge(ms_sum, 1)
                dve.tensor_scalar(ms[:], bank[7][:, 0:TILES], 1.0 / (HEADS0 * D0), 1e-5, ALU.mult, ALU.add)\
                    .then_inc(ms_done, 1)
                dve.wait_ge(rms_done, 1)
                for t in range(TILES):
                    last = dve.scalar_tensor_tensor(branch[:, t, :], acc[:, t, :], rms[:, t:t + 1], g16[:, t, :],
                                                    ALU.mult, ALU.mult)
                    if t % 4 == 3:
                        last.then_inc(branch_done, 1)
                dve.wait_ge(consts, 5)
                dve.tensor_scalar(row_i[:, 0:2], row_i[:, 0:2], 4, 1, ALU.logical_shift_right, ALU.bitwise_and)\
                    .then_inc(consts, 1)
                dve.wait_ge(consts, 6)
                dve.tensor_scalar(par[:, 1:2], row_i[:, 1:2], 0.25, None, ALU.mult).then_inc(consts, 1)
                dve.tensor_scalar(par[:, 0:1], row_i[:, 0:1], -0.25, 0.25, ALU.mult, ALU.add).then_inc(consts, 1)
                dve.tensor_copy(numberf[:], number[:]).then_inc(consts, 1)
                dve.wait_ge(w_in, 16 * N_IN)
                dve.wait_ge(hi_copied, 1)
                dve.tensor_tensor(wqkv_lo[:], wqkv[:], wqkv_hi[:].bitcast(F32), ALU.subtract).then_inc(split_done, 1)
                for c, src in enumerate((acc, branch)):
                    dve.wait_ge(hi_copied, 2 + c)
                    dve.tensor_tensor(w13_lo[:, c, :], src[:].rearrange("p t n -> p (t n)")[:, 0:2 * NE],
                                      w13_hi[:, c, :].bitcast(F32), ALU.subtract).then_inc(split_done, 1)

            @block.scalar
            def _(act):
                act.wait_ge(w_in, 16 * N_IN)
                act.activation(wqkv_hi[:], wqkv[:], ACT.Copy).then_inc(hi_copied, 1)
                act.wait_ge(w13_in, 48)
                for c, src in enumerate((acc, branch)):
                    act.activation(w13_hi[:, c, :], src[:].rearrange("p t n -> p (t n)")[:, 0:2 * NE], ACT.Copy)\
                        .then_inc(hi_copied, 1)

            @block.tensor
            def _(pe):
                pe.wait_ge(ones_done, 1)
                for t in range(TILES):
                    last = pe.matmul(bank[7][:, t:t + 1], ssq[:, t * P:(t + 1) * P], ones[:], start=True, stop=True)
                last.then_inc(ms_sum, 1)

        sequences(nc, ctx, bank, x, ident, identb, wqkv_hi, wqkv_lo, wo, w13_hi, w13_lo,
                  w2, bq, bk, bv, bo, ebias, par, causal, numberf, half, out_d)


def sequences(nc, ctx, bank, x, ident, identb, wqkv_hi, wqkv_lo, wo, w13_hi, w13_lo,
              w2, bq, bk, bv, bo, ebias, par, causal, numberf, half, out_d):
    def sb(name, shape, dt):
        return ctx.enter_context(nc.sbuf_tensor(name, shape, dt))

    def sem(name):
        return ctx.enter_context(nc.semaphore(name))

    NE = EX * P
    GE = EG * P
    HH = HEADS1 // 2
    tick = sb("tick", [P, 1], F32)
    stats = sb("stats1", [P, BT, 6], F32)
    mv = sb("mv1", [P, BT, 2], F32)
    var = sb("var1", [P, BT], F32)
    rstd = sb("rstd1", [P, BT], F32)
    one = sb("one", [P, 1, 1], F32)
    xn = sb("xn1", [P, BT, HID], F32)
    xh = sb("xh", [P, CH, SEQ], F32R)
    xl = sb("xl", [P, CH, SEQ], F32R)
    bqm = sb("bqm", [P, 2, CH], F32)
    qm = sb("qm", [P, 2, CH, SEQ], F32)
    kT = sb("kT", [P, CH, SEQ], F32)
    vm = sb("vm", [P, BT, HEADS1 // 2, 2, 2 * D1], F32)
    v_late = sb("v_late", [P, BT, HH, D1], F32)
    nmax = sb("nmax", [P, HEADS1, BT], F32)
    prob = sb("prob", [P, 4, 3 * P], F32)
    probT = sb("probT", [P, 4, 3 * P], F32)
    sums = sb("sums", [P, BT, HEADS1], F32)
    rinv = sb("rinv", [P, BT, HEADS1], F32)
    rsum = sb("rsum", [P, BT, HEADS1, D1], F32)
    oS = sb("oS", [P, CH * SEQ], F32)
    oT = sb("oT", [P, CH, SEQ], F32)
    s1 = sb("s1", [P, BT, HID], F32)
    en = sb("en", [P, BT, EXPERTS], F32)
    en1 = sb("en1", [P, BT, EXPERTS], F32)
    score = sb("score", [P, BT, EXPERTS], F32)
    ranked = sb("ranked", [P, BT, EXPERTS], F32)
    top = sb("top", [P, BT, 8], F32)
    topi = sb("topi", [P, BT, 8], U32)
    topf = sb("topf", [P, BT, 2], F32)
    first = sb("first", [P, BT, EXPERTS], F32)
    chosen = sb("chosen", [P, BT, EXPERTS], F32)
    share = sb("share", [P, BT, EX], F32)
    half_s = sb("half_s", [P, BT, EX], F32)
    half_s2 = sb("half_s2", [P, BT, EX], F32)
    th = sb("th1", [P, GE], F32)
    tu = sb("tu", [P, GE], F32)
    hh = sb("hh", [P, GE], F32)
    hT = sb("hT", [P, BT, EX, P], F32)
    thy = sb("thy", [P, BT * HID], F32)
    gy = sb("gy", [P, BT * HID], F32)
    prod = sb("prod", [P, BT * HID], F32)
    xo = sb("xo", [P, BT, HID], F32)

    once = sem("once")
    stats_done = sem("stats1_done")
    mv_done = sem("mv1_done")
    var_done = sem("var1_done")
    rstd_done = sem("rstd1_done")
    xn_done = sem("xn1_done")
    xT_done = sem("xT1_done")
    hi_done = sem("hi1_done")
    lo_done = sem("lo1_done")
    qk_proj = sem("qk_proj")
    v_proj = sem("v_proj")
    q_done = sem("q1_done")
    k_done = sem("k1_done")
    v_read = sem("v1_read")
    v_late_done = sem("v_late_done")
    en_done = sem("en_done")
    route = sem("route")
    scored = sem("scored1")
    max_done = sem("max_done")
    exp_done = sem("exp_done")
    turned = sem("turned")
    turn_copied = sem("turn_copied")
    pv_done = sem("pv_done")
    inverted = sem("inverted")
    rsum_done = sem("rsum_done")
    rsum_turned = sem("rsum_turned")
    oS_done = sem("oS_done")
    oT_done = sem("oT_done")
    wo_done = sem("wo_done")
    s1_done = sem("s1_done")
    w3_done = sem("w3_done")
    w1_done = sem("w1_done")
    tanh_done = sem("tanh_done")
    tu_done = sem("tu_done")
    h_done = sem("h_done")
    h_turned = sem("h_turned")
    h_copied = sem("h_copied")
    y_done = sem("y_done")
    thy_done = sem("thy_done")
    gy_done = sem("gy_done")
    prod_done = sem("prod_done")
    xo_done = sem("xo_done")
    stored = sem("stored")
    block = ctx.enter_context(nc.Block())
    ROUTE = 13

    def program(eng, prologue, body, tail):
        prologue()
        body(0, first=True)
        with eng.Fori(1, BATCHES - 1) as b:
            body(b)
        body(BATCHES - 1, last=True)
        tail(BATCHES - 1)

    def tiles_of(b):
        return x[:, 2 * b:2 * b + 2, :] if isinstance(b, int) else x[:, bass.ds(2 * b, 2), :]

    def unit(u):
        return u // (UNITS // BT), u % (UNITS // BT)

    @block.sync
    def _(sp):
        def store(b):
            sp.wait_ge(xo_done, b + 1)
            sp.dma_start(out_d.rearrange("(b t p) d -> b p t d", b=BATCHES, p=P)[b], xo[:]).then_inc(stored, 16)

        store(0)
        with sp.Fori(1, BATCHES) as b:
            store(b)
        sp.wait_ge(stored, 16 * BATCHES)

    @block.gpsimd
    def _(pool):
        def power(b):
            pool.wait_ge(var_done, b + 1)
            pool.tensor_tensor(rstd[:], var[:], half[:, 0:BT], ALU.pow).then_inc(rstd_done, 1)

        def late_values(b):
            pool.wait_ge(v_read, 2 * b + 2)
            wait(pool, pv_done, b)
            for t in range(BT):
                for m in range(2):
                    last = pool.tensor_tensor(
                        vm[:, t, HH // 2:HH, m, m * D1:(m + 1) * D1],
                        v_late[:, t].rearrange("p (q m) d -> p q m d", m=2)[:, :, m, :],
                        bv[:, HH * D1:HID].rearrange("p (q m d) -> p q m d", q=HH // 2, m=2)[:, :, m, :], ALU.add)
            last.then_inc(v_late_done, 1)

        def spread_sums(b, f):
            pool.wait_ge(inverted, 2 * b + f + 1)
            wait(pool, rsum_turned, b)
            heads = slice(f * HH, (f + 1) * HH)
            for t in range(BT):
                wide = rinv[:, t, heads].rearrange("p (h o) -> p h o", o=1).to_broadcast([P, HH, D1])
                last = pool.tensor_tensor(rsum[:, t, heads, :], wide, one[:].to_broadcast([P, HH, D1]), ALU.mult)
            last.then_inc(rsum_done, 1)

        def add(b):
            pool.wait_ge(prod_done, b + 1)
            wait(pool, stored, 16 * b)
            pool.tensor_tensor(xo[:], tiles_of(b), prod[:].rearrange("p (t n) -> p t n", t=BT), ALU.add)\
                .then_inc(xo_done, 1)

        def body(b, first=False, last=False):
            late_values(b)
            if not first:
                add(b - 1)
            if not last:
                power(b + 1)
            spread_sums(b, 0)
            spread_sums(b, 1)

        program(pool, lambda: power(0), body, add)

    @block.vector
    def _(dve):
        dve.memset(one[:], 1.0).then_inc(once, 1)
        dve.memset(vm[:], 0.0).then_inc(once, 1)
        dve.memset(share[:], 1.0).then_inc(once, 1)
        for m in range(2):
            dve.tensor_scalar(bqm[:, m, :], bq[:], par[:, m:m + 1], None, ALU.mult).then_inc(once, 1)
        dve.wait_ge(once, 5)

        def moments(b):
            xt = tiles_of(b)
            for m in range(BT):
                dve.bn_stats(stats[:, m, :], xt[:, m, :]).then_inc(stats_done, 1)
            dve.wait_ge(stats_done, BT * b + BT)
            dve.memset(tick[:], 0.0)
            for m in range(BT):
                dve.bn_aggr(mv[:, m, :], stats[:, m, :]).then_inc(mv_done, 1)
            dve.wait_ge(mv_done, BT * b + BT)
            dve.tensor_scalar(var[:], mv[:, :, 1], 1e-5, None, ALU.add).then_inc(var_done, 1)

        def centre(b):
            xt = tiles_of(b)
            dve.wait_ge(rstd_done, b + 1)
            for m in range(BT):
                dve.tensor_scalar(xn[:, m, :], xt[:, m, :], mv[:, m, 0:1], rstd[:, m:m + 1],
                                  ALU.subtract, ALU.mult).then_inc(xn_done, 1)

        def low_x(b):
            dve.wait_ge(hi_done, b + 1)
            dve.tensor_tensor(xl[:].rearrange("p c n -> p (c n)"), bank[0][:],
                              xh[:].bitcast(F32).rearrange("p c n -> p (c n)"), ALU.subtract).then_inc(lo_done, 1)

        def queries(b, c):
            dve.wait_ge(qk_proj, 2 * b + c + 1)
            for m in range(2):
                last = dve.tensor_scalar(qm[:, m, c, :], bank[7][:, 0:SEQ], par[:, m:m + 1],
                                         bqm[:, m, c:c + 1], ALU.mult, ALU.add)
            last.then_inc(q_done, 1)

        def values(b, t):
            src = bank[6 * t]
            dve.wait_ge(v_proj, 2 * b + t + 1)
            wait(dve, v_late_done, b)
            for m in range(2):
                dve.tensor_tensor(vm[:, t, 0:HH // 2, m, m * D1:(m + 1) * D1],
                                  src[:, 0:HH * D1].rearrange("p (q m d) -> p q m d", q=HH // 2, m=2)[:, :, m, :],
                                  bv[:, 0:HH * D1].rearrange("p (q m d) -> p q m d", q=HH // 2, m=2)[:, :, m, :],
                                  ALU.add)
            dve.tensor_copy(v_late[:, t].rearrange("p h d -> p (h d)"), src[:, HH * D1:HID]).then_inc(v_read, 1)

        def head_max(b, n):
            dve.wait_ge(scored, SLOTS * b + n + 1)
            s = bank[score_bank(n)]
            dve.tensor_reduce(nmax[:, n, 1:2], s[:, 0:2 * P], AX.X, ALU.max, negate=True)
            dve.tensor_reduce(nmax[:, n, 0:1], s[:, 2 * P:3 * P], AX.X, ALU.max, negate=True).then_inc(max_done, 1)

        def copy_turn(b, n):
            dve.wait_ge(turned, SLOTS * b + n + 1)
            dve.tensor_copy(probT[:, n % 4, :], bank[4][:, 0:3 * P]).then_inc(turn_copied, 1)

        def invert_sums(b, f):
            dve.wait_ge(exp_done, SLOTS * b + HH * (f + 1))
            wait(dve, rsum_done, 2 * b - 1 + f)
            heads = slice(f * HH, (f + 1) * HH)
            dve.reciprocal(rinv[:, :, heads], sums[:, :, heads]).then_inc(inverted, 1)

        def scale_heads(b):
            dve.wait_ge(rsum_turned, b + 1)
            dve.wait_ge(oS_done, b + 1)
            dve.tensor_tensor(oT[:].rearrange("p c n -> p (c n)"), bank[0][:], oS[:], ALU.mult).then_inc(oT_done, 1)

        def hidden_tanh(b, u):
            dve.wait_ge(tanh_done, UNITS * b + u + 1)
            dve.scalar_tensor_tensor(tu[:], th[:], 1.0, bank[7][:, 0:GE], ALU.add, ALU.mult).then_inc(tu_done, 1)

        def hidden(b, u):
            t, g = unit(u)
            dve.wait_ge(tu_done, UNITS * b + u + 1)
            dve.wait_ge(w3_done, UNITS * b + u + 1)
            for e in range(EG):
                c = slice(e * P, (e + 1) * P)
                last = dve.scalar_tensor_tensor(hh[:, c], tu[:, c], half_s2[:, t, g * EG + e:g * EG + e + 1],
                                                bank[6][:, c], ALU.mult, ALU.mult)
            last.then_inc(h_done, 1)

        def gate(b):
            dve.wait_ge(thy_done, b + 1)
            dve.scalar_tensor_tensor(gy[:], thy[:], 1.0, bank[6][:], ALU.add, ALU.mult).then_inc(gy_done, 1)

        def finish(b):
            dve.wait_ge(wo_done, b + 1)
            for t in range(BT):
                last = dve.tensor_tensor(s1[:, t], bank[0][:, t * HID:(t + 1) * HID], bo[:], ALU.add)
            last.then_inc(s1_done, 1)
            dve.wait_ge(s1_done, b + 1)
            dve.wait_ge(gy_done, b + 1)
            wait(dve, xo_done, b)
            dve.scalar_tensor_tensor(prod[:], s1[:].rearrange("p t n -> p (t n)"), 0.5, gy[:],
                                     ALU.mult, ALU.mult).then_inc(prod_done, 1)

        def router_scores(b):
            r0 = ROUTE * b

            def link(n):
                dve.wait_ge(route, r0 + n)

            dve.wait_ge(en_done, 2 * b + 2)
            dve.tensor_scalar(en1[:], en[:], 1.0, None, ALU.add).then_inc(route, 1)
            link(1)
            dve.reciprocal(score[:], en1[:]).then_inc(route, 1)
            link(2)
            for t in range(BT):
                dve.tensor_tensor(ranked[:, t], score[:, t], ebias[:], ALU.add).then_inc(route, 1)
            link(4)
            dve.memset(tick[:], 0.0)
            for t in range(BT):
                dve.max(top[:, t], ranked[:, t]).then_inc(route, 1)
            link(6)
            dve.memset(tick[:], 0.0)
            for t in range(BT):
                dve.max_index(topi[:, t], top[:, t], ranked[:, t]).then_inc(route, 1)
            link(8)
            dve.tensor_copy(topf[:], topi[:, :, 0:2]).then_inc(route, 1)
            link(9)
            for t in range(BT):
                last = dve.tensor_scalar(first[:, t], numberf[:], topf[:, t, 0:1], None, ALU.is_equal)
            last.then_inc(route, 1)
            link(10)
            for t in range(BT):
                last = dve.scalar_tensor_tensor(chosen[:, t], numberf[:], topf[:, t, 1:2], first[:, t],
                                                ALU.is_equal, ALU.add)
            last.then_inc(route, 1)
            link(11)
            dve.tensor_tensor(share[:, :, 0:EXPERTS], chosen[:], score[:], ALU.mult).then_inc(route, 1)
            link(12)
            dve.tensor_scalar(half_s[:], share[:], 0.5, None, ALU.mult)
            dve.scalar_tensor_tensor(half_s2[:], share[:], 0.5, share[:], ALU.mult, ALU.mult).then_inc(route, 1)

        def prologue():
            moments(0)
            centre(0)
            low_x(0)
            queries(0, 0)
            values(0, 0)
            queries(0, 1)
            values(0, 1)
            head_max(0, 0)
            head_max(0, 1)
            router_scores(0)

        def body(b, first=False, last=False):
            for n in range(SLOTS):
                if n % 2 == 1:
                    copy_turn(b, n)
                if n == 11 and not last:
                    low_x(b + 1)
                if n + 2 < SLOTS:
                    head_max(b, n + 2)
                elif not last:
                    head_max(b + 1, n + 2 - SLOTS)
                if n % 2 == 0:
                    copy_turn(b, n)
                if n == 0 and not first:
                    scale_heads(b - 1)
                if n == 4 and not first:
                    finish(b - 1)
                if n == 10:
                    invert_sums(b, 0)
                if n == 14:
                    invert_sums(b, 1)
                if n == 6 and not last:
                    moments(b + 1)
                if n == 8 and not last:
                    centre(b + 1)
                if n % 2 == 0 and n // 2 < UNITS:
                    hidden_tanh(b, n // 2)
                    hidden(b, n // 2)
                if not last:
                    if n == 12:
                        queries(b + 1, 0)
                    if n == 13:
                        values(b + 1, 0)
                        values(b + 1, 1)
                        queries(b + 1, 1)
                    if n == 14:
                        router_scores(b + 1)
            gate(b)

        def tail(b):
            scale_heads(b)
            finish(b)

        program(dve, prologue, body, tail)

    @block.scalar
    def _(act):
        def high_x(b):
            act.wait_ge(xT_done, b + 1)
            act.activation(xh[:].rearrange("p c n -> p (c n)"), bank[0][:], ACT.Copy).then_inc(hi_done, 1)

        def keys(b, c):
            act.wait_ge(q_done, 2 * b + c + 1)
            act.activation(kT[:, c, :], bank[7][:, SEQ:2 * SEQ], ACT.Identity, bias=bk[:, c:c + 1])\
                .then_inc(k_done, 1)

        def router_exp(b, t):
            act.wait_ge(v_read, 2 * b + t + 1)
            act.activation(en[:, t, :], bank[6 * t][:, HID:HID + EXPERTS], ACT.Exp, scale=-1.0).then_inc(en_done, 1)

        def exps(b, n):
            act.wait_ge(max_done, SLOTS * b + n + 1)
            wait(act, turned, SLOTS * b + n - 3)
            if n in (0, HH):
                wait(act, inverted, 2 * b - 1 + n // HH)
            s, h = bank[score_bank(n)], ORDER[n]
            act.activation(prob[:, n % 4, 0:2 * P], s[:, 0:2 * P], ACT.Exp, bias=nmax[:, n, 1:2],
                           accum_out=sums[:, 1, h:h + 1])
            act.activation(prob[:, n % 4, 2 * P:3 * P], s[:, 2 * P:3 * P], ACT.Exp, bias=nmax[:, n, 0:1],
                           accum_out=sums[:, 0, h:h + 1]).then_inc(exp_done, 1)

        def tanhs(b, u):
            t, g = unit(u)
            act.wait_ge(w1_done, UNITS * b + u + 1)
            act.wait_ge(route, ROUTE * b + ROUTE)
            wait(act, tu_done, UNITS * b + u)
            for e in range(EG):
                c = slice(e * P, (e + 1) * P)
                last = act.activation(th[:, c], bank[7][:, c], ACT.Tanh,
                                      scale=half_s[:, t, g * EG + e:g * EG + e + 1])
            last.then_inc(tanh_done, 1)

        def copy_hidden(b, u):
            t, g = unit(u)
            act.wait_ge(h_turned, UNITS * b + u + 1)
            act.activation(hT[:, t, g * EG:(g + 1) * EG, :].rearrange("p e n -> p (e n)"), bank[6][:, 0:GE],
                           ACT.Copy).then_inc(h_copied, 1)

        def copy_heads(b):
            act.wait_ge(pv_done, b + 1)
            wait(act, oT_done, b)
            act.activation(oS[:], bank[5][:], ACT.Copy).then_inc(oS_done, 1)

        def gate(b):
            act.wait_ge(y_done, b + 1)
            act.activation(thy[:], bank[6][:], ACT.Tanh, scale=0.5).then_inc(thy_done, 1)

        def prologue():
            high_x(0)
            keys(0, 0)
            router_exp(0, 0)
            keys(0, 1)
            router_exp(0, 1)
            exps(0, 0)
            exps(0, 1)

        def body(b, first=False, last=False):
            for n in range(SLOTS):
                if n == 0 and not first:
                    copy_heads(b - 1)
                if n == 11 and not last:
                    high_x(b + 1)
                if n % 2 == 1 and n // 2 < UNITS:
                    copy_hidden(b, n // 2)
                if n + 2 < SLOTS:
                    exps(b, n + 2)
                elif not last:
                    exps(b + 1, n + 2 - SLOTS)
                if n % 2 == 0 and n // 2 < UNITS:
                    tanhs(b, n // 2)
                if not last:
                    if n == 12:
                        keys(b + 1, 0)
                    if n == 13:
                        router_exp(b + 1, 0)
                        router_exp(b + 1, 1)
                        keys(b + 1, 1)
            gate(b)

        program(act, prologue, body, copy_heads)

    @block.tensor
    def _(pe):
        pe.wait_ge(once, 5)

        def three(out, a_hi, a_lo, b_hi, b_lo, first, last):
            pe.matmul(out, a_hi, b_hi, start=first, stop=False)
            pe.matmul(out, a_hi, b_lo, start=False, stop=False)
            return pe.matmul(out, a_lo, b_hi, start=False, stop=last)

        def turn_x(b):
            pe.wait_ge(xn_done, BT * b + BT)
            wait(pe, s1_done, b - 1)
            for m in range(BT):
                for c in range(CH):
                    last = pe.transpose(bank[0][:, c * SEQ + m * P:c * SEQ + (m + 1) * P],
                                        xn[:, m, c * P:(c + 1) * P], ident[:])
            last.then_inc(xT_done, 1)

        def project_qk(b, f):
            if f == 0:
                pe.wait_ge(lo_done, b + 1)
                wait(pe, h_done, UNITS * b)
            else:
                pe.wait_ge(q_done, 2 * b + 1)
                pe.wait_ge(k_done, 2 * b + 1)
            for i in range(2):
                w = slice(i * HID + f * P, i * HID + (f + 1) * P)
                for c in range(CH):
                    last = three(bank[7][:, i * SEQ:(i + 1) * SEQ], wqkv_hi[:, c, w], wqkv_lo[:, c, w],
                                 xh[:, c, :], xl[:, c, :], c == 0, c == CH - 1)
            last.then_inc(qk_proj, 1)

        def project_v(b, t):
            if t == 0:
                pe.wait_ge(lo_done, b + 1)
            else:
                wait(pe, h_copied, UNITS * b)
            for c in range(CH):
                s = slice(t * P, (t + 1) * P)
                last = three(bank[6 * t][:, 0:HID + EXPERTS], xh[:, c, s], xl[:, c, s],
                             wqkv_hi[:, c, 2 * HID:QKVR], wqkv_lo[:, c, 2 * HID:QKVR], c == 0, c == CH - 1)
            last.then_inc(v_proj, 1)

        def scores(b, n):
            if n % HH == 0:
                pe.wait_ge(q_done, 2 * b + n // HH + 1)
                pe.wait_ge(k_done, 2 * b + n // HH + 1)
            wait(pe, exp_done, SLOTS * b + score_bank_before(n) + 1)
            h = ORDER[n]
            c, r = h // HH, slice(32 * (h % HH // 2), 32 * (h % HH // 2) + 32)
            out = bank[score_bank(n)]
            pe.matmul(out[:, 0:2 * P], qm[r, h % 2, c, P:SEQ], kT[r, c, :], start=True, stop=False)
            pe.matmul(out[:, 2 * P:3 * P], qm[r, h % 2, c, 0:P], kT[r, c, 0:P], start=False, stop=False)
            pe.matmul(out[:, P:3 * P], identb[:], causal[:], start=False, stop=True).then_inc(scored, 1)

        def turn(b, n):
            pe.wait_ge(exp_done, SLOTS * b + n + 1)
            wait(pe, turn_copied, SLOTS * b + n)
            for to, block in ((0, 2), (1, 0), (2, 1)):
                last = pe.transpose(bank[4][:, to * P:(to + 1) * P], prob[:, n % 4, block * P:(block + 1) * P],
                                    ident[:])
            last.then_inc(turned, 1)

        def product(b, n):
            pe.wait_ge(turn_copied, SLOTS * b + n + 2)
            if n == 0:
                pe.wait_ge(v_read, 2 * b + 2)
                wait(pe, oS_done, b)
            if n == HH:
                pe.wait_ge(v_late_done, b + 1)
            for key in range(2):
                for i in range(2):
                    h = ORDER[n + i]
                    c, r = h // HH, slice(32 * (h % HH // 2), 32 * (h % HH // 2) + 32)
                    last = pe.matmul(bank[5][r, c * SEQ + key * P:(c + 1) * SEQ], vm[:, key, h // 2, h % 2, :],
                                     probT[:, (n + i) % 4, 2 * key * P:(2 + key) * P],
                                     start=(h % 2 == 0 and key == 0), stop=(h % 2 == 1 and key == 1))
            if n == SLOTS - 2:
                last.then_inc(pv_done, 1)

        def up(b, u, i):
            t, g = unit(u)
            if i == 0:
                if u:
                    pe.wait_ge(h_done, UNITS * b + u)
                else:
                    pe.wait_ge(q_done, 2 * b + 2)
                    pe.wait_ge(k_done, 2 * b + 2)
            else:
                if u:
                    pe.wait_ge(h_copied, UNITS * b + u)
                else:
                    pe.wait_ge(v_read, 2 * b + 2)
                    pe.wait_ge(en_done, 2 * b + 2)
                    wait(pe, gy_done, b)
            w = slice(i * NE + g * GE, i * NE + (g + 1) * GE)
            for c in range(CH):
                s = slice(t * P, (t + 1) * P)
                last = three(bank[7 - i][:, 0:GE], xh[:, c, s], xl[:, c, s], w13_hi[:, c, w], w13_lo[:, c, w],
                             c == 0, c == CH - 1)
            last.then_inc(w3_done if i else w1_done, 1)

        def turn_hidden(b, u):
            pe.wait_ge(h_done, UNITS * b + u + 1)
            for e in range(EG):
                last = pe.transpose(bank[6][:, e * P:(e + 1) * P], hh[:, e * P:(e + 1) * P], ident[:])
            last.then_inc(h_turned, 1)

        def experts_sum(b, t, last):
            pe.wait_ge(h_copied, UNITS * b + UNITS)
            if t == 0 and not last:
                pe.wait_ge(v_read, 2 * b + 4)
                pe.wait_ge(en_done, 2 * b + 4)
            for e in range(EX):
                last = pe.matmul(bank[6][:, t * HID:(t + 1) * HID], hT[:, t, e, :], w2[:, e, :],
                                 start=(e == 0), stop=(e == EX - 1))
            if t == BT - 1:
                last.then_inc(y_done, 1)

        def turn_sums(b):
            pe.wait_ge(rsum_done, 2 * b + 2)
            if isinstance(b, int) and b == BATCHES - 1:
                pe.wait_ge(s1_done, b)
            else:
                pe.wait_ge(v_read, 2 * b + 3)
                pe.wait_ge(en_done, 2 * b + 3)
            for m in range(BT):
                for c in range(CH):
                    last = pe.transpose(bank[0][:, c * SEQ + m * P:c * SEQ + (m + 1) * P],
                                        rsum[:, m, c * HH:(c + 1) * HH, :].rearrange("p h d -> p (h d)"), ident[:])
            last.then_inc(rsum_turned, 1)

        def project_out(b):
            pe.wait_ge(oT_done, b + 1)
            for t in range(BT):
                for c in range(CH):
                    last = pe.matmul(bank[0][:, t * HID:(t + 1) * HID], oT[:, c, t * P:(t + 1) * P], wo[:, c, :],
                                     start=(c == 0), stop=(c == CH - 1))
            last.then_inc(wo_done, 1)

        def prologue():
            turn_x(0)
            project_qk(0, 0)
            project_v(0, 0)
            project_qk(0, 1)
            project_v(0, 1)
            scores(0, 0)
            scores(0, 1)

        def body(b, first=False, last=False):
            for n in range(SLOTS):
                if n + 2 < SLOTS:
                    scores(b, n + 2)
                elif not last:
                    scores(b + 1, n + 2 - SLOTS)
                if n % 2 == 0 and 1 <= n // 2 <= UNITS:
                    turn_hidden(b, n // 2 - 1)
                if n % 2 == 0 and n // 2 < UNITS:
                    up(b, n // 2, 0)
                turn(b, n)
                if n % 2 == 0 and n // 2 < UNITS:
                    up(b, n // 2, 1)
                if n == 10 and not last:
                    turn_x(b + 1)
                if n % 2 == 1 and n > 1:
                    product(b, n - 3)
                if n == 0 and not first:
                    turn_sums(b - 1)
                if n == 1 and not first:
                    project_out(b - 1)
                if n in (14, 15):
                    experts_sum(b, n - 14, last)
                if not last:
                    if n == 12:
                        project_qk(b + 1, 0)
                        project_v(b + 1, 0)
                    if n == 13:
                        project_v(b + 1, 1)
                        project_qk(b + 1, 1)
            product(b, SLOTS - 2)

        def tail(b):
            turn_sums(b)
            project_out(b)

        program(pe, prologue, body, tail)


def kernel(**inputs):
    import numpy as np
    import concourse.bacc as bacc
    from concourse.bass_utils import run_bass_kernel_spmd

    a = {n: np.asarray(v) for n, v in inputs.items()}

    def rows(name):
        v = a[name].reshape(1, -1)
        return np.broadcast_to(v, (P, v.shape[1]))

    heads = a["L0_attn_qkv_w"].reshape(PAIRS, 2, 3, D0, HID).transpose(0, 2, 1, 3, 4).reshape(PAIRS, 3 * P, HID)
    gates = a["L0_attn_gate_w"].reshape(PAIRS, P, HID)
    w0 = np.concatenate([heads, gates], axis=1).transpose(0, 2, 1).reshape(PAIRS, CH, P, COLS)
    w0 = np.concatenate([w0.transpose(0, 2, 1, 3).reshape(PAIRS, P, CH * COLS),
                         a["L0_attn_out_w"].T.reshape(PAIRS, P, HID),
                         a["L0_attn_norm_w"].reshape(PAIRS, P, 1)], axis=2)
    e1 = np.concatenate([a["L1_ffn_w1"].reshape(-1, HID), a["L1_ffn_sw1"]], axis=0)
    e3 = np.concatenate([a["L1_ffn_w3"].reshape(-1, HID), a["L1_ffn_sw3"]], axis=0)
    arrays = {
        "x": a["L0_attn_hidden_states"].reshape(TOK, HID),
        "w0": w0,
        "ffn_w": np.ascontiguousarray(a["L0_ffn_weight"].T).view(np.int32),
        "ffn_sc": rows("L0_ffn_w_scale"),
        "ffn_b": rows("L0_ffn_bias"),
        "wqkv1": np.concatenate([a["L1_attn_Wq"].T, a["L1_attn_Wk"].T, a["L1_attn_Wv"].T,
                                 a["L1_ffn_gate_w"].T], axis=1),
        "wo1": a["L1_attn_Wo"].T,
        "bq": a["L1_attn_bq"].reshape(CH, P).T,
        "bk": a["L1_attn_bk"].reshape(CH, P).T,
        "bv": rows("L1_attn_bv"),
        "bo": rows("L1_attn_bo"),
        "ebias": rows("L1_ffn_expert_bias"),
        "w13": np.concatenate([e1.T, e3.T], axis=1),
        "w2": np.concatenate([a["L1_ffn_w2"].transpose(0, 2, 1), a["L1_ffn_sw2"].T[None]], axis=0),
    }
    nc = bacc.Bacc("TRN2", target_bir_lowering=False, num_devices=1)
    given, args = {}, []
    for name, v in arrays.items():
        v = np.ascontiguousarray(v)
        given[f"in_{name}"] = v
        args.append(nc.dram_tensor(f"in_{name}", v.shape, mybir.dt.from_np(v.dtype), kind="ExternalInput").ap())
    args.append(nc.dram_tensor("out_0", (TOK, HID), F32, kind="ExternalOutput").ap())
    build(nc, *args)
    r = run_bass_kernel_spmd(nc, [given], core_ids=[0])
    return r.results[0]["out_0"].reshape(BATCHES, SEQ, HID)
```

```python
from contextlib import ExitStack

import concourse.bass as bass
from concourse import mybir

ALU = mybir.AluOpType
ACT = mybir.ActivationFunctionType
AX = mybir.AxisListType
F32 = mybir.dt.float32
F32R = mybir.dt.float32r
F16 = mybir.dt.float16
BF16 = mybir.dt.bfloat16
I8 = mybir.dt.int8
I32 = mybir.dt.int32
U32 = mybir.dt.uint32

P = 128
BATCHES, SEQ, HID = 8, 256, 256
TOK = BATCHES * SEQ
TILES = TOK // P
CH = HID // P

HEADS0, D0 = 32, 64
PAIRS = HEADS0 // 2
GROUP = 512
GROUPS = TOK // GROUP
GT = GROUP // P
COLS = 4 * P
WROW = CH * COLS + HID + 1
STEPS = PAIRS * GROUPS
BODY = 2 * GROUPS
ROUND = 12582912.0
EARLY = BATCHES // 2

HEADS1, D1 = 16, 16
EXPERTS = 8
EX = EXPERTS + 1
EG = 3
BT = SEQ // P
UNITS = BT * (EX // EG)
QKVR = 3 * HID + EXPERTS


def wait(eng, sem, value):
    if isinstance(value, int) and value <= 0:
        return
    eng.wait_ge(sem, value)


def slopes():
    base = 1.0 / 2.0 ** (8.0 / HEADS0)
    factor = 1.0 - 0 / (32 - 1 + 1e-05) + 1e-05
    return [base ** (h + 1.0) * factor for h in range(HEADS0)]


def build(nc, x_d, w0_d, ffn_w_d, ffn_sc_d, ffn_b_d, wqkv1_d, wo1_d, bq_d, bk_d, bv_d, bo_d,
          ebias_d, w13_d, w2_d, out_d):
    with ExitStack() as keep:
        def ksb(name, shape, dt):
            return keep.enter_context(nc.sbuf_tensor(name, shape, dt))

        bank = [keep.enter_context(nc.psum_tensor(f"bank{i}", [P, 512], F32)) for i in range(8)]
        x = ksb("x", [P, TILES, HID], F32)
        acc = ksb("acc", [P, TILES, HID], F32)
        g16 = ksb("g16", [P, TILES, HID], F16)
        ident = ksb("ident", [P, P], F32)
        identb = ksb("identb", [P, P], BF16)
        ones = ksb("ones", [P, 1], F32)
        xn1 = ksb("xn1", [P, BT, HID], F32)
        wqkv = ksb("wqkv", [P, CH, QKVR], F32)
        wqkv_in = keep.enter_context(nc.semaphore("wqkv_in"))
        with ExitStack() as layer0:
            def sb(name, shape, dt):
                return layer0.enter_context(nc.sbuf_tensor(name, shape, dt))

            ssq = sb("ssq", [P, TOK], F32)
            xn_hi = sb("xn_hi", [P, CH, TOK], F32R)
            xn_lo = sb("xn_lo", [P, CH, TOK], F32R)
            decay = sb("decay", [P, HEADS0, 2 * P], F32)
            mv = sb("mv", [P, TILES, 2], F32)
            rstd = sb("rstd", [P, TILES], F32)
            wb = sb("wb", [P, CH, HID], BF16)
            w_sc = sb("w_sc", [P, HID], F32)
            bias = sb("bias", [P, HID], F32)
            stage = [sb(f"w_stage{i}", [P, WROW], F32) for i in range(2)]
            w0_in = [layer0.enter_context(nc.semaphore(f"w0_in{i}")) for i in range(2)]
            w_hi = sb("w_hi", [P, 2, CH, COLS], F32R)
            w_lo = sb("w_lo", [P, 2, CH, COLS], F32R)
            half = sb("half", [P, TILES], F32)
            x_last_in = layer0.enter_context(nc.semaphore("x_last_in"))
            w_hi_done = layer0.enter_context(nc.semaphore("w_hi_done"))
            w_split = layer0.enter_context(nc.semaphore("w_split"))
            v_split = layer0.enter_context(nc.semaphore("v_split"))
            projected = layer0.enter_context(nc.semaphore("projected"))
            normalise(nc, bank, x, ident, identb, ones, xn_hi, xn_lo, decay, ssq, acc, mv, rstd, wb, w_sc, bias,
                      stage, w0_in, w_hi, w_lo, w_hi_done, w_split, v_split, projected, half, x_last_in, wqkv, wqkv_in,
                      x_d, w0_d, ffn_w_d, ffn_sc_d, ffn_b_d, wqkv1_d)
            linear_attention(nc, bank, ident, identb, ones, xn1, xn_hi, xn_lo, decay, acc, ssq, x, g16, mv, rstd,
                             wb, w_sc, bias, stage, w0_in, w_hi, w_lo, w_hi_done, w_split, v_split, projected, half,
                             x_last_in, w0_d)
        layer_one(nc, bank, x, xn1, acc, g16, ident, identb, ones, wqkv, wqkv_in, wo1_d, bq_d, bk_d, bv_d, bo_d,
                  ebias_d, w13_d, w2_d, out_d)


def normalise(nc, bank, x, ident, identb, ones, xn_hi, xn_lo, decay, ssq, acc, mv, rstd, wb, w_sc, bias,
              stage, w0_in, w_hi, w_lo, w_hi_done, w_split, v_split, projected, half, x_last_in, wqkv, wqkv_in,
              x_d, w0_d, ffn_w_d, ffn_sc_d, ffn_b_d, wqkv1_d):
    with ExitStack() as ctx:
        def sb(name, shape, dt):
            return ctx.enter_context(nc.sbuf_tensor(name, shape, dt))

        def sem(name):
            return ctx.enter_context(nc.semaphore(name))

        xn = sb("xn", [P, 8, HID], F32)
        stats = sb("stats", [P, TILES, 6], F32)
        var = sb("var", [P, TILES], F32)
        w8 = sb("w8", [P, CH, HID // 4], I32)
        dist_i = sb("dist_i", [P, 2 * P], I32)
        dist = sb("dist", [P, 2 * P], F32)
        warm = sb("warm0", [P, 1], F32)

        x_in = [sem(f"x_in{g}") for g in range(TILES // 4 - 1)] + [x_last_in]
        w_in = sem("ffn_w_in")
        consts = sem("consts")
        idents = sem("idents")
        dist_ready = sem("dist_ready")
        decay_exp = sem("decay_exp")
        decay_ready = sem("decay_ready")
        stats_done = sem("stats_done")
        mv_done = sem("mv_done")
        var_done = sem("var_done")
        rstd_done = sem("rstd_done")
        xn_done = sem("xn_done")
        wb_done = sem("wb_done")
        xT_done = sem("xT_done")
        hi_done = sem("hi_done")
        lo_done = sem("lo_done")
        block = ctx.enter_context(nc.Block())
        NG = TILES // 4
        NB = EARLY
        MORE = 4

        @block.sync
        def _(sp):
            xv = x_d.rearrange("(g t p) d -> g p t d", g=NG, p=P)
            for g in range(NG):
                sp.dma_start(x[:, 4 * g:4 * g + 4, :], xv[g]).then_inc(x_in[g], 16)
                if g >= 1 and g < 3:
                    sp.dma_start(stage[g - 1][:], w0_d[g - 1]).then_inc(w0_in[g - 1], 16)
            sp.dma_start(w8[:], ffn_w_d.rearrange("(c p) n -> p c n", p=P)).then_inc(w_in, 16)
            sp.dma_start(w_sc[:], ffn_sc_d).then_inc(w_in, 16)
            sp.dma_start(bias[:], ffn_b_d).then_inc(w_in, 16)
            sp.dma_start(wqkv[:], wqkv1_d.rearrange("(c p) n -> p c n", p=P)).then_inc(wqkv_in, 16)

        @block.gpsimd
        def _(pool):
            pool.iota(dist_i[:], pattern=[[1, 2 * P]], base=0, channel_multiplier=-1).then_inc(dist_ready, 1)
            pool.wait_ge(dist_ready, 1)
            pool.tensor_scalar(dist[:], dist_i[:], 0.0, 1.0, ALU.max, ALU.mult).then_inc(dist_ready, 1)
            pool.memset(half[:], -0.5).then_inc(consts, 1)
            pool.memset(ident[:], 0.0).then_inc(consts, 1)
            pool.memset(identb[:], 0.0).then_inc(consts, 1)
            pool.memset(ones[:], 1.0).then_inc(consts, 1)
            pool.wait_ge(consts, 4)
            pool.affine_select(out=ident[:], in_=ident[:], compare_op=ALU.not_equal, fill=1.0,
                               base=0, pattern=[[-1, P]], channel_multiplier=1).then_inc(idents, 1)
            pool.affine_select(out=identb[:], in_=identb[:], compare_op=ALU.not_equal, fill=1.0,
                               base=0, pattern=[[-1, P]], channel_multiplier=1).then_inc(idents, 1)
            pool.memset(ssq[:], 0.0).then_inc(decay_ready, 1)
            for g in range(NG - 1):
                pool.wait_ge(var_done, g + 1)
                s = slice(4 * g, 4 * g + 4)
                pool.tensor_tensor(rstd[:, s], var[:, s], half[:, s], ALU.pow).then_inc(rstd_done, 1)
                if g < 2:
                    pool.memset(acc[:, s, :], 0.0).then_inc(decay_ready, 1)
                    pool.wait_ge(decay_exp, (g + 1) * HEADS0 // NG)
                    heads = slice(g * HEADS0 // NG, (g + 1) * HEADS0 // NG)
                    pool.affine_select(out=decay[:, heads, 0:P], in_=decay[:, heads, 0:P], compare_op=ALU.is_ge,
                                       fill=0.0, base=0, pattern=[[0, HEADS0 // NG], [1, P]],
                                       channel_multiplier=-1).then_inc(decay_ready, 1)
                if g == 1:
                    pool.wait_ge(w_hi_done, 1)
                    pool.tensor_tensor(w_lo[:, 0], stage[0][:, 0:CH * COLS].rearrange("p (c n) -> p c n", c=CH),
                                       w_hi[:, 0].bitcast(F32), ALU.subtract).then_inc(w_split, 1)
            pool.wait_ge(w_hi_done, 2)
            wide = stage[1][:, 0:CH * COLS].rearrange("p (c n) -> p c n", c=CH)
            pool.tensor_tensor(w_lo[:, 1, :, 2 * P:3 * P], wide[:, :, 2 * P:3 * P],
                               w_hi[:, 1, :, 2 * P:3 * P].bitcast(F32), ALU.subtract).then_inc(v_split, 1)
            pool.tensor_tensor(w_lo[:, 1, :, 0:2 * P], wide[:, :, 0:2 * P],
                               w_hi[:, 1, :, 0:2 * P].bitcast(F32), ALU.subtract)
            pool.tensor_tensor(w_lo[:, 1, :, 3 * P:4 * P], wide[:, :, 3 * P:4 * P],
                               w_hi[:, 1, :, 3 * P:4 * P].bitcast(F32), ALU.subtract).then_inc(w_split, 1)

        @block.vector
        def _(dve):
            def moments(g):
                dve.wait_ge(x_in[g], 16)
                for t in range(4 * g, 4 * g + 4):
                    dve.bn_stats(stats[:, t, :], x[:, t, :]).then_inc(stats_done, 1)
                for t in range(4 * g, 4 * g + 4):
                    dve.wait_ge(stats_done, t + 1)
                    dve.bn_aggr(mv[:, t, :], stats[:, t, :]).then_inc(mv_done, 1)
                dve.wait_ge(mv_done, 4 * g + 4)
                s = slice(4 * g, 4 * g + 4)
                dve.tensor_scalar(var[:, s], mv[:, s, 1], 1e-5, None, ALU.add).then_inc(var_done, 1)

            def centre(g):
                dve.wait_ge(rstd_done, g + 1)
                for t in range(4 * g, 4 * g + 4):
                    dve.tensor_scalar(xn[:, t, :], x[:, t, :], mv[:, t, 0:1], rstd[:, t:t + 1],
                                      ALU.subtract, ALU.mult).then_inc(xn_done, 1)

            def low(g):
                for b in range(2 * g, 2 * g + 2):
                    dve.wait_ge(hi_done, b + 1)
                    c = slice(b * SEQ, (b + 1) * SEQ)
                    dve.tensor_tensor(xn_lo[:, :, c], bank[b % 4][:].rearrange("p (c n) -> p c n", c=CH),
                                      xn_hi[:, :, c].bitcast(F32), ALU.subtract).then_inc(lo_done, 1)

            moments(0)
            moments(1)
            centre(0)
            centre(1)
            low(0)
            moments(2)
            low(1)
            dve.wait_ge(w_in, 48)
            dve.tensor_copy(wb[:], w8[:].bitcast(I8)).then_inc(wb_done, 1)

        @block.scalar
        def _(act):
            act.wait_ge(dist_ready, 2)
            for b in range(NB):
                ahead = HEADS0 - MORE * (NB - 1)
                for h in range(ahead + MORE * (b - 1) if b else 0, min(ahead + MORE * b, HEADS0)):
                    act.activation(decay[:, h, :], dist[:], ACT.Exp, scale=-float(slopes()[h]))\
                        .then_inc(decay_exp, 1)
                act.wait_ge(xT_done, b + 1)
                act.activation(xn_hi[:, :, b * SEQ:(b + 1) * SEQ],
                               bank[b % 4][:].rearrange("p (c n) -> p c n", c=CH), ACT.Copy).then_inc(hi_done, 1)
                if b in (1, 2):
                    act.wait_ge(w0_in[b - 1], 16)
                    act.activation(w_hi[:, b - 1], stage[b - 1][:, 0:CH * COLS].rearrange("p (c n) -> p c n", c=CH),
                                   ACT.Copy).then_inc(w_hi_done, 1)
            act.wait_ge(idents, 2)
            act.activation(warm[:], ident[:, 0:1], ACT.Silu)

        @block.tensor
        def _(pe):
            pe.wait_ge(idents, 2)
            for b in range(NB):
                pe.wait_ge(xn_done, 2 * b + 2)
                for m in range(2):
                    for c in range(CH):
                        last = pe.transpose(bank[b % 4][:, c * SEQ + m * P:c * SEQ + (m + 1) * P],
                                            xn[:, 2 * b + m, c * P:(c + 1) * P], ident[:])
                last.then_inc(xT_done, 1)
            pe.wait_ge(lo_done, GROUP // SEQ)
            pe.wait_ge(w_split, 1)
            for what in range(2):
                for c in range(CH):
                    cols = slice(what * P, (what + 1) * P)
                    for a, b in ((w_hi, xn_hi), (w_hi, xn_lo), (w_lo, xn_hi)):
                        last = pe.matmul(bank[what][:], a[:, 0, c, cols], b[:, c, 0:GROUP],
                                         start=(c == 0 and a is w_hi and b is xn_hi),
                                         stop=(c == CH - 1 and a is w_lo))
                last.then_inc(projected, 1)


def linear_attention(nc, bank, ident, identb, ones, xn1, xn_hi, xn_lo, decay, acc, ssq, x, g16, mv, rstd,
                     wb, w_sc, bias, stage, w_in, w_hi, w_lo, w_hi_done, w_split, v_split, projected, half,
                     x_last_in, w0_d):
    with ExitStack() as ctx:
        def sb(name, shape, dt):
            return ctx.enter_context(nc.sbuf_tensor(name, shape, dt))

        def sem(name):
            return ctx.enter_context(nc.semaphore(name))

        wo = [sb(f"wo{i}", [P, HID], F32) for i in range(2)]
        wo_hi = [sb(f"wo_hi{i}", [P, HID], F32R) for i in range(2)]
        wo_lo = [sb(f"wo_lo{i}", [P, HID], F32R) for i in range(2)]
        q = sb("q", [P, GROUP], F32)
        k = sb("k", [P, GROUP], F32)
        q_parts = [sb(f"q_parts{h}", [P, GROUP], F32R) for h in range(2)]
        k_twice = [sb(f"k_twice{h}", [P, GROUP], F32R) for h in range(2)]
        k_lo = sb("k_lo", [P, GROUP], F32R)
        v = sb("v", [P, 2, GT, 2, P], F32)
        th = sb("th", [P, GROUP], F32)
        aw = sb("aw", [P, 4, 3 * P], F32)
        gated = sb("gated", [P, GROUP], F32)
        gated_hi = sb("gated_hi", [P, 2, GROUP], F32R)
        gated_lo = sb("gated_lo", [P, 2, GROUP], F32R)
        sq = sb("sq", [P, GROUP], F32)
        xn = sb("xn_late", [P, GT, HID], F32)
        stats = sb("stats_late", [P, GT, 6], F32)
        var = sb("var_late", [P, GT], F32)
        ms_first = sb("ms_first", [P, BT], F32)
        rms_first = sb("rms_first", [P, BT], F32)
        mean_now = sb("mean_now", [P, BT], F32)
        rstd_now = sb("rstd_now", [P, BT], F32)
        xq = sb("xq", [P, BT, HID], F32)
        absmax = sb("absmax", [P, BT], F32)
        in_sc = sb("in_sc", [P, BT], F32)
        in_inv = sb("in_inv", [P, BT], F32)
        q16 = sb("q16", [P, BT, HID], BF16)
        qT = sb("qT", [P, CH, SEQ], BF16)
        z = xq
        z16 = sb("z16", [P, BT, HID], F16)
        thz = z
        sg16 = xn[:, 2, :].bitcast(F16).rearrange("p (t n) -> p t n", t=BT)

        wo_ready = sem("wo_ready")
        activated = sem("activated")
        moment_step = sem("moment_step")
        rstd_late = sem("rstd_late")
        sums_cleared = sem("sums_cleared")
        tables_masked = sem("tables_masked")
        xn_done = sem("xn_late_done")
        xT_done = sem("xT_late_done")
        x_high = sem("x_high")
        x_low = sem("x_low")
        q_high = sem("q_high")
        q_low = sem("q_low")
        k_high = sem("k_high")
        k_spread = sem("k_spread")
        k_low = sem("k_low")
        scored = sem("scored")
        decayed = sem("decayed")
        attended = sem("attended")
        squared = sem("squared")
        ssq_added = sem("ssq_added")
        gated_done = sem("gated_done")
        gated_high = sem("gated_high")
        gated_split = sem("gated_split")
        wo_high = sem("wo_high")
        wo_split = sem("wo_split")
        squares_summed = sem("squares_summed")
        ms_first_done = sem("ms_first_done")
        rms_first_done = sem("rms_first_done")
        branch_first_done = sem("branch_first_done")
        x1_first_done = sem("x1_first_done")
        rstd_first_done = sem("rstd_first_done")
        out_done = sem("out_done")
        int8_step = sem("int8_step")
        q_turned = sem("q_turned")
        linear_done = sem("linear_done")
        z_tanh = sem("z_tanh")
        acc_done = sem("acc_done")
        block = ctx.enter_context(nc.Block())

        LINKS = 13

        def count(n, s, what):
            kinds = ("q", "k", "gate") if s % 2 else ("q", "k", "v0", "v1", "gate")
            return 4 * n + s % 2 + kinds.index(what) + 1

        def late(it, s):
            return isinstance(it, int) and it == 0 and s < (BATCHES - EARLY) // 2

        def rows(h):
            return slice(h * D0, (h + 1) * D0)

        def sequence(tensor, b):
            return tensor[:, 2 * b:2 * b + 2] if isinstance(b, int) else tensor[:, bass.ds(2 * b, 2)]

        @block.sync
        def _(sp):
            def load(pair, i):
                wait(sp, w_split, pair - 1)
                wait(sp, wo_ready, pair - 1)
                sp.dma_start(stage[i][:], w0_d[pair]).then_inc(w_in[i], 16)

            with sp.Fori(1, PAIRS // 2) as it:
                load(2 * it, 0)
                load(2 * it + 1, 1)

        @block.gpsimd
        def _(pool):
            def split(pair, i):
                pool.wait_ge(w_hi_done, pair + 1)
                wide = stage[i][:, 0:CH * COLS].rearrange("p (c n) -> p c n", c=CH)
                for cols, done in ((slice(2 * P, 3 * P), v_split), (slice(0, 2 * P), None),
                                   (slice(3 * P, 4 * P), w_split)):
                    part = pool.tensor_tensor(w_lo[:, i, :, cols], wide[:, :, cols],
                                              w_hi[:, i, :, cols].bitcast(F32), ALU.subtract)
                    if done is not None:
                        part.then_inc(done, 1)

            def split_out_weights(pair, i):
                pool.wait_ge(wo_high, pair + 1)
                pool.tensor_tensor(wo_lo[i][:], wo[i][:], wo_hi[i][:].bitcast(F32), ALU.subtract)\
                    .then_inc(wo_split, 1)

            def split_gated(t, s):
                pool.wait_ge(gated_high, t + 1)
                pool.tensor_tensor(gated_lo[:, s % 2, :], gated[:], gated_hi[:, s % 2, :].bitcast(F32),
                                   ALU.subtract).then_inc(gated_split, 1)

            def add_squares(t, s):
                pool.wait_ge(squared, t + 1)
                g = s // 2
                wait(pool, ssq_added, t)
                pool.tensor_tensor(ssq[:, g * GROUP:(g + 1) * GROUP], ssq[:, g * GROUP:(g + 1) * GROUP],
                                   sq[:], ALU.add).then_inc(ssq_added, 1)

            def steps(it, last=False):
                for s in range(BODY):
                    if s >= BODY - 2 and not last:
                        split(2 * it + 2 + s % 2, s % 2)
                    if last and s == BODY - 1:
                        first_sequence()
                        split_gated(it * BODY + s, s)
                    add_squares(it * BODY + s, s)
                    if not (last and s == BODY - 1):
                        split_gated(it * BODY + s, s)
                    if s < 2:
                        split_out_weights(2 * it + s, s)

            def first_sequence():
                pool.wait_ge(ms_first_done, 1)
                pool.tensor_tensor(rms_first[:], ms_first[:], half[:, 0:BT], ALU.pow).then_inc(rms_first_done, 1)
                pool.wait_ge(branch_first_done, 1)
                pool.tensor_tensor(x[:, 0:BT, :], x[:, 0:BT, :], xn[:, 0:BT, :], ALU.add).then_inc(x1_first_done, 1)
                pool.wait_ge(moment_step, 2 * GT + 2 + 2 * BT)
                pool.tensor_tensor(rstd[:, 0:BT], var[:, 0:BT], half[:, 0:BT], ALU.pow).then_inc(rstd_first_done, 1)

            pool.wait_ge(moment_step, 2 * GT + 1)
            pool.tensor_tensor(rstd[:, TILES - GT:TILES], var[:], half[:, 0:GT], ALU.pow).then_inc(rstd_late, 1)
            pool.memset(acc[:, TILES // 2:TILES, :], 0.0).then_inc(sums_cleared, 1)
            heads = decay[:, HEADS0 // 2:HEADS0, 0:P]
            pool.affine_select(out=heads, in_=heads, compare_op=ALU.is_ge, fill=0.0, base=0,
                               pattern=[[0, HEADS0 // 2], [1, P]], channel_multiplier=-1).then_inc(tables_masked, 1)
            steps(0)
            with pool.Fori(1, STEPS // BODY - 1) as it:
                steps(it)
            steps(STEPS // BODY - 1, True)

        @block.scalar
        def _(act):
            def silu(n, s, what, src, dst):
                act.wait_ge(projected, count(n, s, what))
                act.activation(dst, src, ACT.Silu).then_inc(activated, 1)

            def high_x(i):
                act.wait_ge(xT_done, i + 1)
                act.activation(xn_hi[:, :, (EARLY + i) * SEQ:(EARLY + i + 1) * SEQ],
                               bank[7][:].rearrange("p (c n) -> p c n", c=CH), ACT.Copy).then_inc(x_high, 1)

            def qkv(n, s):
                wait(act, q_low, n)
                silu(n, s, "q", bank[0][:], q[:])
                act.wait_ge(activated, count(n, s, "q"))
                wait(act, scored, 4 * n)
                for h in range(2):
                    last = act.activation(q_parts[h][rows(h)], q[rows(h)], ACT.Copy)
                last.then_inc(q_high, 1)
                if isinstance(n, int) and 0 < n and late(0, n - 1):
                    high_x(2 * (n - 1))
                wait(act, k_low, n)
                silu(n, s, "k", bank[1][:], k[:])
                act.wait_ge(activated, count(n, s, "k"))
                for h in range(2):
                    last = act.activation(k_twice[h][rows(h)], k[rows(h)], ACT.Copy)
                last.then_inc(k_high, 1)
                if s % 2 == 0:
                    for i in range(2):
                        out = v[:, s // 2 % 2, 2 * i:2 * i + 2].rearrange("p t i n -> p (t i n)")
                        silu(n, s, f"v{i}", bank[7 - 7 * i][:], out)
                if isinstance(n, int) and 0 < n and late(0, n - 1):
                    high_x(2 * (n - 1) + 1)
                for h in range(2):
                    last = act.activation(k_twice[h][rows(1 - h)], k[rows(h)], ACT.Copy)
                last.then_inc(k_spread, 1)

            def gate(n, s):
                act.wait_ge(projected, count(n, s, "gate"))
                wait(act, gated_done, n)
                act.activation(th[:], bank[1][:], ACT.Tanh, scale=0.5).then_inc(activated, 1)

            def high_weights(pair, i, turn):
                if not (isinstance(pair, int) and pair < 2):
                    act.wait_ge(projected, count(BODY * turn - 2 + i, i, "gate"))
                act.wait_ge(w_in[i], 16 * (turn + 1))
                act.activation(w_hi[:, i], stage[i][:, 0:CH * COLS].rearrange("p (c n) -> p c n", c=CH),
                               ACT.Copy).then_inc(w_hi_done, 1)

            def high_out_weights(pair, i, turn):
                act.wait_ge(wo_ready, pair + 1)
                wait(act, out_done, 2 * (BODY * turn - 1 + i))
                act.activation(wo_hi[i][:], wo[i][:], ACT.Copy).then_inc(wo_high, 1)

            def high_gated(t, s):
                act.wait_ge(gated_done, t + 1)
                wait(act, out_done, 2 * t - 2)
                act.activation(gated_hi[:, s % 2, :], gated[:], ACT.Copy).then_inc(gated_high, 1)

            def square(t, s):
                act.wait_ge(attended, t + 1)
                wait(act, ssq_added, t)
                act.activation(sq[:], bank[4][:], ACT.Square).then_inc(squared, 1)

            def tanh_z(b):
                act.wait_ge(int8_step, LINKS * b + 12)
                act.activation(thz[:], z16[:], ACT.Tanh, scale=0.5).then_inc(z_tanh, 1)

            def steps(it, last=False):
                for s in range(BODY):
                    t = it * BODY + s
                    more = not (last and s == BODY - 1)
                    if s == 7:
                        tanh_z(it)
                    if s >= BODY - 2 and not last:
                        high_weights(2 * it + 2 + s % 2, s % 2, it + 1)
                    if more:
                        qkv(t + 1, s + 1)
                    square(t, s)
                    if more:
                        gate(t + 1, s + 1)
                    high_gated(t, s)
                    if s < 2:
                        high_out_weights(2 * it + s, s, it)

            qkv(0, 0)
            gate(0, 0)
            steps(0)
            with act.Fori(1, STEPS // BODY - 1) as it:
                steps(it)
            steps(STEPS // BODY - 1, True)

        @block.vector
        def _(dve):
            def out_weights(pair, i, turn):
                wait(dve, wo_split, pair - 1)
                dve.wait_ge(w_in[i], 16 * (turn + 1))
                dve.tensor_scalar(wo[i][:], stage[i][:, CH * COLS:CH * COLS + HID],
                                  stage[i][:, WROW - 1:WROW], 0.5, ALU.mult, ALU.mult).then_inc(wo_ready, 1)

            def decays(t, j, pair):
                dve.wait_ge(scored, 4 * t + j + 1)
                head = 2 * pair + j % 2
                dve.tensor_tensor(aw[:, j, 0:2 * P], bank[2 + j % 2][:, 0:2 * P], decay[:, head, :], ALU.mult)
                dve.tensor_tensor(aw[:, j, 2 * P:3 * P], bank[2 + j % 2][:, 2 * P:3 * P],
                                  decay[:, head, 0:P], ALU.mult).then_inc(decayed, 1)

            def low_queries(n):
                dve.wait_ge(q_high, n + 1)
                for h in range(2):
                    last = dve.tensor_tensor(q_parts[h][rows(1 - h)], q[rows(h)], q_parts[h][rows(h)].bitcast(F32),
                                             ALU.subtract)
                last.then_inc(q_low, 1)

            def low_keys(n):
                dve.wait_ge(k_high, n + 1)
                wait(dve, scored, 4 * n)
                for h in range(2):
                    last = dve.tensor_tensor(k_lo[rows(h)], k[rows(h)], k_twice[h][rows(h)].bitcast(F32),
                                             ALU.subtract)
                last.then_inc(k_low, 1)

            def gates(t, s):
                dve.wait_ge(squared, t + 1)
                dve.wait_ge(activated, count(t, s, "gate"))
                wait(dve, gated_split, t)
                dve.scalar_tensor_tensor(gated[:], th[:], 1.0, bank[4][:], ALU.add, ALU.mult)\
                    .then_inc(gated_done, 1)

            def accumulate(t, s, u):
                dve.wait_ge(out_done, 2 * t + u + 1)
                wait(dve, acc_done, 2 * t + u - 1)
                m = GT * (s % BODY // 2) + 2 * u
                part = acc[:, m:m + 2, :].rearrange("p t n -> p (t n)")
                dve.tensor_tensor(part, bank[5 + u][:], part, ALU.add).then_inc(acc_done, 1)

            def int8_layer(b, s):
                k = LINKS * b

                def link(n):
                    dve.wait_ge(int8_step, k + n)

                if s == 0:
                    dve.tensor_copy(mean_now[:], sequence(mv, b)[:, :, 0]).then_inc(int8_step, 1)
                    dve.tensor_copy(rstd_now[:], sequence(rstd, b)).then_inc(int8_step, 1)
                if s == 1:
                    link(2)
                    for m in range(BT):
                        last = dve.tensor_scalar(xq[:, m, :], sequence(x, b)[:, m, :], mean_now[:, m:m + 1],
                                                 rstd_now[:, m:m + 1], ALU.subtract, ALU.mult)
                    last.then_inc(int8_step, 1)
                if s == 2:
                    link(3)
                    dve.tensor_reduce(absmax[:], xq[:], AX.X, ALU.max, apply_absolute_value=True)\
                        .then_inc(int8_step, 1)
                    link(4)
                    dve.tensor_scalar(in_sc[:], absmax[:], 1e-7, 1.0 / 127.0, ALU.max, ALU.mult)\
                        .then_inc(int8_step, 1)
                    link(5)
                    dve.reciprocal(in_inv[:], in_sc[:]).then_inc(int8_step, 1)
                if s == 3:
                    link(6)
                    for m in range(BT):
                        last = dve.tensor_scalar(xq[:, m, :], xq[:, m, :], in_inv[:, m:m + 1], ROUND,
                                                 ALU.mult, ALU.add)
                    last.then_inc(int8_step, 1)
                    link(7)
                    dve.tensor_scalar(xq[:], xq[:], ROUND + 127.0, ROUND - 128.0, ALU.min, ALU.max)\
                        .then_inc(int8_step, 1)
                if s == 4:
                    link(8)
                    dve.tensor_scalar(q16[:], xq[:], -ROUND, None, ALU.add).then_inc(int8_step, 1)
                if s == 5:
                    dve.wait_ge(q_turned, b + 1)
                    dve.tensor_copy(qT[:], bank[7][:, 0:HID].bitcast(BF16).rearrange("p (c n) -> p c n", c=CH))\
                        .then_inc(int8_step, 1)
                if s == 6:
                    dve.wait_ge(linear_done, b + 1)
                    for m in range(BT):
                        last = dve.scalar_tensor_tensor(z[:, m, :], bank[7][:, m * HID:(m + 1) * HID],
                                                        in_sc[:, m:m + 1], w_sc[:], ALU.mult, ALU.mult)
                    last.then_inc(int8_step, 1)
                if s == 7:
                    dve.wait_ge(z_tanh, b + 1)
                    dve.tensor_scalar(sg16, thz[:], 0.5, 0.5, ALU.mult, ALU.add).then_inc(int8_step, 1)
                    link(13)
                    dve.tensor_tensor(sequence(g16, b), z16[:], sg16, ALU.mult)

            def int8_bias(b):
                dve.wait_ge(int8_step, LINKS * b + 11)
                for m in range(BT):
                    last = dve.tensor_tensor(z16[:, m, :], z[:, m, :], bias[:], ALU.add)
                last.then_inc(int8_step, 1)

            def last_moments():
                dve.wait_ge(x_last_in, 16)
                for m in range(GT):
                    dve.bn_stats(stats[:, m, :], x[:, TILES - GT + m, :]).then_inc(moment_step, 1)
                for m in range(GT):
                    dve.wait_ge(moment_step, m + 1)
                    dve.bn_aggr(mv[:, TILES - GT + m, :], stats[:, m, :]).then_inc(moment_step, 1)
                dve.wait_ge(moment_step, 2 * GT)
                dve.tensor_scalar(var[:], mv[:, TILES - GT:TILES, 1], 1e-5, None, ALU.add)\
                    .then_inc(moment_step, 1)

            def centre(s):
                if s:
                    dve.wait_ge(rstd_late, 1)
                wait(dve, xT_done, 2 * s)
                for m in range(GT):
                    t = 2 * EARLY + GT * s + m
                    last = dve.tensor_scalar(xn[:, m, :], x[:, t, :], mv[:, t, 0:1], rstd[:, t:t + 1],
                                             ALU.subtract, ALU.mult)
                last.then_inc(xn_done, 1)

            def first_squares():
                dve.wait_ge(squares_summed, BT)
                dve.tensor_scalar(ms_first[:], bank[7][:, 0:BT], 1.0 / (HEADS0 * D0), 1e-5, ALU.mult, ALU.add)\
                    .then_inc(ms_first_done, 1)

            def first_branch():
                dve.wait_ge(acc_done, 2 * (STEPS - BODY + 2))
                dve.wait_ge(rms_first_done, 1)
                for m in range(BT):
                    last = dve.scalar_tensor_tensor(xn[:, m, :], acc[:, m, :], rms_first[:, m:m + 1], g16[:, m, :],
                                                    ALU.mult, ALU.mult)
                last.then_inc(branch_first_done, 1)

            def first_moments():
                dve.wait_ge(x1_first_done, 1)
                for m in range(BT):
                    dve.bn_stats(stats[:, m, :], x[:, m, :]).then_inc(moment_step, 1)
                dve.wait_ge(moment_step, 2 * GT + 1 + BT)
                for m in range(BT):
                    dve.bn_aggr(mv[:, m, :], stats[:, m, :]).then_inc(moment_step, 1)
                dve.wait_ge(moment_step, 2 * GT + 1 + 2 * BT)
                dve.tensor_scalar(var[:, 0:BT], mv[:, 0:BT, 1], 1e-5, None, ALU.add).then_inc(moment_step, 1)

            def first_centre():
                dve.wait_ge(rstd_first_done, 1)
                for m in range(BT):
                    dve.tensor_scalar(xn1[:, m, :], x[:, m, :], mv[:, m, 0:1], rstd[:, m:m + 1],
                                      ALU.subtract, ALU.mult)

            def low_x(i):
                dve.wait_ge(x_high, i + 1)
                c = slice((EARLY + i) * SEQ, (EARLY + i + 1) * SEQ)
                dve.tensor_tensor(xn_lo[:, :, c], bank[7][:].rearrange("p (c n) -> p c n", c=CH),
                                  xn_hi[:, :, c].bitcast(F32), ALU.subtract).then_inc(x_low, 1)

            def steps(it, last=False):
                for s in range(BODY):
                    t = it * BODY + s
                    if late(it, s):
                        centre(s)
                    if isinstance(it, int) and it == 0 and s == BODY // 2:
                        dve.wait_ge(sums_cleared, 1)
                        dve.wait_ge(tables_masked, 1)
                    if last and s == BODY - 1:
                        first_squares()
                    for j in range(4):
                        if j == 2 and s == 6:
                            int8_layer(it, s)
                        decays(t, j, 2 * it + s % 2)
                    if not (last and s == BODY - 1):
                        low_queries(t + 1)
                    if s == 6:
                        int8_bias(it)
                    if late(it, s):
                        low_x(2 * s)
                    if s == BODY - 1 and not last:
                        out_weights(2 * it + 2, 0, it + 1)
                    if s not in (5, 6):
                        int8_layer(it, s)
                    if not (last and s == BODY - 1):
                        low_keys(t + 1)
                    if last and s == BODY - 1:
                        first_branch()
                    for u in range(2):
                        if s or not isinstance(it, int) or it:
                            accumulate(t - 1, s + BODY - 1, u)
                    if last and s == BODY - 1:
                        first_moments()
                    if s == 5:
                        int8_layer(it, s)
                    if late(it, s):
                        low_x(2 * s + 1)
                    gates(t, s)
                    if s == BODY - 1 and not last:
                        out_weights(2 * it + 3, 1, it + 1)

            out_weights(0, 0, 0)
            out_weights(1, 1, 0)
            last_moments()
            low_queries(0)
            low_keys(0)
            steps(0)
            with dve.Fori(1, STEPS // BODY - 1) as it:
                steps(it)
            steps(STEPS // BODY - 1, True)
            first_centre()
            for u in range(2):
                accumulate(STEPS - 1, BODY - 1, u)

        @block.tensor
        def _(pe):
            def columns(n, s, what, out):
                i, g = s % 2, s % BODY // 2
                toks = slice(g * GROUP, (g + 1) * GROUP)
                cols = slice(what * P, (what + 1) * P)
                for c in range(CH):
                    for a, b in ((w_hi, xn_hi), (w_hi, xn_lo), (w_lo, xn_hi)):
                        last = pe.matmul(out, a[:, i, c, cols], b[:, c, toks],
                                         start=(c == 0 and a is w_hi and b is xn_hi),
                                         stop=(c == CH - 1 and a is w_lo))
                last.then_inc(projected, 1)

            def turn_x(i, t):
                pe.wait_ge(xn_done, i // 2 + 1)
                if i == 0:
                    pe.wait_ge(activated, count(0, 0, "v0"))
                else:
                    pe.wait_ge(x_low, i)
                if i == 3:
                    pe.wait_ge(activated, count(2, 2, "v0"))
                for m in range(BT):
                    for c in range(CH):
                        last = pe.transpose(bank[7][:, c * SEQ + m * P:c * SEQ + (m + 1) * P],
                                            xn[:, BT * (i % 2) + m, c * P:(c + 1) * P], ident[:])
                last.then_inc(xT_done, 1)

            def query(n, s, pair):
                pe.wait_ge(w_split, pair + 1)
                if isinstance(n, int) and EARLY <= n < BODY:
                    pe.wait_ge(x_low, 2 * (n // 2) - EARLY + 2)
                wait(pe, activated, count(n - 1, s - 1, "q" if s % 2 == 0 else "v1"))
                columns(n, s, 0, bank[0][:])

            def key(n, s):
                wait(pe, activated, count(n - 1, s - 1, "gate"))
                columns(n, s, 1, bank[1][:])

            def values(n, s, it):
                for i in range(2):
                    if i:
                        pe.wait_ge(activated, count(n, s, "q"))
                    else:
                        pe.wait_ge(v_split, 2 * it + 1 + (2 if s == BODY else 0))
                        if isinstance(n, int) and 0 < n < BODY:
                            pe.wait_ge(x_low, min(n + 1, BATCHES - EARLY))
                        if s == BODY:
                            pe.wait_ge(int8_step, LINKS * it + 11)
                    for m in range(2):
                        tile = GT * (s % BODY // 2) + 2 * i + m
                        toks = slice(tile * P, (tile + 1) * P)
                        for c in range(CH):
                            for a, b in ((xn_hi, w_hi), (xn_lo, w_hi), (xn_hi, w_lo)):
                                last = pe.matmul(bank[7 - 7 * i][:, m * 2 * P:(m + 1) * 2 * P], a[:, c, toks],
                                                 b[:, :, c, 2 * P:3 * P],
                                                 start=(c == 0 and a is xn_hi and b is w_hi),
                                                 stop=(c == CH - 1 and b is w_lo))
                    last.then_inc(projected, 1)

            def gate(n, s):
                pe.wait_ge(activated, count(n, s, "k"))
                columns(n, s, 3, bank[1][:])

            def scores(t, s, j):
                pe.wait_ge(q_low, t + 1)
                pe.wait_ge(k_low, t + 1)
                pe.wait_ge(k_spread, t + 1)
                wait(pe, decayed, 4 * t + j - 1)
                b, h = (j // 2) * SEQ, j % 2
                out = bank[2 + h]
                for o, keys, n in ((0, b, SEQ), (SEQ, b + P, P)):
                    queries = slice(b + SEQ - n, b + SEQ)
                    pe.matmul(out[:, o:o + n], k_twice[h][:, keys:keys + P], q_parts[h][:, queries],
                              start=True, stop=False)
                    last = pe.matmul(out[:, o:o + n], k_lo[rows(h), keys:keys + P], q_parts[h][rows(h), queries],
                                     start=False, stop=True)
                last.then_inc(scored, 1)

            def attend(t, s):
                pe.wait_ge(decayed, 4 * t + 4)
                if s % 2 == 0:
                    pe.wait_ge(activated, count(t, s, "v1"))
                wait(pe, gated_done, t)
                wait(pe, squared, t)
                for b in range(2):
                    for tile in range(2):
                        for h in range(2):
                            r = slice(D0 * h, D0 * (h + 1))
                            cols = aw[:, 2 * b + h, 0:2 * P] if tile == 0 else aw[:, 2 * b + h, 2 * P:3 * P]
                            out = bank[4][r, b * SEQ + tile * P:(b + 1) * SEQ]
                            last = pe.matmul(out, v[:, s // 2 % 2, 2 * b + tile, s % 2, r], cols,
                                             start=(tile == 0), stop=(tile == 1))
                last.then_inc(attended, 1)

            def sum_squares(m0, m1):
                pe.wait_ge(ssq_added, STEPS - BODY + 2 * ((m1 + GT - 1) // GT))
                for m in range(m0, m1):
                    pe.matmul(bank[7][:, m:m + 1], ssq[:, m * P:(m + 1) * P], ones[:], start=True, stop=True)\
                        .then_inc(squares_summed, 1)

            def turn_quantised(b):
                pe.wait_ge(int8_step, LINKS * b + 9)
                pe.wait_ge(activated, count(BODY * b + 6, 6, "v0"))
                for m in range(BT):
                    for c in range(CH):
                        last = pe.transpose(bank[7][:].bitcast(BF16)[:, c * SEQ + m * P:c * SEQ + (m + 1) * P],
                                            q16[:, m, c * P:(c + 1) * P], identb[:])
                last.then_inc(q_turned, 1)

            def linear(b):
                pe.wait_ge(int8_step, LINKS * b + 10)
                for m in range(BT):
                    for c in range(CH):
                        last = pe.matmul(bank[7][:, m * HID:(m + 1) * HID], qT[:, c, m * P:(m + 1) * P],
                                         wb[:, c, :], start=(c == 0), stop=(c == CH - 1))
                last.then_inc(linear_done, 1)

            def back(t, s, pair):
                i = s % 2
                pe.wait_ge(gated_split, t + 1)
                pe.wait_ge(wo_split, pair + 1)
                for u in range(2):
                    wait(pe, acc_done, 2 * t + u - 1)
                    for m in range(2):
                        toks = slice((2 * u + m) * P, (2 * u + m + 1) * P)
                        for a, b in ((gated_hi, wo_hi), (gated_hi, wo_lo), (gated_lo, wo_hi)):
                            last = pe.matmul(bank[5 + u][:, m * HID:(m + 1) * HID], a[:, s % 2, toks], b[i][:],
                                             start=(a is gated_hi and b is wo_hi), stop=(a is gated_lo))
                    last.then_inc(out_done, 1)

            def steps(it, last=False):
                for s in range(BODY):
                    t = it * BODY + s
                    more = not (last and s == BODY - 1)
                    if not more:
                        pe.wait_ge(int8_step, LINKS * (BATCHES - 1) + 11)
                        sum_squares(0, BT)
                    scores(t, s, 0)
                    scores(t, s, 1)
                    if s == 6:
                        linear(it)
                    if more:
                        query(t + 1, s + 1, 2 * it + (s + 1) % 2 + (2 if s == BODY - 1 else 0))
                    scores(t, s, 2)
                    scores(t, s, 3)
                    if late(it, s):
                        turn_x(2 * s, t)
                    if more:
                        key(t + 1, s + 1)
                    if s or not isinstance(it, int) or it:
                        back(t - 1, s + BODY - 1, 2 * it + (s + 1) % 2 - (2 if s == 0 else 0))
                    if more and s % 2:
                        values(t + 1, s + 1, it)
                    if late(it, s):
                        turn_x(2 * s + 1, t)
                    if s == 5:
                        turn_quantised(it)
                    attend(t, s)
                    if not more:
                        pe.wait_ge(ms_first_done, 1)
                        sum_squares(BT, TILES - GT)
                    if more:
                        gate(t + 1, s + 1)

            values(0, 0, 0)
            gate(0, 0)
            steps(0)
            with pe.Fori(1, STEPS // BODY - 1) as it:
                steps(it)
            steps(STEPS // BODY - 1, True)
            back(STEPS - 1, BODY - 1, PAIRS - 1)
            sum_squares(TILES - GT, TILES)


ORDER = [4 * k + i for k in range(HEADS1 // 4) for i in (0, 2, 1, 3)]
SLOTS = len(ORDER)


def score_bank(n):
    return 1 + (1 if n == SLOTS - 1 else n % 3)


def score_bank_before(n):
    return {0: -4, 1: -1, 2: -2, SLOTS - 1: SLOTS - 3}.get(n, n - 3)


def layer_one(nc, bank, x, xn, acc, g16, ident, identb, ones, wqkv, wqkv_in, wo_d, bq_d, bk_d, bv_d, bo_d,
              ebias_d, w13_d, w2_d, out_d):
    ctx = ExitStack()

    def sb(name, shape, dt):
        return ctx.enter_context(nc.sbuf_tensor(name, shape, dt))

    def sem(name):
        return ctx.enter_context(nc.semaphore(name))

    GE = EG * P
    HH = HEADS1 // 2
    ms = sb("ms", [P, TILES], F32)
    half = sb("half1", [P, TILES], F32)
    rms_now = sb("rms_now", [P, BT], F32)
    branch = sb("branch", [P, BT, HID], F32)
    wqkv_hi = sb("wqkv_hi", [P, CH, QKVR], F32R)
    wqkv_lo = sb("wqkv_lo", [P, CH, QKVR], F32R)
    wo = sb("w_out1", [P, CH, HID], F32)
    with nc.sbuf_tensor("w13", [P, EX // EG, CH, 2, GE], F32) as w13:
        pass
    w2_hi = sb("w2_hi", [P, EX, HID], F32R)
    w2_lo = sb("w2_lo", [P, EX, HID], F32R)
    w13_hi = sb("w13_hi", [P, EX // EG, CH, 2, GE], F32R)
    w13_lo = sb("w13_lo", [P, EX // EG, CH, 2, GE], F32R)
    w2 = sb("w2", [P, EX, HID], F32)
    bq = sb("bq", [P, CH], F32)
    bk = sb("bk", [P, CH], F32)
    bv = sb("bv", [P, HID], F32)
    bo = sb("bo", [P, HID], F32)
    ebias = sb("ebias", [P, EXPERTS], F32)
    row_i = sb("row_i", [P, 2], I32)
    par = sb("par", [P, 2], F32)
    causal = sb("causal", [P, 2 * P], BF16)
    number = sb("number", [P, EXPERTS], I32)
    numberf = sb("numberf", [P, EXPERTS], F32)
    tick = sb("tick", [P, 1], F32)
    warm = sb("warm", [P, 1], F32)
    stats = sb("stats1", [P, BT, 6], F32)
    mv = sb("mv1", [P, BT, 2], F32)
    var = sb("var1", [P, BT], F32)
    rstd = sb("rstd1", [P, BT], F32)
    one = sb("one", [P, 1, 1], F32)
    xh = sb("xh", [P, CH, SEQ], F32R)
    xl = sb("xl", [P, CH, SEQ], F32R)
    bqm = sb("bqm", [P, 2, CH], F32)
    qm = sb("qm", [P, 2, CH, SEQ], F32)
    kT = sb("kT", [P, CH, SEQ], F32)
    vm = sb("vm", [P, BT, HEADS1 // 2, 2, 2 * D1], F32)
    v_late = sb("v_late", [P, BT, HH, D1], F32)
    nmax = sb("nmax", [P, HEADS1, BT], F32)
    prob = sb("prob", [P, 4, 3 * P], F32)
    probT = sb("probT", [P, 4, 3 * P], F32)
    sums = sb("sums", [P, BT, HEADS1], F32)
    rinv = sb("rinv", [P, BT, HEADS1], F32)
    rsum = sb("rsum", [P, BT, HEADS1, D1], F32)
    oS = sb("oS", [P, CH * SEQ], F32)
    oT = sb("oT", [P, CH, SEQ], F32)
    s1 = sb("s1", [P, BT, HID], F32)
    en = sb("en", [P, BT, EXPERTS], F32)
    en1 = sb("en1", [P, BT, EXPERTS], F32)
    score = sb("score", [P, BT, EXPERTS], F32)
    ranked = sb("ranked", [P, BT, EXPERTS], F32)
    top = sb("top", [P, BT, 8], F32)
    topi = sb("topi", [P, BT, 8], U32)
    topf = sb("topf", [P, BT, 2], F32)
    first = sb("first", [P, BT, EXPERTS], F32)
    chosen = sb("chosen", [P, BT, EXPERTS], F32)
    share = sb("share", [P, BT, EX], F32)
    half_s = sb("half_s", [P, BT, EX], F32)
    half_s2 = sb("half_s2", [P, BT, EX], F32)
    th = sb("th1", [P, GE], F32)
    tu = sb("tu", [P, GE], F32)
    hh = sb("hh", [P, GE], F32)
    hT_hi = sb("hT_hi", [P, BT, EX, P], F32R)
    hT_lo = sb("hT_lo", [P, BT, EX, P], F32R)
    thy = sb("thy", [P, BT * HID], F32)
    gy = sb("gy", [P, BT * HID], F32)
    prod = sb("prod", [P, BT * HID], F32)
    xo = sb("xo", [P, BT, HID], F32)

    w_in = sem("w1_in")
    w13_in = [sem(f"w13_in{g}") for g in range(EX // EG)]
    w2_in = sem("w2_in")
    consts = sem("consts1")
    ms_done = sem("ms_done")
    rms_done = sem("rms_done")
    branch_done = sem("branch_done")
    x1_done = sem("x1_done")
    wqkv_high = sem("wqkv_high")
    wqkv_split = sem("wqkv_split")
    wv_split = sem("wv_split")
    w13_high = sem("w13_high")
    w13_split = sem("w13_split")
    once = sem("once")
    stats_done = sem("stats1_done")
    mv_done = sem("mv1_done")
    var_done = sem("var1_done")
    rstd_done = sem("rstd1_done")
    xn_done = sem("xn1_done")
    xT_done = sem("xT1_done")
    hi_done = sem("hi1_done")
    lo_done = sem("lo1_done")
    qk_proj = sem("qk_proj")
    v_proj = sem("v_proj")
    q_done = sem("q1_done")
    k_done = sem("k1_done")
    v_read = sem("v1_read")
    v_late_done = sem("v_late_done")
    en_done = sem("en_done")
    route = sem("route")
    scored = sem("scored1")
    max_done = sem("max_done")
    exp_done = sem("exp_done")
    turned = sem("turned")
    turn_copied = sem("turn_copied")
    pv_done = sem("pv_done")
    inverted = sem("inverted")
    rsum_done = sem("rsum_done")
    rsum_turned = sem("rsum_turned")
    oS_done = sem("oS_done")
    oT_done = sem("oT_done")
    wo_done = sem("wo_done")
    s1_done = sem("s1_done")
    w3_done = sem("w3_done")
    w1_done = sem("w1_done")
    tanh_done = sem("tanh_done")
    tu_done = sem("tu_done")
    h_done = sem("h_done")
    h_turned = sem("h_turned")
    h_high = sem("h_high")
    h_copied = sem("h_copied")
    w2_high = sem("w2_high")
    w2_split = sem("w2_split")
    y_done = sem("y_done")
    thy_done = sem("thy_done")
    gy_done = sem("gy_done")
    prod_done = sem("prod_done")
    xo_done = sem("xo_done")
    stored = sem("stored")
    block = ctx.enter_context(nc.Block())
    ROUTE = 13

    def program(eng, prologue, body, tail):
        prologue()
        body(0, first=True)
        with eng.Fori(1, BATCHES - 1) as b:
            body(b)
        body(BATCHES - 1, last=True)
        tail(BATCHES - 1)

    def sequence(tensor, b):
        return tensor[:, 2 * b:2 * b + 2] if isinstance(b, int) else tensor[:, bass.ds(2 * b, 2)]

    def unit(u):
        return u // (UNITS // BT), u % (UNITS // BT)

    @block.sync
    def _(sp):
        def store(b):
            sp.wait_ge(xo_done, b + 1)
            sp.dma_start(out_d.rearrange("(b t p) d -> b p t d", b=BATCHES, p=P)[b], xo[:]).then_inc(stored, 16)

        sp.dma_start(bq[:], bq_d).then_inc(w_in, 16)
        sp.dma_start(bk[:], bk_d).then_inc(w_in, 16)
        sp.dma_start(bv[:], bv_d).then_inc(w_in, 16)
        sp.dma_start(ebias[:], ebias_d).then_inc(w_in, 16)
        for g in range(EX // EG):
            sp.dma_start(w13[:, g], w13_d[g].rearrange("(c p) i n -> p c i n", p=P)).then_inc(w13_in[g], 16)
        sp.dma_start(w2[:], w2_d.rearrange("e p n -> p e n")).then_inc(w2_in, 16)
        sp.dma_start(wo[:], wo_d.rearrange("(c p) n -> p c n", p=P)).then_inc(w2_in, 16)
        sp.dma_start(bo[:], bo_d).then_inc(w2_in, 16)
        store(0)
        with sp.Fori(1, BATCHES) as b:
            store(b)
        sp.wait_ge(stored, 16 * BATCHES)

    @block.gpsimd
    def _(pool):
        def constants():
            pool.memset(half[:], -0.5).then_inc(consts, 1)
            pool.memset(causal[:], 0.0).then_inc(consts, 1)
            pool.iota(row_i[:], pattern=[[0, 2]], base=0, channel_multiplier=1).then_inc(consts, 1)
            pool.iota(number[:], pattern=[[1, EXPERTS]], base=0, channel_multiplier=0).then_inc(consts, 1)
            pool.wait_ge(consts, 4)
            pool.affine_select(out=causal[:].rearrange("p (i n) -> p i n", i=2),
                               in_=causal[:].rearrange("p (i n) -> p i n", i=2), compare_op=ALU.is_ge,
                               fill=-1e30, base=0, pattern=[[0, 2], [-1, P]], channel_multiplier=1)\
                .then_inc(consts, 1)
            pool.memset(vm[:], 0.0).then_inc(once, 1)
            pool.memset(share[:], 1.0).then_inc(once, 1)

        def split_values():
            pool.wait_ge(wqkv_high, 2)
            pool.tensor_tensor(wqkv_lo[:, :, 2 * HID:QKVR], wqkv[:, :, 2 * HID:QKVR],
                               wqkv_hi[:, :, 2 * HID:QKVR].bitcast(F32), ALU.subtract).then_inc(wv_split, 1)

        def split_experts(g):
            pool.wait_ge(w13_high, g + 1)
            pool.tensor_tensor(w13_lo[:, g].rearrange("p c i n -> p (c i n)"),
                               w13[:, g].rearrange("p c i n -> p (c i n)"),
                               w13_hi[:, g].bitcast(F32).rearrange("p c i n -> p (c i n)"), ALU.subtract)\
                .then_inc(w13_split, 1)

        def root(b):
            if isinstance(b, int) and b == 1:
                pool.wait_ge(ms_done, 1)
            wait(pool, branch_done, b - 1)
            pool.tensor_tensor(rms_now[:], sequence(ms, b), half[:, 0:BT], ALU.pow).then_inc(rms_done, 1)

        def add_branch(b):
            pool.wait_ge(branch_done, b)
            pool.tensor_tensor(sequence(x, b), sequence(x, b), branch[:], ALU.add).then_inc(x1_done, 1)

        def power(b):
            pool.wait_ge(var_done, b)
            pool.tensor_tensor(rstd[:], var[:], half[:, 0:BT], ALU.pow).then_inc(rstd_done, 1)

        def late_values(b):
            pool.wait_ge(v_read, 2 * b + 2)
            wait(pool, pv_done, b)
            for t in range(BT):
                for m in range(2):
                    last = pool.tensor_tensor(
                        vm[:, t, HH // 2:HH, m, m * D1:(m + 1) * D1],
                        v_late[:, t].rearrange("p (q m) d -> p q m d", m=2)[:, :, m, :],
                        bv[:, HH * D1:HID].rearrange("p (q m d) -> p q m d", q=HH // 2, m=2)[:, :, m, :], ALU.add)
            last.then_inc(v_late_done, 1)

        def spread_sums(b, f):
            pool.wait_ge(inverted, 2 * b + f + 1)
            wait(pool, rsum_turned, b)
            heads = slice(f * HH, (f + 1) * HH)
            for t in range(BT):
                wide = rinv[:, t, heads].rearrange("p (h o) -> p h o", o=1).to_broadcast([P, HH, D1])
                last = pool.tensor_tensor(rsum[:, t, heads, :], wide, one[:].to_broadcast([P, HH, D1]), ALU.mult)
            last.then_inc(rsum_done, 1)

        def add(b):
            pool.wait_ge(prod_done, b + 1)
            wait(pool, stored, 16 * b)
            pool.tensor_tensor(xo[:], sequence(x, b), prod[:].rearrange("p (t n) -> p t n", t=BT), ALU.add)\
                .then_inc(xo_done, 1)

        def body(b, first=False, last=False):
            if not last:
                root(b + 1)
            late_values(b)
            if not first:
                add(b - 1)
            if not last:
                add_branch(b + 1)
                power(b + 1)
            if first:
                pool.wait_ge(w2_high, 1)
                pool.tensor_tensor(w2_lo[:], w2[:], w2_hi[:].bitcast(F32), ALU.subtract).then_inc(w2_split, 1)
            spread_sums(b, 0)
            spread_sums(b, 1)

        def prologue():
            constants()
            split_values()
            for g in range(EX // EG):
                split_experts(g)

        program(pool, prologue, body, add)

    @block.vector
    def _(dve):
        dve.memset(one[:], 1.0).then_inc(once, 1)

        def constants():
            dve.wait_ge(consts, 5)
            dve.tensor_scalar(row_i[:, 0:2], row_i[:, 0:2], 4, 1, ALU.logical_shift_right, ALU.bitwise_and)\
                .then_inc(consts, 1)
            dve.wait_ge(consts, 6)
            dve.tensor_scalar(par[:, 1:2], row_i[:, 1:2], 0.25, None, ALU.mult).then_inc(consts, 1)
            dve.tensor_scalar(par[:, 0:1], row_i[:, 0:1], -0.25, 0.25, ALU.mult, ALU.add).then_inc(consts, 1)
            dve.tensor_copy(numberf[:], number[:]).then_inc(consts, 1)
            dve.wait_ge(w_in, 64)
            dve.wait_ge(consts, 9)
            for m in range(2):
                dve.tensor_scalar(bqm[:, m, :], bq[:], par[:, m:m + 1], None, ALU.mult).then_inc(once, 1)
            dve.wait_ge(once, 5)

        def split_qkv():
            dve.wait_ge(wqkv_high, 1)
            dve.tensor_tensor(wqkv_lo[:, :, 0:2 * HID], wqkv[:, :, 0:2 * HID],
                              wqkv_hi[:, :, 0:2 * HID].bitcast(F32), ALU.subtract).then_inc(wqkv_split, 1)

        def squares():
            dve.tensor_scalar(ms[:], bank[7][:, 0:TILES], 1.0 / (HEADS0 * D0), 1e-5, ALU.mult, ALU.add)\
                .then_inc(ms_done, 1)

        def layer0_branch(b):
            dve.wait_ge(rms_done, b)
            wait(dve, x1_done, b - 1)
            for m in range(BT):
                last = dve.scalar_tensor_tensor(branch[:, m, :], sequence(acc, b)[:, m, :], rms_now[:, m:m + 1],
                                                sequence(g16, b)[:, m, :], ALU.mult, ALU.mult)
            last.then_inc(branch_done, 1)

        def moments(b):
            xt = sequence(x, b)
            dve.wait_ge(x1_done, b)
            dve.memset(tick[:], 0.0)
            for m in range(BT):
                dve.bn_stats(stats[:, m, :], xt[:, m, :]).then_inc(stats_done, 1)
            dve.wait_ge(stats_done, BT * b)
            dve.memset(tick[:], 0.0)
            for m in range(BT):
                dve.bn_aggr(mv[:, m, :], stats[:, m, :]).then_inc(mv_done, 1)
            dve.wait_ge(mv_done, BT * b)
            dve.tensor_scalar(var[:], mv[:, :, 1], 1e-5, None, ALU.add).then_inc(var_done, 1)

        def centre(b):
            xt = sequence(x, b)
            dve.wait_ge(rstd_done, b)
            for m in range(BT):
                dve.tensor_scalar(xn[:, m, :], xt[:, m, :], mv[:, m, 0:1], rstd[:, m:m + 1],
                                  ALU.subtract, ALU.mult).then_inc(xn_done, 1)

        def low_x(b):
            dve.wait_ge(hi_done, b + 1)
            dve.tensor_tensor(xl[:].rearrange("p c n -> p (c n)"), bank[0][:],
                              xh[:].bitcast(F32).rearrange("p c n -> p (c n)"), ALU.subtract).then_inc(lo_done, 1)

        def queries(b, c):
            dve.wait_ge(qk_proj, 2 * b + c + 1)
            for m in range(2):
                last = dve.tensor_scalar(qm[:, m, c, :], bank[7][:, 0:SEQ], par[:, m:m + 1],
                                         bqm[:, m, c:c + 1], ALU.mult, ALU.add)
            last.then_inc(q_done, 1)

        def values(b, t):
            src = bank[6 * t]
            dve.wait_ge(v_proj, 2 * b + t + 1)
            wait(dve, v_late_done, b)
            for m in range(2):
                dve.tensor_tensor(vm[:, t, 0:HH // 2, m, m * D1:(m + 1) * D1],
                                  src[:, 0:HH * D1].rearrange("p (q m d) -> p q m d", q=HH // 2, m=2)[:, :, m, :],
                                  bv[:, 0:HH * D1].rearrange("p (q m d) -> p q m d", q=HH // 2, m=2)[:, :, m, :],
                                  ALU.add)
            dve.tensor_copy(v_late[:, t].rearrange("p h d -> p (h d)"), src[:, HH * D1:HID]).then_inc(v_read, 1)

        def head_max(b, n):
            dve.wait_ge(scored, SLOTS * b + n + 1)
            s = bank[score_bank(n)]
            dve.tensor_reduce(nmax[:, n, 1:2], s[:, 0:2 * P], AX.X, ALU.max, negate=True)
            dve.tensor_reduce(nmax[:, n, 0:1], s[:, 2 * P:3 * P], AX.X, ALU.max, negate=True).then_inc(max_done, 1)

        def copy_turn(b, n):
            dve.wait_ge(turned, SLOTS * b + n + 1)
            dve.tensor_copy(probT[:, n % 4, :], bank[4][:, 0:3 * P]).then_inc(turn_copied, 1)

        def invert_sums(b, f):
            dve.wait_ge(exp_done, SLOTS * b + HH * (f + 1))
            wait(dve, rsum_done, 2 * b - 1 + f)
            heads = slice(f * HH, (f + 1) * HH)
            dve.reciprocal(rinv[:, :, heads], sums[:, :, heads]).then_inc(inverted, 1)

        def scale_heads(b):
            dve.wait_ge(rsum_turned, b + 1)
            dve.wait_ge(oS_done, b + 1)
            dve.tensor_tensor(oT[:].rearrange("p c n -> p (c n)"), bank[0][:], oS[:], ALU.mult).then_inc(oT_done, 1)

        def hidden_tanh(b, u):
            dve.wait_ge(tanh_done, UNITS * b + u + 1)
            dve.scalar_tensor_tensor(tu[:], th[:], 1.0, bank[7][:, 0:GE], ALU.add, ALU.mult).then_inc(tu_done, 1)

        def hidden(b, u):
            t, g = unit(u)
            dve.wait_ge(tu_done, UNITS * b + u + 1)
            dve.wait_ge(w3_done, UNITS * b + u + 1)
            for e in range(EG):
                c = slice(e * P, (e + 1) * P)
                last = dve.scalar_tensor_tensor(hh[:, c], tu[:, c], half_s2[:, t, g * EG + e:g * EG + e + 1],
                                                bank[6][:, c], ALU.mult, ALU.mult)
            last.then_inc(h_done, 1)

        def low_hidden(b, u):
            t, g = unit(u)
            dve.wait_ge(h_high, UNITS * b + u + 1)
            part = slice(g * EG, (g + 1) * EG)
            dve.tensor_tensor(hT_lo[:, t, part, :].rearrange("p e n -> p (e n)"), bank[6][:, 0:GE],
                              hT_hi[:, t, part, :].bitcast(F32).rearrange("p e n -> p (e n)"), ALU.subtract)\
                .then_inc(h_copied, 1)

        def gate(b):
            dve.wait_ge(thy_done, b + 1)
            dve.scalar_tensor_tensor(gy[:], thy[:], 1.0, bank[6][:], ALU.add, ALU.mult).then_inc(gy_done, 1)

        def finish(b):
            if isinstance(b, int) and b == 0:
                dve.wait_ge(w2_in, 48)
            dve.wait_ge(wo_done, b + 1)
            for t in range(BT):
                last = dve.tensor_tensor(s1[:, t], bank[0][:, t * HID:(t + 1) * HID], bo[:], ALU.add)
            last.then_inc(s1_done, 1)
            dve.wait_ge(s1_done, b + 1)
            dve.wait_ge(gy_done, b + 1)
            wait(dve, xo_done, b)
            dve.scalar_tensor_tensor(prod[:], s1[:].rearrange("p t n -> p (t n)"), 0.5, gy[:],
                                     ALU.mult, ALU.mult).then_inc(prod_done, 1)

        def router_scores(b):
            r0 = ROUTE * b

            def link(n):
                dve.wait_ge(route, r0 + n)

            dve.wait_ge(en_done, 2 * b + 2)
            dve.tensor_scalar(en1[:], en[:], 1.0, None, ALU.add).then_inc(route, 1)
            link(1)
            dve.reciprocal(score[:], en1[:]).then_inc(route, 1)
            link(2)
            for t in range(BT):
                dve.tensor_tensor(ranked[:, t], score[:, t], ebias[:], ALU.add).then_inc(route, 1)
            link(4)
            dve.memset(tick[:], 0.0)
            for t in range(BT):
                dve.max(top[:, t], ranked[:, t]).then_inc(route, 1)
            link(6)
            dve.memset(tick[:], 0.0)
            for t in range(BT):
                dve.max_index(topi[:, t], top[:, t], ranked[:, t]).then_inc(route, 1)
            link(8)
            dve.tensor_copy(topf[:], topi[:, :, 0:2]).then_inc(route, 1)
            link(9)
            for t in range(BT):
                last = dve.tensor_scalar(first[:, t], numberf[:], topf[:, t, 0:1], None, ALU.is_equal)
            last.then_inc(route, 1)
            link(10)
            for t in range(BT):
                last = dve.scalar_tensor_tensor(chosen[:, t], numberf[:], topf[:, t, 1:2], first[:, t],
                                                ALU.is_equal, ALU.add)
            last.then_inc(route, 1)
            link(11)
            dve.tensor_tensor(share[:, :, 0:EXPERTS], chosen[:], score[:], ALU.mult).then_inc(route, 1)
            link(12)
            dve.tensor_scalar(half_s[:], share[:], 0.5, None, ALU.mult)
            dve.scalar_tensor_tensor(half_s2[:], share[:], 0.5, share[:], ALU.mult, ALU.mult).then_inc(route, 1)

        def prologue():
            squares()
            split_qkv()
            low_x(0)
            constants()
            queries(0, 0)
            values(0, 0)
            queries(0, 1)
            values(0, 1)
            head_max(0, 0)
            head_max(0, 1)
            router_scores(0)

        def body(b, first=False, last=False):
            for n in range(SLOTS):
                if n == 12 and not last:
                    low_x(b + 1)
                if n + 2 < SLOTS:
                    head_max(b, n + 2)
                elif not last:
                    head_max(b + 1, n + 2 - SLOTS)
                if n % 2 == 0 and 1 <= n // 2 <= UNITS:
                    low_hidden(b, n // 2 - 1)
                if n % 2 == 0:
                    copy_turn(b, n)
                if n % 2 == 1 and n // 2 < UNITS:
                    hidden(b, n // 2)
                if n == 0 and not first:
                    scale_heads(b - 1)
                if n == 4 and not first:
                    finish(b - 1)
                if n == 2 and not last:
                    layer0_branch(b + 1)
                if n == 10:
                    invert_sums(b, 0)
                if n == 14:
                    invert_sums(b, 1)
                if n == 6 and not last:
                    moments(b + 1)
                if n == 8 and not last:
                    centre(b + 1)
                if n % 2 == 0 and n // 2 < UNITS:
                    hidden_tanh(b, n // 2)
                if not last:
                    if n == 12:
                        queries(b + 1, 0)
                    if n == 13:
                        values(b + 1, 0)
                        values(b + 1, 1)
                        queries(b + 1, 1)
                    if n == 14:
                        router_scores(b + 1)
            gate(b)

        def tail(b):
            scale_heads(b)
            finish(b)

        program(dve, prologue, body, tail)

    @block.scalar
    def _(act):
        def high_qkv(v):
            act.wait_ge(wqkv_in, 16)
            part = slice(v * 2 * HID, QKVR if v else 2 * HID)
            act.activation(wqkv_hi[:, :, part], wqkv[:, :, part], ACT.Copy).then_inc(wqkv_high, 1)

        def high_experts(g):
            act.wait_ge(w13_in[g], 16)
            act.activation(w13_hi[:, g].rearrange("p c i n -> p (c i n)"),
                           w13[:, g].rearrange("p c i n -> p (c i n)"), ACT.Copy).then_inc(w13_high, 1)

        def high_x(b):
            act.wait_ge(xT_done, b + 1)
            act.activation(xh[:].rearrange("p c n -> p (c n)"), bank[0][:], ACT.Copy).then_inc(hi_done, 1)

        def keys(b, c):
            act.wait_ge(q_done, 2 * b + c + 1)
            act.activation(kT[:, c, :], bank[7][:, SEQ:2 * SEQ], ACT.Identity, bias=bk[:, c:c + 1])\
                .then_inc(k_done, 1)

        def router_exp(b, t):
            act.wait_ge(v_read, 2 * b + t + 1)
            act.activation(en[:, t, :], bank[6 * t][:, HID:HID + EXPERTS], ACT.Exp, scale=-1.0).then_inc(en_done, 1)

        def exps(b, n):
            act.wait_ge(max_done, SLOTS * b + n + 1)
            wait(act, turned, SLOTS * b + n - 3)
            if n in (0, HH):
                wait(act, inverted, 2 * b - 1 + n // HH)
            s, h = bank[score_bank(n)], ORDER[n]
            act.activation(prob[:, n % 4, 0:2 * P], s[:, 0:2 * P], ACT.Exp, bias=nmax[:, n, 1:2],
                           accum_out=sums[:, 1, h:h + 1])
            act.activation(prob[:, n % 4, 2 * P:3 * P], s[:, 2 * P:3 * P], ACT.Exp, bias=nmax[:, n, 0:1],
                           accum_out=sums[:, 0, h:h + 1]).then_inc(exp_done, 1)

        def copy_turn(b, n):
            act.wait_ge(turned, SLOTS * b + n + 1)
            act.activation(probT[:, n % 4, :], bank[4][:, 0:3 * P], ACT.Copy).then_inc(turn_copied, 1)

        def tanhs(b, u):
            t, g = unit(u)
            act.wait_ge(w1_done, UNITS * b + u + 1)
            act.wait_ge(route, ROUTE * b + ROUTE)
            wait(act, tu_done, UNITS * b + u)
            for e in range(EG):
                c = slice(e * P, (e + 1) * P)
                last = act.activation(th[:, c], bank[7][:, c], ACT.Tanh,
                                      scale=half_s[:, t, g * EG + e:g * EG + e + 1])
            last.then_inc(tanh_done, 1)

        def copy_hidden(b, u):
            t, g = unit(u)
            act.wait_ge(h_turned, UNITS * b + u + 1)
            act.activation(hT_hi[:, t, g * EG:(g + 1) * EG, :].rearrange("p e n -> p (e n)"), bank[6][:, 0:GE],
                           ACT.Copy).then_inc(h_high, 1)

        def high_w2():
            act.wait_ge(w2_in, 48)
            act.wait_ge(w13_split, EX // EG)
            act.activation(w2_hi[:], w2[:], ACT.Copy).then_inc(w2_high, 1)

        def copy_heads(b):
            act.wait_ge(pv_done, b + 1)
            wait(act, oT_done, b)
            act.activation(oS[:], bank[5][:], ACT.Copy).then_inc(oS_done, 1)

        def gate(b):
            act.wait_ge(y_done, b + 1)
            act.activation(thy[:], bank[6][:], ACT.Tanh, scale=0.5).then_inc(thy_done, 1)

        def prologue():
            high_qkv(0)
            high_x(0)
            high_qkv(1)
            act.activation(warm[:], ones[:], ACT.Exp)
            high_experts(0)
            keys(0, 0)
            router_exp(0, 0)
            high_experts(1)
            keys(0, 1)
            router_exp(0, 1)
            exps(0, 0)
            exps(0, 1)
            high_experts(2)

        def body(b, first=False, last=False):
            for n in range(SLOTS):
                if n == 0 and not first:
                    copy_heads(b - 1)
                if n == 12 and not last:
                    high_x(b + 1)
                if n % 2 == 0 and 1 <= n // 2 <= UNITS:
                    copy_hidden(b, n // 2 - 1)
                if n + 2 < SLOTS:
                    exps(b, n + 2)
                elif not last:
                    exps(b + 1, n + 2 - SLOTS)
                if n % 2 == 1:
                    copy_turn(b, n)
                if n % 2 == 0 and n // 2 < UNITS:
                    tanhs(b, n // 2)
                if n == 5 and first:
                    high_w2()
                if not last:
                    if n == 12:
                        keys(b + 1, 0)
                    if n == 13:
                        router_exp(b + 1, 0)
                        router_exp(b + 1, 1)
                        keys(b + 1, 1)
            gate(b)

        program(act, prologue, body, copy_heads)

    @block.tensor
    def _(pe):
        def three(out, a_hi, a_lo, b_hi, b_lo, first, last):
            pe.matmul(out, a_hi, b_hi, start=first, stop=False)
            pe.matmul(out, a_hi, b_lo, start=False, stop=False)
            return pe.matmul(out, a_lo, b_hi, start=False, stop=last)

        def turn_x(b):
            wait(pe, xn_done, BT * b)
            wait(pe, s1_done, b - 1)
            for m in range(BT):
                for c in range(CH):
                    last = pe.transpose(bank[0][:, c * SEQ + m * P:c * SEQ + (m + 1) * P],
                                        xn[:, m, c * P:(c + 1) * P], ident[:])
            last.then_inc(xT_done, 1)

        def project_qk(b, f):
            if f == 0:
                pe.wait_ge(lo_done, b + 1)
                wait(pe, tu_done, UNITS * b)
            else:
                pe.wait_ge(q_done, 2 * b + 1)
                pe.wait_ge(k_done, 2 * b + 1)
            for i in range(2):
                w = slice(i * HID + f * P, i * HID + (f + 1) * P)
                for c in range(CH):
                    last = three(bank[7][:, i * SEQ:(i + 1) * SEQ], wqkv_hi[:, c, w], wqkv_lo[:, c, w],
                                 xh[:, c, :], xl[:, c, :], c == 0, c == CH - 1)
            last.then_inc(qk_proj, 1)

        def project_v(b, t):
            if t == 0:
                pe.wait_ge(lo_done, b + 1)
            else:
                wait(pe, h_copied, UNITS * b)
            for c in range(CH):
                s = slice(t * P, (t + 1) * P)
                last = three(bank[6 * t][:, 0:HID + EXPERTS], xh[:, c, s], xl[:, c, s],
                             wqkv_hi[:, c, 2 * HID:QKVR], wqkv_lo[:, c, 2 * HID:QKVR], c == 0, c == CH - 1)
            last.then_inc(v_proj, 1)

        def scores(b, n):
            if n % HH == 0:
                pe.wait_ge(q_done, 2 * b + n // HH + 1)
                pe.wait_ge(k_done, 2 * b + n // HH + 1)
            wait(pe, exp_done, SLOTS * b + score_bank_before(n) + 1)
            h = ORDER[n]
            c, r = h // HH, slice(32 * (h % HH // 2), 32 * (h % HH // 2) + 32)
            out = bank[score_bank(n)]
            pe.matmul(out[:, 0:2 * P], qm[r, h % 2, c, P:SEQ], kT[r, c, :], start=True, stop=False)
            pe.matmul(out[:, 2 * P:3 * P], qm[r, h % 2, c, 0:P], kT[r, c, 0:P], start=False, stop=False)
            pe.matmul(out[:, P:3 * P], identb[:], causal[:], start=False, stop=True).then_inc(scored, 1)

        def turn(b, n):
            pe.wait_ge(exp_done, SLOTS * b + n + 1)
            wait(pe, turn_copied, SLOTS * b + n)
            for to, block in ((0, 2), (1, 0), (2, 1)):
                last = pe.transpose(bank[4][:, to * P:(to + 1) * P], prob[:, n % 4, block * P:(block + 1) * P],
                                    ident[:])
            last.then_inc(turned, 1)

        def product(b, n):
            pe.wait_ge(turn_copied, SLOTS * b + n + 2)
            if n == 0:
                pe.wait_ge(v_read, 2 * b + 2)
                wait(pe, oS_done, b)
            if n == HH:
                pe.wait_ge(v_late_done, b + 1)
            for key in range(2):
                for i in range(2):
                    h = ORDER[n + i]
                    c, r = h // HH, slice(32 * (h % HH // 2), 32 * (h % HH // 2) + 32)
                    last = pe.matmul(bank[5][r, c * SEQ + key * P:(c + 1) * SEQ], vm[:, key, h // 2, h % 2, :],
                                     probT[:, (n + i) % 4, 2 * key * P:(2 + key) * P],
                                     start=(h % 2 == 0 and key == 0), stop=(h % 2 == 1 and key == 1))
            if n == SLOTS - 2:
                last.then_inc(pv_done, 1)

        def up(b, u, i):
            t, g = unit(u)
            if i == 0:
                if u:
                    pe.wait_ge(tu_done, UNITS * b + u)
                else:
                    pe.wait_ge(q_done, 2 * b + 2)
                    pe.wait_ge(k_done, 2 * b + 2)
            else:
                if u:
                    pe.wait_ge(h_copied, UNITS * b + u)
                else:
                    pe.wait_ge(v_read, 2 * b + 2)
                    pe.wait_ge(en_done, 2 * b + 2)
                    wait(pe, gy_done, b)
            if isinstance(b, int) and b == 0 and u < EX // EG:
                pe.wait_ge(w13_split, u + 1)
            for c in range(CH):
                s = slice(t * P, (t + 1) * P)
                last = three(bank[7 - i][:, 0:GE], xh[:, c, s], xl[:, c, s],
                             w13_hi[:, g, c, i, :], w13_lo[:, g, c, i, :], c == 0, c == CH - 1)
            last.then_inc(w3_done if i else w1_done, 1)

        def turn_hidden(b, u):
            pe.wait_ge(h_done, UNITS * b + u + 1)
            for e in range(EG):
                last = pe.transpose(bank[6][:, e * P:(e + 1) * P], hh[:, e * P:(e + 1) * P], ident[:])
            last.then_inc(h_turned, 1)

        def experts_sum(b, t, last):
            pe.wait_ge(h_copied, UNITS * b + UNITS)
            if isinstance(b, int) and b == 0:
                pe.wait_ge(w2_split, 1)
            if t == 0 and not last:
                pe.wait_ge(v_read, 2 * b + 4)
                pe.wait_ge(en_done, 2 * b + 4)
            for e in range(EX):
                last = three(bank[6][:, t * HID:(t + 1) * HID], hT_hi[:, t, e, :], hT_lo[:, t, e, :],
                             w2_hi[:, e, :], w2_lo[:, e, :], e == 0, e == EX - 1)
            if t == BT - 1:
                last.then_inc(y_done, 1)

        def turn_sums(b):
            pe.wait_ge(rsum_done, 2 * b + 2)
            if isinstance(b, int) and b == BATCHES - 1:
                pe.wait_ge(s1_done, b)
            else:
                pe.wait_ge(v_read, 2 * b + 3)
                pe.wait_ge(en_done, 2 * b + 3)
            for m in range(BT):
                for c in range(CH):
                    last = pe.transpose(bank[0][:, c * SEQ + m * P:c * SEQ + (m + 1) * P],
                                        rsum[:, m, c * HH:(c + 1) * HH, :].rearrange("p h d -> p (h d)"), ident[:])
            last.then_inc(rsum_turned, 1)

        def project_out(b):
            if isinstance(b, int) and b == 0:
                pe.wait_ge(w2_in, 48)
            pe.wait_ge(oT_done, b + 1)
            for t in range(BT):
                for c in range(CH):
                    last = pe.matmul(bank[0][:, t * HID:(t + 1) * HID], oT[:, c, t * P:(t + 1) * P], wo[:, c, :],
                                     start=(c == 0), stop=(c == CH - 1))
            last.then_inc(wo_done, 1)

        def prologue():
            turn_x(0)
            pe.wait_ge(ms_done, 1)
            pe.wait_ge(wqkv_split, 1)
            project_qk(0, 0)
            pe.wait_ge(wv_split, 1)
            project_v(0, 0)
            project_qk(0, 1)
            project_v(0, 1)
            scores(0, 0)
            scores(0, 1)

        def body(b, first=False, last=False):
            for n in range(SLOTS):
                if n + 2 < SLOTS:
                    scores(b, n + 2)
                elif not last:
                    scores(b + 1, n + 2 - SLOTS)
                if n % 2 == 0 and n // 2 < UNITS:
                    up(b, n // 2, 0)
                if n % 2 == 0 and 1 <= n // 2 <= UNITS:
                    turn_hidden(b, n // 2 - 1)
                if n % 2 == 0 and n >= 4:
                    product(b, n - 4)
                if n % 2 == 1 and n // 2 < UNITS:
                    up(b, n // 2, 1)
                turn(b, n)
                if n == 11 and not last:
                    turn_x(b + 1)
                if n == SLOTS - 1:
                    product(b, n - 3)
                if n == 0 and not first:
                    turn_sums(b - 1)
                if n == 1 and not first:
                    project_out(b - 1)
                if n in (14, 15):
                    experts_sum(b, n - 14, last)
                if not last:
                    if n == 12:
                        project_qk(b + 1, 0)
                        project_v(b + 1, 0)
                    if n == 13:
                        project_v(b + 1, 1)
                        project_qk(b + 1, 1)
            product(b, SLOTS - 2)

        def tail(b):
            turn_sums(b)
            project_out(b)

        program(pe, prologue, body, tail)
    ctx.close()


def kernel(**inputs):
    import numpy as np
    import concourse.bacc as bacc
    from concourse.bass_utils import run_bass_kernel_spmd

    a = {n: np.asarray(v) for n, v in inputs.items()}

    def rows(name):
        v = a[name].reshape(1, -1)
        return np.broadcast_to(v, (P, v.shape[1]))

    heads = a["L0_attn_qkv_w"].reshape(PAIRS, 2, 3, D0, HID).transpose(0, 2, 1, 3, 4).reshape(PAIRS, 3 * P, HID)
    gates = a["L0_attn_gate_w"].reshape(PAIRS, P, HID)
    w0 = np.concatenate([heads, gates], axis=1).transpose(0, 2, 1).reshape(PAIRS, CH, P, COLS)
    w0 = np.concatenate([w0.transpose(0, 2, 1, 3).reshape(PAIRS, P, CH * COLS),
                         a["L0_attn_out_w"].T.reshape(PAIRS, P, HID),
                         a["L0_attn_norm_w"].reshape(PAIRS, P, 1)], axis=2)
    e1 = np.concatenate([a["L1_ffn_w1"].reshape(-1, HID), a["L1_ffn_sw1"]], axis=0)
    e3 = np.concatenate([a["L1_ffn_w3"].reshape(-1, HID), a["L1_ffn_sw3"]], axis=0)
    arrays = {
        "x": a["L0_attn_hidden_states"].reshape(TOK, HID),
        "w0": w0,
        "ffn_w": np.ascontiguousarray(a["L0_ffn_weight"].T).view(np.int32),
        "ffn_sc": rows("L0_ffn_w_scale"),
        "ffn_b": rows("L0_ffn_bias"),
        "wqkv1": np.concatenate([a["L1_attn_Wq"].T, a["L1_attn_Wk"].T, a["L1_attn_Wv"].T,
                                 a["L1_ffn_gate_w"].T], axis=1),
        "wo1": a["L1_attn_Wo"].T,
        "bq": a["L1_attn_bq"].reshape(CH, P).T,
        "bk": a["L1_attn_bk"].reshape(CH, P).T,
        "bv": rows("L1_attn_bv"),
        "bo": rows("L1_attn_bo"),
        "ebias": rows("L1_ffn_expert_bias"),
        "w13": np.stack([e1.T.reshape(HID, EX // EG, EG * P), e3.T.reshape(HID, EX // EG, EG * P)], axis=2)
        .transpose(1, 0, 2, 3),
        "w2": np.concatenate([a["L1_ffn_w2"].transpose(0, 2, 1), a["L1_ffn_sw2"].T[None]], axis=0),
    }
    nc = bacc.Bacc("TRN2", target_bir_lowering=False, num_devices=1)
    given, args = {}, []
    for name, v in arrays.items():
        v = np.ascontiguousarray(v)
        given[f"in_{name}"] = v
        args.append(nc.dram_tensor(f"in_{name}", v.shape, mybir.dt.from_np(v.dtype), kind="ExternalInput").ap())
    args.append(nc.dram_tensor("out_0", (TOK, HID), F32, kind="ExternalOutput").ap())
    build(nc, *args)
    r = run_bass_kernel_spmd(nc, [given], core_ids=[0])
    return r.results[0]["out_0"].reshape(BATCHES, SEQ, HID)
```
